# Optimizing a Trainium2 kernel written in Bass

```python
import numpy as np
import jax
import jax.numpy as jnp

def _softmax(x, axis=-1):
    return jax.nn.softmax(x, axis=axis)

def _gelu(x):
    return jax.nn.gelu(x, approximate=True)

def _silu(x):
    return jax.nn.silu(x)

def _sigmoid(x):
    return jax.nn.sigmoid(x)

def _layernorm(x, axis=-1, eps=1e-05):
    m = jnp.mean(x, axis=axis, keepdims=True)
    v = jnp.var(x, axis=axis, keepdims=True)
    return (x - m) / jnp.sqrt(v + eps)

def _scatter_add(tgt, idx, src, axis=0):
    return tgt.at[idx].add(src)

def _segment_sum(src, seg, n):
    return jax.ops.segment_sum(src, seg, n)
kernel_name = 'mk_gnn_resnorm_d4_gnn_r32_c0821f'

def setup_inputs(seed: int=0):
    np.random.seed(seed)
    _w = jnp.asarray

    def _rec_inputs():
        import jax
        import jax.numpy as jnp
        _gk = jax.random.key(seed)
        x = -0.0003713 + 1 * jax.random.normal(jax.random.fold_in(_gk, 1), (50000, 128), jnp.float32)
        src = jax.random.randint(jax.random.fold_in(_gk, 2), (25000,), 0, 50000, jnp.int32)
        dst = jax.random.randint(jax.random.fold_in(_gk, 3), (25000,), 0, 50000, jnp.int32)
        _o = jnp.argsort(dst, stable=True)
        src = src[_o]
        dst = dst[_o]
        edge_attr_128 = -8.16379e-05 + 0.999858 * jax.random.normal(jax.random.fold_in(_gk, 12), (25000, 128), jnp.float32)
        edge_weight = jax.random.uniform(jax.random.fold_in(_gk, 15), (25000,), jnp.float32, 0.0, 1)
        return (x, src, dst, edge_attr_128, edge_weight)
    x, src, dst, edge_attr_128, edge_weight = _rec_inputs()

    def _L0_gnn_setup():
        import jax, jax.numpy as jnp
        import numpy as np
        N_NODES = 3125
        N_EDGES = 50000
        IN_F = 128
        H = 8
        F = 16
        NEG_SLOPE = 0.2
        EPS = 1e-16
        key = jax.random.key(seed)
        k1, k2, k3, k4, k5, k6 = jax.random.split(key, 6)
        x = jax.random.normal(k1, (N_NODES, IN_F), dtype=jnp.float32)
        edge_index = jax.random.randint(k2, (2, N_EDGES), 0, N_NODES, dtype=jnp.int64)
        W_proj = jax.random.normal(k3, (IN_F, H * F), dtype=jnp.float32) * (1.0 / np.sqrt(IN_F))
        W_skip = jax.random.normal(k4, (IN_F, H * F), dtype=jnp.float32) * (1.0 / np.sqrt(IN_F))
        a_src = jax.random.normal(k5, (1, H, F), dtype=jnp.float32) * 0.1
        a_tgt = jax.random.normal(k6, (1, H, F), dtype=jnp.float32) * 0.1
        return {'x': x, 'edge_index': edge_index, 'W_proj': W_proj, 'W_skip': W_skip, 'a_src': a_src, 'a_tgt': a_tgt}
    _L0_gnn_all = _L0_gnn_setup()
    _L0_gnn_in = {k: v for k, v in _L0_gnn_all.items() if k in ('W_proj', 'W_skip', 'a_src', 'a_tgt')}
    del _L0_gnn_all

    def _L1_gnn_setup():
        import jax, jax.numpy as jnp
        import numpy as np
        N_NODES = 3125
        N_EDGES = 50000
        NFEAT = 128
        NHID = 64

        def _gcn_layer(h, src, dst, edge_weight, w, b, n_nodes):
            support = h @ w
            msgs = support[src] * edge_weight[:, None]
            agg = jax.ops.segment_sum(msgs, dst, num_segments=n_nodes)
            return agg + b
        key = jax.random.key(seed)
        ks = jax.random.split(key, 8)
        x = jax.random.normal(ks[0], (N_NODES, NFEAT), dtype=jnp.float32)
        src = jax.random.randint(ks[1], (N_EDGES,), 0, N_NODES, dtype=jnp.int32)
        dst = jax.random.randint(ks[2], (N_EDGES,), 0, N_NODES, dtype=jnp.int32)
        edge_weight = jax.random.uniform(ks[3], (N_EDGES,), dtype=jnp.float32)
        w1 = jax.random.normal(ks[4], (NFEAT, NHID), dtype=jnp.float32) * (1.0 / np.sqrt(NFEAT))
        b1 = jnp.zeros((NHID,), dtype=jnp.float32)
        w2 = jax.random.normal(ks[5], (NHID, 2 * NHID), dtype=jnp.float32) * (1.0 / np.sqrt(NHID))
        b2 = jnp.zeros((2 * NHID,), dtype=jnp.float32)
        return {'x': x, 'src': src, 'dst': dst, 'edge_weight': edge_weight, 'w1': w1, 'b1': b1, 'w2': w2, 'b2': b2}
    _L1_gnn_all = _L1_gnn_setup()
    _L1_gnn_in = {k: v for k, v in _L1_gnn_all.items() if k in ('w1', 'b1', 'w2', 'b2')}
    del _L1_gnn_all

    def _L2_gnn_setup():
        import jax, jax.numpy as jnp
        import numpy as np
        N_NODES = 50000
        N_EDGES = 25000
        DIM = 128
        key = jax.random.key(seed)
        k1, k2, k3, k4, k5, k6 = jax.random.split(key, 6)
        node_emb = jax.random.normal(k1, (N_NODES, DIM), dtype=jnp.float32)
        edge_emb = jax.random.normal(k2, (N_EDGES, DIM), dtype=jnp.float32)
        W_att_w = jax.random.normal(k3, (2 * DIM,), dtype=jnp.float32) * 0.05
        W_att_b = jax.random.normal(k4, (1,), dtype=jnp.float32) * 0.05
        src = jax.random.randint(k5, (N_EDGES,), 0, N_NODES, dtype=jnp.int32)
        off = jax.random.randint(k6, (N_EDGES,), 1, N_NODES, dtype=jnp.int32)
        dst = (src + off) % N_NODES
        edge_list = jnp.stack([src, dst], axis=1)
        return {'node_emb': node_emb, 'edge_emb': edge_emb, 'W_att_w': W_att_w, 'W_att_b': W_att_b, 'edge_list': edge_list}
    _L2_gnn_all = _L2_gnn_setup()
    _L2_gnn_in = {k: v for k, v in _L2_gnn_all.items() if k in ('W_att_w', 'W_att_b')}
    del _L2_gnn_all

    def _L3_gnn_setup():
        import jax, jax.numpy as jnp
        import numpy as np
        N_NODES = 50000
        N_EDGES = 18750
        HIDDEN = 128
        NUM_STEPS = 3

        def _gru_cell(m, h, w_ih, w_hh, b_ih, b_hh):
            gi = m @ w_ih.T + b_ih
            gh = h @ w_hh.T + b_hh
            gi_r, gi_z, gi_n = jnp.split(gi, 3, axis=-1)
            gh_r, gh_z, gh_n = jnp.split(gh, 3, axis=-1)
            r = jax.nn.sigmoid(gi_r + gh_r)
            z = jax.nn.sigmoid(gi_z + gh_z)
            n = jnp.tanh(gi_n + r * gh_n)
            return (1.0 - z) * n + z * h
        key = jax.random.key(seed)
        ks = jax.random.split(key, 8)
        x = jax.random.normal(ks[0], (N_NODES, HIDDEN), dtype=jnp.float32)
        edge_index = jax.random.randint(ks[1], (2, N_EDGES), 0, N_NODES, dtype=jnp.int64)
        edge_weight = jax.random.uniform(ks[2], (N_EDGES,), dtype=jnp.float32)
        s = 1.0 / np.sqrt(HIDDEN)
        W = jax.random.uniform(ks[3], (NUM_STEPS, HIDDEN, HIDDEN), minval=-s, maxval=s, dtype=jnp.float32)
        w_ih = jax.random.uniform(ks[4], (3 * HIDDEN, HIDDEN), minval=-s, maxval=s, dtype=jnp.float32)
        w_hh = jax.random.uniform(ks[5], (3 * HIDDEN, HIDDEN), minval=-s, maxval=s, dtype=jnp.float32)
        b_ih = jax.random.uniform(ks[6], (3 * HIDDEN,), minval=-s, maxval=s, dtype=jnp.float32)
        b_hh = jax.random.uniform(ks[7], (3 * HIDDEN,), minval=-s, maxval=s, dtype=jnp.float32)
        return {'x': x, 'edge_index': edge_index, 'edge_weight': edge_weight, 'W': W, 'w_ih': w_ih, 'w_hh': w_hh, 'b_ih': b_ih, 'b_hh': b_hh}
    _L3_gnn_all = _L3_gnn_setup()
    _L3_gnn_in = {k: v for k, v in _L3_gnn_all.items() if k in ('W', 'w_ih', 'w_hh', 'b_ih', 'b_hh')}
    del _L3_gnn_all
    return {'x': x, 'src': src, 'dst': dst, 'edge_attr_128': edge_attr_128, 'edge_weight': edge_weight, 'L0_gnn_W_proj': _L0_gnn_in['W_proj'], 'L0_gnn_W_skip': _L0_gnn_in['W_skip'], 'L0_gnn_a_src': _L0_gnn_in['a_src'], 'L0_gnn_a_tgt': _L0_gnn_in['a_tgt'], 'L1_gnn_w1': _L1_gnn_in['w1'], 'L1_gnn_b1': _L1_gnn_in['b1'], 'L1_gnn_w2': _L1_gnn_in['w2'], 'L1_gnn_b2': _L1_gnn_in['b2'], 'L2_gnn_W_att_w': _L2_gnn_in['W_att_w'], 'L2_gnn_W_att_b': _L2_gnn_in['W_att_b'], 'L3_gnn_W': _L3_gnn_in['W'], 'L3_gnn_w_ih': _L3_gnn_in['w_ih'], 'L3_gnn_w_hh': _L3_gnn_in['w_hh'], 'L3_gnn_b_ih': _L3_gnn_in['b_ih'], 'L3_gnn_b_hh': _L3_gnn_in['b_hh']}

def reference(x, src, dst, edge_attr_128, edge_weight, L0_gnn_W_proj, L0_gnn_W_skip, L0_gnn_a_src, L0_gnn_a_tgt, L1_gnn_w1, L1_gnn_b1, L1_gnn_w2, L1_gnn_b2, L2_gnn_W_att_w, L2_gnn_W_att_b, L3_gnn_W, L3_gnn_w_ih, L3_gnn_w_hh, L3_gnn_b_ih, L3_gnn_b_hh):
    import jax
    import jax.numpy as jnp

    def _L0_gnn_ref(x, edge_index, W_proj, W_skip, a_src, a_tgt):
        import jax, jax.numpy as jnp
        import numpy as np
        N_NODES = 3125
        N_EDGES = 50000
        IN_F = 128
        H = 8
        F = 16
        NEG_SLOPE = 0.2
        EPS = 1e-16
        N = x.shape[0]
        p = (x @ W_proj).reshape(N, H, F)
        scores_src = jnp.sum(p * a_src, axis=-1)
        scores_tgt = jnp.sum(p * a_tgt, axis=-1)
        src = edge_index[0]
        tgt = edge_index[1]
        s = jax.nn.leaky_relu(scores_src[src] + scores_tgt[tgt], negative_slope=NEG_SLOPE)
        e = jnp.exp(s - jnp.max(s))
        denom = jax.ops.segment_sum(e, tgt, num_segments=N)[tgt]
        att = e / (denom + EPS)
        msg = p[src] * att[:, :, None]
        out = jax.ops.segment_sum(msg, tgt, num_segments=N)
        out = out + (x @ W_skip).reshape(N, H, F)
        out = out.reshape(N, H * F)
        return jax.nn.elu(out)

    def _L1_gnn_ref(x, src, dst, edge_weight, w1, b1, w2, b2):
        import jax, jax.numpy as jnp
        import numpy as np
        N_NODES = 3125
        N_EDGES = 50000
        NFEAT = 128
        NHID = 64

        def _gcn_layer(h, src, dst, edge_weight, w, b, n_nodes):
            support = h @ w
            msgs = support[src] * edge_weight[:, None]
            agg = jax.ops.segment_sum(msgs, dst, num_segments=n_nodes)
            return agg + b
        n = x.shape[0]
        h = jax.nn.sigmoid(_gcn_layer(x, src, dst, edge_weight, w1, b1, n))
        out = jax.nn.sigmoid(_gcn_layer(h, src, dst, edge_weight, w2, b2, n))
        return out

    def _L2_gnn_ref(node_emb, edge_emb, W_att_w, W_att_b, edge_list):
        import jax, jax.numpy as jnp
        import numpy as np
        N_NODES = 50000
        N_EDGES = 25000
        DIM = 128
        n_nodes, node_dim = node_emb.shape
        n_edges = edge_emb.shape[0]
        w_n = W_att_w[:node_dim]
        w_e = W_att_w[node_dim:]
        b = W_att_b[0]
        seg = jnp.concatenate([edge_list[:, 0], edge_list[:, 1]])
        s_node = node_emb @ w_n
        s_edge = edge_emb @ w_e
        raw = s_node[seg] + jnp.concatenate([s_edge, s_edge]) + b
        score = jax.nn.leaky_relu(raw, negative_slope=0.2)
        m = jax.ops.segment_max(score, seg, num_segments=n_nodes)
        m = jnp.where(jnp.isfinite(m), m, 0.0)
        ex = jnp.exp(score - m[seg])
        denom = jax.ops.segment_sum(ex, seg, num_segments=n_nodes)
        denom_safe = jnp.where(denom > 0, denom, 1.0)
        att = ex / denom_safe[seg]
        ee2 = jnp.concatenate([edge_emb, edge_emb], axis=0)
        agg = jax.ops.segment_sum(att[:, None] * ee2, seg, num_segments=n_nodes)
        out = jax.nn.gelu(agg, approximate=False)
        deg = jax.ops.segment_sum(jnp.ones_like(score), seg, num_segments=n_nodes)
        return jnp.where((deg > 0)[:, None], out, node_emb)

    def _L3_gnn_ref(x, edge_index, edge_weight, W, w_ih, w_hh, b_ih, b_hh):
        import jax, jax.numpy as jnp
        import numpy as np
        N_NODES = 50000
        N_EDGES = 18750
        HIDDEN = 128
        NUM_STEPS = 3

        def _gru_cell(m, h, w_ih, w_hh, b_ih, b_hh):
            gi = m @ w_ih.T + b_ih
            gh = h @ w_hh.T + b_hh
            gi_r, gi_z, gi_n = jnp.split(gi, 3, axis=-1)
            gh_r, gh_z, gh_n = jnp.split(gh, 3, axis=-1)
            r = jax.nn.sigmoid(gi_r + gh_r)
            z = jax.nn.sigmoid(gi_z + gh_z)
            n = jnp.tanh(gi_n + r * gh_n)
            return (1.0 - z) * n + z * h
        src, dst = (edge_index[0], edge_index[1])
        n_nodes = x.shape[0]
        h = x
        for i in range(NUM_STEPS):
            m = h @ W[i]
            msg = edge_weight[:, None] * m[src]
            agg = jax.ops.segment_sum(msg, dst, num_segments=n_nodes)
            h = _gru_cell(agg, h, w_ih, w_hh, b_ih, b_hh)
        return h
    edge_index = jnp.stack([src, dst])
    edge_index_t = jnp.stack([src, dst], axis=1)
    x = _layernorm(x + _L0_gnn_ref(x, edge_index, L0_gnn_W_proj, L0_gnn_W_skip, L0_gnn_a_src, L0_gnn_a_tgt), axis=-1)
    x = _layernorm(x + _L1_gnn_ref(x, src, dst, edge_weight, L1_gnn_w1, L1_gnn_b1, L1_gnn_w2, L1_gnn_b2), axis=-1)
    x = _layernorm(x + _L2_gnn_ref(x, edge_attr_128, L2_gnn_W_att_w, L2_gnn_W_att_b, edge_index_t), axis=-1)
    x = _layernorm(x + _L3_gnn_ref(x, edge_index, edge_weight, L3_gnn_W, L3_gnn_w_ih, L3_gnn_w_hh, L3_gnn_b_ih, L3_gnn_b_hh), axis=-1)
    return x

_drawn_inputs = setup_inputs


def setup_inputs(seed=0):
    import zlib

    import numpy as np

    out = dict(_drawn_inputs(seed))
    spreads = {'L1_gnn_b1': (0.0, 0.8), 'L1_gnn_b2': (0.0, 0.307)}
    factors = {'L0_gnn_a_tgt': 6.472, 'L1_gnn_w1': 7.426, 'L3_gnn_b_hh': 2.737}
    for name, (base, spread) in spreads.items():
        noise = np.random.default_rng([zlib.crc32(name.encode()), seed]).standard_normal(out[name].shape)
        drawn = base * np.exp(spread * noise) if base else spread * noise
        out[name] = jnp.asarray(drawn.astype(out[name].dtype))
    for name, factor in factors.items():
        out[name] = (out[name] * factor).astype(out[name].dtype)
    return out
```

```python
from contextlib import ExitStack, contextmanager

import concourse.bass as bass
from concourse import mybir

F32 = mybir.dt.float32
I32 = mybir.dt.int32
BF16 = mybir.dt.bfloat16
ALU = mybir.AluOpType
ACT = mybir.ActivationFunctionType
AX_X = mybir.AxisListType.X
RMAX = bass.bass_isa.ReduceOp.max

N = 50000
E = 25000
D = 128
HEADS = 8
HF = D // HEADS
HID = 64
P = 128
CH = -(-E // P)
EP = CH * P
SP_P, SP_B = 125, 200
LO = 256
HG = 98
PAD_KEY = 2 * HG * LO - 1
AW = 136
U = 7
GROUPS = CH // U
NP_, NJ = 100, 5
NB = NP_ * NJ
TILES = N // NB
UB = 10
LN_EPS = 1e-5
FAR = -1e30


class Count:

    def __init__(self, sem, kind):
        self.sem, self.base, self.kind = sem, 0, kind

    def up(self, n):
        self.base += n


class Chain:

    def __init__(self, eng, count, per=0):
        self.eng, self.count, self.per = eng, count, per
        self.n, self.iv, self.extra = 0, None, 0

    def start(self, iv):
        self.iv, self.n = iv, 0

    def value(self):
        v = self.count.base + self.extra + self.n
        return v if self.iv is None else self.iv * self.per + v

    def step(self, ins):
        self.n += 1
        ins.then_inc(self.count.sem, 1)
        return ins

    def hold(self):
        self.eng.wait_ge(self.count.sem, self.value())

    def link(self, ins):
        self.step(ins)
        self.hold()

    def loop_done(self, steps):
        assert self.n == self.per, (self.n, self.per)
        self.extra += steps * self.per
        self.n, self.iv = 0, None

    def finish(self):
        self.count.up(self.extra + self.n)


class Net:

    def __init__(self, nc, ctx, some_input):
        self.nc, self.ctx, self.counts, self.passes = nc, ctx, {}, 0
        self.spare = {"": [], "pool_dma": [], "dma": []}
        self.fresh = []
        self.some_input = some_input
        self.raise_buf = self.sb("raise_buf", [P, 64])
        self.passed = ctx.enter_context(nc.semaphore("passed"))

    def sem(self, name, kind=""):
        if name not in self.counts:
            spare = self.spare[kind]
            if not spare:
                spare.append(Count(self.ctx.enter_context(self.nc.semaphore(f"{name}_{self.passes}")), kind))
                self.fresh.append(spare[-1])
            self.counts[name] = spare.pop()
        return self.counts[name]

    @contextmanager
    def block(self):
        fresh, self.fresh, nc = self.fresh, [], self.nc
        if fresh:
            raised = [c for c in fresh if c.kind == ""]
            by_sp = [c for c in fresh if c.kind == "dma"]
            by_pool = [c for c in fresh if c.kind == "pool_dma"]

            def few_bytes(eng, counts, row):
                for n, c in enumerate(counts):
                    eng.dma_start(self.raise_buf[row:row + 1, n:n + 1],
                                  self.some_input[0:1, 0:1]).then_inc(c.sem, 16)
                for c in counts:
                    eng.wait_ge(c.sem, 16)
                    c.base += 16

            with nc.Block() as block:
                @block.sync
                def _(sp):
                    few_bytes(sp, by_sp, 0)

                @block.gpsimd
                def _(pool):
                    for c in raised:
                        pool.sem_inc(c.sem, 1)
                        c.base += 1
                    few_bytes(pool, by_pool, 32)
        with nc.Block() as block:
            yield block

    def end_of_pass(self):
        for count in self.counts.values():
            self.spare[count.kind].append(count)
        self.counts = {}

    def sb(self, name, shape, dt=F32):
        return self.ctx.enter_context(self.nc.sbuf_tensor(name, shape, dt))

    def dram(self, name, shape, dt=F32):
        return self.nc.dram_tensor(name, shape, dt, kind="Internal").ap()


def scope(g):
    nc, ctx = g.nc, ExitStack()
    g.end_of_pass()
    g.passes += 1
    of = f"pass{g.passes}_"

    def sb(name, shape, dt=F32):
        return ctx.enter_context(nc.sbuf_tensor(of + name, shape, dt))

    def ps(name, shape, dt=F32):
        return ctx.enter_context(nc.psum_tensor(of + name, shape, dt))

    return ctx, sb, ps


def gate(g, eng):
    eng.sem_inc(g.passed, 1)


def bcast(row, parts):
    return row.rearrange("(a n) -> a n", a=1).partition_broadcast(parts)


def constants_pass(g):
    nc = g.nc
    made = g.sem("consts_made")
    g.ident = g.sb("ident", [P, P])
    g.iota_lo = g.sb("iota_lo", [P, LO], BF16)
    g.iota_hi = g.sb("iota_hi", [P, 2 * HG], BF16)
    g.iota_p = g.sb("iota_p", [P, 2])
    g.earlier = g.sb("earlier", [P, P])
    g.zero = g.sb("zero", [P, 4 * AW])
    with g.block() as block:
        @block.gpsimd
        def _(pool):
            nc.gpsimd.memset(g.ident[:], 0.0).then_inc(made.sem, 1)
            nc.gpsimd.memset(g.earlier[:], 1.0).then_inc(made.sem, 1)
            nc.gpsimd.memset(g.zero[:], 0.0).then_inc(made.sem, 1)
            nc.gpsimd.iota(g.iota_lo[:], [[1, LO]], base=0, channel_multiplier=0,
                           allow_small_or_imprecise_dtypes=True).then_inc(made.sem, 1)
            nc.gpsimd.iota(g.iota_hi[:], [[1, 2 * HG]], base=0, channel_multiplier=0,
                           allow_small_or_imprecise_dtypes=True).then_inc(made.sem, 1)
            nc.gpsimd.iota(g.iota_p[:], [[HG, 2]], base=0, channel_multiplier=1,
                           allow_small_or_imprecise_dtypes=True).then_inc(made.sem, 1)
            pool.wait_ge(made.sem, made.base + 6)
            nc.gpsimd.affine_select(out=g.ident[:], in_=g.ident[:], compare_op=ALU.not_equal, fill=1.0,
                                    base=0, pattern=[[-1, P]], channel_multiplier=1).then_inc(made.sem, 1)
            nc.gpsimd.affine_select(out=g.earlier[:], in_=g.earlier[:], compare_op=ALU.is_gt, fill=0.0,
                                    base=0, pattern=[[-1, P]], channel_multiplier=1).then_inc(made.sem, 1)
            pool.wait_ge(made.sem, made.base + 8)
    made.up(8)


def sort_pass(g, src, dst, weight):
    nc = g.nc
    keys_in = {"dst": dst, "src": src}
    g.rec = {k: g.dram(f"rec_{k}", [EP, 4]) for k in keys_in}
    g.agg_dst = g.dram("agg_dst", [N, AW])
    g.agg_src = g.dram("agg_src", [N, AW])
    g.agg_hid = g.dram("agg_hid", [N, HID])

    zeroed = g.sem("tables_zeroed", "dma")
    with g.block() as block:

        def zero_fill(eng, table, width):
            rows = 4 if width == AW else 8
            v = table.rearrange("(t p r) w -> t p (r w)", p=125, r=rows)
            with eng.Fori(0, N // (125 * rows)) as t:
                eng.dma_start(v[bass.ds(t, 1)].rearrange("a p m -> (a p) m"),
                              g.zero[0:125, 0:rows * width]).then_inc(zeroed.sem, 16)
            return 16 * (N // (125 * rows))

        total = []

        @block.sync
        def _(sp):
            total.append(zero_fill(sp, g.agg_dst, AW))
            total.append(zero_fill(sp, g.agg_hid, HID))

        @block.scalar
        def _(act):
            total.append(zero_fill(act, g.agg_src, AW))
            act.wait_ge(zeroed.sem, zeroed.base + sum(total))
    zeroed.up(sum(total))

    ctx, sb, ps = scope(g)
    with ctx:
        rec = sb("rec", [SP_P, SP_B, 4])
        ints = sb("ints", [SP_P, 2, SP_B], I32)
        hi_lo = sb("hi_lo", [SP_P, 2, SP_B], I32)
        wcol = sb("wcol", [SP_P, SP_B])
        hi_f = sb("hi_f", [SP_P, SP_B])
        lo_f = sb("lo_f", [SP_P, SP_B])
        key_f = sb("key_f", [SP_P, SP_B])
        row = sb("row", [SP_P, E], I32)
        oh_lo = sb("oh_lo", [SP_P, 2, UB, LO], BF16)
        oh_hi = sb("oh_hi", [SP_P, 2, UB, 2 * HG], BF16)
        hi_t = sb("hi_t", [HG, UB, SP_P], I32)
        oh_t = sb("oh_t", [HG, 2, UB, 2, SP_P])
        junk_eq = sb("junk_eq", [SP_P, 2, UB, SP_P], BF16)
        junk_lo = sb("junk_lo", [SP_P, 2, UB, LO], BF16)
        rank = sb("rank", [SP_P, 2, 2, UB])
        pos = sb("pos", [SP_P, 2, UB])
        pos_i = sb("pos_i", [SP_P, 2, UB], I32)
        low_i = sb("low_i", [SP_P, 2, UB], I32)
        high_i = sb("high_i", [SP_P, 2, UB], I32)
        place = sb("place", [SP_P, 2, UB], I32)
        rec_stage = sb("rec_stage", [SP_P, 2, UB, 4])
        hist = sb("hist", [HG, 2, LO])
        scan = sb("scan", [HG, 2, LO])
        tot = sb("tot", [HG, 4])
        offs = sb("offs", [HG, 2])
        ones = sb("ones", [HG, HG])
        later = sb("later", [HG, HG])
        hist_sb = sb("hist_sb", [HG, 2, 2 * LO])
        pad = sb("pad", [88, 4])
        h_ps = ps("h_ps", [HG, 2 * LO])
        look_ps = ps("look_ps", [SP_P, 4, 512])
        off_ps = ps("off_ps", [HG, 512])
        steps = SP_B // UB // 2

        for key in ("dst", "src"):
            key_in = keys_in[key]
            ki = 1 if key == "dst" else 0
            out = g.rec[key]
            loaded, dve, prep = g.sem("sort_loaded", "dma"), g.sem("sort_dve"), g.sem("sort_prep")
            padded, numbered, summed = g.sem("sort_padded", "dma"), g.sem("sort_numbered"), g.sem("sort_summed")
            snap, counted_b = g.sem("sort_snapped"), g.sem("sort_counted_block")
            looked = [g.sem(f"sort_looked{h}") for h in range(2)]
            ranked = [g.sem(f"sort_ranked{h}") for h in range(2)]
            placed = [g.sem(f"sort_placed{h}") for h in range(2)]
            scattered = [g.sem(f"sort_scattered{h}", "pool_dma") for h in range(2)]
            onehots = [g.sem(f"sort_onehots{h}") for h in range(2)]
            counted = [g.sem(f"sort_counted{h}") for h in range(2)]
            with g.block() as block:
                @block.sync
                def _(sp):
                    v = lambda a: a.rearrange("(p b) -> p b", b=SP_B)
                    sp.dma_start(ints[:, 0, :], v(src)).then_inc(loaded.sem, 16)
                    sp.dma_start(ints[:, 1, :], v(dst)).then_inc(loaded.sem, 16)
                    sp.dma_start(wcol[:], v(weight)).then_inc(loaded.sem, 16)
                    sp.dma_start(row[:], bcast(key_in, SP_P)).then_inc(loaded.sem, 16)
                    sp.wait_ge(prep.sem, prep.base + 1)
                    sp.dma_start(out.rearrange("(q c) k -> q c k", c=CH)[0:88, CH - 1, :],
                                 pad[:]).then_inc(padded.sem, 16)
                    sp.wait_ge(padded.sem, padded.base + 16)

                @block.vector
                def _(v):
                    ch = Chain(v, dve)
                    ch.step(nc.vector.memset(ones[:], 1.0))
                    ch.step(nc.vector.memset(pad[:], 0.0))
                    ch.link(nc.vector.tensor_scalar(later[:], g.earlier[0:HG, 0:HG], -1.0, 1.0, ALU.mult, ALU.add))
                    ch.step(nc.vector.tensor_tensor(later[:], later[:], g.ident[0:HG, 0:HG], ALU.subtract))
                    nc.vector.memset(pad[:, ki:ki + 1], float(PAD_KEY)).then_inc(prep.sem, 1)
                    v.wait_ge(loaded.sem, loaded.base + 64)
                    ch.step(nc.vector.tensor_copy(rec[:, :, 0], ints[:, 0, :]))
                    ch.step(nc.vector.tensor_copy(rec[:, :, 1], ints[:, 1, :]))
                    ch.step(nc.vector.tensor_copy(rec[:, :, 2], wcol[:]))
                    ch.step(nc.vector.tensor_scalar(hi_lo[:, 0, :], ints[:, ki, :], 8, None, ALU.logical_shift_right))
                    ch.link(nc.vector.tensor_scalar(hi_lo[:, 1, :], ints[:, ki, :], LO - 1, None, ALU.bitwise_and))
                    ch.step(nc.vector.tensor_copy(hi_f[:], hi_lo[:, 0, :]))
                    ch.step(nc.vector.tensor_copy(key_f[:], ints[:, ki, :]))
                    ch.link(nc.vector.tensor_copy(lo_f[:], hi_lo[:, 1, :]))
                    ch.finish()

                @block.gpsimd
                def _(pool):
                    nc.gpsimd.iota(rec[:, :, 3], [[1, SP_B]], base=0, channel_multiplier=SP_B,
                                   allow_small_or_imprecise_dtypes=True).then_inc(numbered.sem, 1)
                    pool.wait_ge(numbered.sem, numbered.base + 1)
            loaded.up(64)
            padded.up(16)
            prep.up(1)
            numbered.up(1)

            def onehots_of(par, b, i):
                nc.vector.tensor_scalar(oh_lo[:, par, b, :], g.iota_lo[0:SP_P, :],
                                        lo_f[:, bass.ds(i, 1)], None, ALU.is_equal)
                return nc.vector.tensor_scalar(oh_hi[:, par, b, :], g.iota_hi[0:SP_P, :],
                                               hi_f[:, bass.ds(i, 1)], None, ALU.is_equal)

            def count(par, b):
                for h in range(2):
                    last = nc.tensor.matmul(h_ps[:, h * LO:(h + 1) * LO], oh_hi[:, par, b, h * HG:(h + 1) * HG],
                                            oh_lo[:, par, b, :], start=False, stop=True, skip_group_check=True)
                return last

            with g.block() as block:
                @block.vector
                def _(v):
                    with v.Fori(0, steps) as it:
                        for par in range(2):
                            v.wait_ge(counted[par].sem, it + counted[par].base)
                            for b in range(UB):
                                last = onehots_of(par, b, it * (2 * UB) + (par * UB + b))
                            last.then_inc(onehots[par].sem, 1)

                @block.tensor
                def _(pe):
                    nc.tensor.matmul(h_ps[:, :], g.zero[:, 0:HG], g.zero[:, 0:2 * LO], start=True, stop=True)
                    with pe.Fori(0, steps) as it:
                        for par in range(2):
                            pe.wait_ge(onehots[par].sem, it + (onehots[par].base + 1))
                            for b in range(UB):
                                last = count(par, b)
                            last.then_inc(counted[par].sem, 1)
            for h in range(2):
                onehots[h].up(steps)
                counted[h].up(steps)

            with g.block() as block:
                @block.vector
                def _(v):
                    ch = Chain(v, dve)
                    ch.step(nc.vector.memset(tot[:], 0.0))
                    ch.link(nc.vector.tensor_copy(hist[:].rearrange("p a b -> p (a b)"), h_ps[:]))
                    for h in range(2):
                        ch.step(nc.vector.tensor_tensor_scan(scan[:, h, :], hist[:, h, :], g.zero[0:HG, 0:LO],
                                                             0.0, ALU.add, ALU.add))
                    ch.hold()
                    ch.step(nc.vector.tensor_copy(tot[:, 0:2], scan[:, :, LO - 1]))
                    ch.step(nc.vector.tensor_copy(tot[:, 3:4], scan[:, 0, LO - 1:LO]))
                    ch.link(nc.vector.tensor_tensor(hist[:], scan[:], hist[:], ALU.subtract))
                    ch.finish()
            with g.block() as block:
                @block.tensor
                def _(pe):
                    nc.tensor.matmul(off_ps[:, 0:2], later[:], tot[:, 0:2], start=True, stop=False)
                    nc.tensor.matmul(off_ps[:, 0:2], ones[:], tot[:, 2:4], start=False,
                                     stop=True).then_inc(summed.sem, 1)
                    pe.wait_ge(summed.sem, summed.base + 3)
                    nc.tensor.matmul(h_ps[:, :], g.ident[0:HG, 0:HG],
                                     hist[:].rearrange("p a b -> p (a b)"), start=True,
                                     stop=True).then_inc(summed.sem, 1)
                    pe.wait_ge(summed.sem, summed.base + 4)

                @block.vector
                def _(v):
                    v.wait_ge(summed.sem, summed.base + 1)
                    for h in range(2):
                        nc.vector.tensor_scalar(hist[:, h, :], hist[:, h, :], off_ps[:, h:h + 1], None,
                                                ALU.add).then_inc(summed.sem, 1)
            summed.up(4)

            with g.block() as block:
                @block.scalar
                def _(act):
                    with act.Fori(0, SP_B // 2) as it:
                        for p2 in range(2):
                            act.wait_ge(counted_b.sem, it * 2 + (counted_b.base + p2))
                            act.wait_ge(looked[p2].sem, it + looked[p2].base)
                            nc.scalar.copy(hist_sb[:, p2, :], h_ps[:]).then_inc(snap.sem, 1)

                @block.tensor
                def _(pe):
                    with pe.Fori(0, SP_B // (2 * UB)) as it:
                        for par in range(2):
                            pe.wait_ge(onehots[par].sem, it + (onehots[par].base + 1))
                            for b in range(UB):
                                k = par * UB + b
                                p2 = b % 2
                                pe.wait_ge(snap.sem, it * (2 * UB) + (snap.base + k + 1))
                                count(par, b).then_inc(counted_b.sem, 1)
                                pe.wait_ge(ranked[p2].sem, it * UB + (ranked[p2].base + k // 2))
                                for h in range(2):
                                    last = nc.tensor.matmul(look_ps[:, p2, 0:LO], oh_t[:, par, b, h, :],
                                                            hist_sb[:, p2, h * LO:(h + 1) * LO],
                                                            start=(h == 0), stop=(h == 1))
                                last.then_inc(looked[p2].sem, 1)

                @block.vector
                def _(v):
                    ch = Chain(v, dve, per=2 * 6)
                    with v.Fori(0, SP_B // (2 * UB)) as it:
                        ch.start(it)
                        for par in range(2):
                            rv = row[:].rearrange("p (a b) -> p b a", b=SP_B)
                            blocks = bass.ds(it * (2 * UB) + par * UB, UB)
                            for p2 in range(2):
                                v.wait_ge(looked[p2].sem, it * UB + (looked[p2].base + (par * UB) // 2))
                            ch.link(nc.vector.tensor_scalar(hi_t[:], rv[0:HG, blocks, :], 8, None,
                                                            ALU.logical_shift_right))
                            for h in range(2):
                                nc.vector.tensor_scalar(oh_t[:, par, :, h, :], hi_t[:], g.iota_p[0:HG, h:h + 1],
                                                        None, ALU.is_equal)
                            for b in range(UB):
                                i = it * (2 * UB) + (par * UB + b)
                                last = onehots_of(par, b, i)
                            last.then_inc(onehots[par].sem, 1)
                            for b in range(UB):
                                i = it * (2 * UB) + (par * UB + b)
                                nc.vector.scalar_tensor_tensor(
                                    junk_eq[:, par, b, :], rv[:, bass.ds(i, 1), :].rearrange("p a b -> p (a b)"),
                                    key_f[:, bass.ds(i, 1)],
                                    g.earlier[0:SP_P, 0:SP_P], ALU.is_equal, ALU.mult,
                                    accum_out=rank[:, par, 0, b:b + 1])
                            for b in range(UB):
                                i = it * (2 * UB) + (par * UB + b)
                                p2 = b % 2
                                v.wait_ge(looked[p2].sem, it * UB + (looked[p2].base + (par * UB + b) // 2 + 1))
                                nc.vector.scalar_tensor_tensor(
                                    junk_lo[:, par, b, :], g.iota_lo[0:SP_P, :], lo_f[:, bass.ds(i, 1)],
                                    look_ps[:, p2, 0:LO], ALU.is_equal, ALU.mult,
                                    accum_out=rank[:, par, 1, b:b + 1]).then_inc(ranked[p2].sem, 1)
                            for p2 in range(2):
                                v.wait_ge(ranked[p2].sem, it * UB + (ranked[p2].base + (par + 1) * UB // 2))
                            v.wait_ge(scattered[par].sem, it * (16 * UB) + scattered[par].base)
                            ch.step(nc.vector.tensor_copy(rec_stage[:, par, :, :], rec[:, blocks, :]))
                            ch.link(nc.vector.tensor_tensor(pos_i[:, par, :], rank[:, par, 0, :],
                                                            rank[:, par, 1, :], ALU.add))
                            ch.step(nc.vector.tensor_scalar(low_i[:, par, :], pos_i[:, par, :], P - 1, None,
                                                            ALU.bitwise_and))
                            ch.link(nc.vector.tensor_scalar(high_i[:, par, :], pos_i[:, par, :], 7, None,
                                                            ALU.logical_shift_right))
                            ch.link(nc.vector.tensor_scalar(pos[:, par, :], low_i[:, par, :], -float(CH),
                                                            float((P - 1) * CH), ALU.mult, ALU.add))
                            nc.vector.tensor_tensor(place[:, par, :], pos[:, par, :],
                                                    high_i[:, par, :], ALU.add).then_inc(placed[par].sem, 1)
                    ch.loop_done(SP_B // (2 * UB))
                    ch.finish()

                @block.gpsimd
                def _(pool):
                    bound = pool.to_reg(EP - 1)
                    with pool.Fori(0, SP_B // (2 * UB)) as it:
                        for par in range(2):
                            pool.wait_ge(placed[par].sem, it + (placed[par].base + 1))
                            gate(g, pool)
                            for b in range(UB):
                                pool.indirect_dma_start(
                                    out=out, out_offset=bass.IndirectOffsetOnAxis(ap=place[:, par, b:b + 1], axis=0),
                                    in_=rec_stage[:, par, b, :], in_offset=None, bounds_check=bound,
                                    oob_is_err=False).then_inc(scattered[par].sem, 16)
                    for par in range(2):
                        pool.wait_ge(scattered[par].sem, scattered[par].base + 16 * SP_B // 2)
            snap.up(SP_B)
            counted_b.up(SP_B)
            for h in range(2):
                onehots[h].up(steps)
                looked[h].up(SP_B // 2)
                ranked[h].up(SP_B // 2)
                placed[h].up(steps)
                scattered[h].up(16 * SP_B // 2)


class Halves:

    def __init__(self, g, name, k=1, by_pool=False):
        kind = "" if k % 16 else ("pool_dma" if by_pool else "dma")
        self.c = [g.sem(f"{name}{h}", kind) for h in range(2)]
        self.g, self.k = g, k

    def wait(self, eng, half, value):
        eng.wait_ge(self.c[half].sem, value)
        if eng in (self.g.nc.gpsimd, self.g.nc.sync):
            gate(self.g, eng)

    def inc(self, ins, half):
        return ins.then_inc(self.c[half].sem, self.k)

    def this(self, eng, half, it):
        self.wait(eng, half, it * self.k + (self.c[half].base + self.k))

    def part(self, eng, half, it, n):
        self.wait(eng, half, it * self.k + (self.c[half].base + n))

    def two_back(self, eng, half, it):
        self.wait(eng, half, it * self.k + self.c[half].base)

    def one_back(self, eng, half, it):
        self.wait(eng, 1 - half, it * self.k + (self.c[1 - half].base + self.k * half))

    def up(self, tiles):
        for c in self.c:
            c.up(self.k * tiles)


def all_halves(g, *names, k=1):
    return [Halves(g, n, k) for n in names]


class Side:

    def __init__(self, g, name):
        self.name = name
        self.rec = g.rec[name]
        self.key = g.sb(f"{name}_key", [P, CH])
        self.weight = g.sb(f"{name}_weight", [P, CH])
        self.before = g.sb(f"{name}_before", [1, CH])
        self.other_i = g.sb(f"{name}_other_i", [P, CH], I32)
        self.edge_i = g.sb(f"{name}_edge_i", [P, CH], I32)
        self.key_i = g.sb(f"{name}_key_i", [P, CH], I32)
        self.last_i = g.sb(f"{name}_last_i", [P, CH], I32)
        self.key_d = g.dram(f"{name}_key_d", [P, CH])


def side_pass(g, s):
    nc = g.nc
    kc = 1 if s.name == "dst" else 0
    ctx, sb, ps = scope(g)
    with ctx:
        rec = sb("side_rec", [P, CH, 4])
        after = sb("side_after", [P, CH])
        tmp = sb("side_tmp", [P, CH])
        tmp2 = sb("side_tmp2", [P, CH])
        loaded, dve, keyed, wrote = g.sem("side_loaded", "dma"), g.sem("side_dve"), g.sem("side_keyed"), g.sem("side_wrote", "dma")
        shifted = g.sem("side_shifted", "dma")
        with g.block() as block:
            @block.sync
            def _(sp):
                sp.dma_start(rec[:], s.rec.rearrange("(q c) k -> q c k", c=CH)).then_inc(loaded.sem, 16)
                sp.wait_ge(keyed.sem, keyed.base + 1)
                sp.dma_start(s.key_d, s.key[:]).then_inc(wrote.sem, 16)
                sp.wait_ge(wrote.sem, wrote.base + 16)
                sp.dma_start(after[1:P, :], s.key_d[0:P - 1, :]).then_inc(shifted.sem, 16)
                sp.dma_start(after[0:1, 0:CH - 1], s.key_d[P - 1:P, 1:CH]).then_inc(shifted.sem, 16)
                sp.dma_start(s.before[0:1, 1:CH], s.key_d[0:1, 0:CH - 1]).then_inc(shifted.sem, 16)
                sp.wait_ge(shifted.sem, shifted.base + 48)

            @block.vector
            def _(v):
                ch = Chain(v, dve)
                ch.step(nc.vector.memset(after[0:1, CH - 1:CH], -1.0))
                ch.step(nc.vector.memset(s.before[0:1, 0:1], -1.0))
                v.wait_ge(loaded.sem, loaded.base + 16)
                nc.vector.tensor_copy(s.key[:], rec[:, :, kc]).then_inc(keyed.sem, 1)
                ch.step(nc.vector.tensor_copy(s.weight[:], rec[:, :, 2]))
                ch.step(nc.vector.tensor_copy(s.other_i[:], rec[:, :, 0]))
                ch.step(nc.vector.tensor_copy(s.edge_i[:], rec[:, :, 3]))
                v.wait_ge(keyed.sem, keyed.base + 1)
                ch.step(nc.vector.tensor_scalar(s.key_i[:], s.key[:], float(N - 1), None, ALU.min))
                v.wait_ge(shifted.sem, shifted.base + 48)
                ch.link(nc.vector.tensor_tensor(tmp[:], s.key[:], after[:], ALU.is_equal))
                ch.link(nc.vector.tensor_scalar(tmp2[:], tmp[:], float(4 * N), None, ALU.mult))
                ch.link(nc.vector.tensor_tensor(s.last_i[:], tmp2[:], s.key[:], ALU.add))
                ch.finish()
        loaded.up(16)
        keyed.up(1)
        wrote.up(16)
        shifted.up(48)


def key_row_pass(g, s):
    nc = g.nc
    loaded = g.sem("key_row_loaded", "dma")
    with g.block() as block:
        @block.sync
        def _(sp):
            sp.dma_start(g.key_row[:], bcast(s.key_d.rearrange("q c -> (q c)"), P)).then_inc(loaded.sem, 16)
            sp.wait_ge(loaded.sem, loaded.base + 16)
    loaded.up(16)


def chunk_keys(g, c, parts=slice(0, P)):
    return g.key_row[parts, :].rearrange("p (q c) -> p c q", c=CH)[:, bass.ds(c, 1), :].rearrange("p a q -> p (a q)")


def group_keys(g, c, parts=slice(0, P)):
    return g.key_row[parts, :].rearrange("p (q c) -> p c q", c=CH)[:, bass.ds(c, U), :]


class Stage:

    def __init__(self, g, sb, name):
        self.buf = sb(f"stage_{name}", [P, 2, U], I32)
        self.there = Halves(g, f"staged_{name}", 16)

    def load(self, sp, idx, half, it):
        self.there.inc(sp.dma_start(self.buf[:, half, :], idx[:, bass.ds(it * (2 * U) + half * U, U)]), half)


def gather(pool, stage, table, out, half):
    for u in range(U):
        last = pool.indirect_dma_start(out=out(u), out_offset=None, in_=table,
                                       in_offset=bass.IndirectOffsetOnAxis(ap=stage.buf[:, half, u:u + 1], axis=0))
        yield last


STEPS = GROUPS // 2


def edge_pass(g, s, table=None, idx=None, rows=None, width=D, weight=None, heads=None, seg_max=None,
              out=None, out_width=None):
    nc = g.nc
    wide = D + HEADS if heads is not None else (D + 1 if seg_max is not None else width)
    ctx, sb, ps = scope(g)
    with ctx:
        rowbuf = sb("rowbuf", [P, 2, U, AW])
        same = sb("same", [P, 2, U, P])
        carry = sb("carry", [1, 2, U, P])
        sums = sb("sums", [P, 2, U, out_width])
        scaled = sb("scaled", [P, 2, U, AW]) if heads is not None else rowbuf
        sum_ps = ps("sum_ps", [P, U, 512])
        st_in = Stage(g, sb, "gather")
        st_out = Stage(g, sb, "scatter")
        got = Halves(g, "edge_rows", 16 * U if rows is None else 16, by_pool=rows is None)
        put = Halves(g, "edge_put", 16 * U, by_pool=True)
        matrices, = all_halves(g, "edge_matrices")
        used, copied = all_halves(g, "edge_used", "edge_copied", k=U)
        cleared, dve = g.sem("edge_cleared"), g.sem("edge_dve")

        with g.block() as block:
            @block.vector
            def _(v):
                nc.vector.memset(sums[:], 0.0).then_inc(cleared.sem, 1)
                nc.vector.memset(rowbuf[:], 1.0).then_inc(cleared.sem, 1)
                v.wait_ge(cleared.sem, cleared.base + 2)
        cleared.up(2)

        with g.block() as block:
            @block.sync
            def _(sp):
                with sp.Fori(0, STEPS) as it:
                    for half in range(2):
                        if rows is None:
                            got.two_back(sp, half, it)
                            st_in.load(sp, idx, half, it)
                        else:
                            used.two_back(sp, half, it)
                            got.inc(sp.dma_start(rowbuf[:, half, :, 0:D],
                                                 rows[bass.ds(it * 2 + half, 1)].rearrange("a p u d -> (a p) u d")),
                                    half)
                        put.two_back(sp, half, it)
                        st_out.load(sp, s.last_i, half, it)

            @block.gpsimd
            def _(pool):
                bound = pool.to_reg(N - 1)

                def gathers(half, it):
                    st_in.there.this(pool, half, it)
                    used.two_back(pool, half, it)
                    for ins in gather(pool, st_in, table, lambda u: rowbuf[:, half, u, 0:width], half):
                        ins.then_inc(got.c[half].sem, 16)

                def scatters(half, it):
                    st_out.there.this(pool, half, it)
                    copied.this(pool, half, it)
                    if seg_max is not None:
                        matrices.this(pool, half, it)
                    for u in range(U):
                        pool.indirect_dma_start(
                            out=out, out_offset=bass.IndirectOffsetOnAxis(ap=st_out.buf[:, half, u:u + 1], axis=0),
                            in_=sums[:, half, u, :], in_offset=None, bounds_check=bound,
                            oob_is_err=False).then_inc(put.c[half].sem, 16)

                if rows is None:
                    gathers(0, 0)
                with pool.Fori(0, STEPS - 1) as it:
                    for half in range(2):
                        if rows is None:
                            gathers(1 - half, it + half)
                        scatters(half, it)
                if rows is None:
                    gathers(1, STEPS - 1)
                scatters(0, STEPS - 1)
                scatters(1, STEPS - 1)
                for half in range(2):
                    put.two_back(pool, half, STEPS)

            @block.vector
            def _(v):
                with v.Fori(0, STEPS) as it:
                    for half in range(2):
                        first = it * (2 * U) + half * U
                        used.two_back(v, half, it)
                        for u in range(U):
                            args = (None, ALU.is_equal) if weight is None else \
                                (weight[:, bass.ds(first + u, 1)], ALU.is_equal, ALU.mult)
                            nc.vector.tensor_scalar(same[:, half, u, :], chunk_keys(g, first + u),
                                                    s.key[:, bass.ds(first + u, 1)], *args)
                        if seg_max is not None:
                            put.two_back(v, half, it)
                            nc.vector.tensor_copy(sums[:, half, :, D + 1], seg_max[:, bass.ds(first, U)])
                        if heads is not None:
                            got.this(v, half, it)
                            exps = heads[:, bass.ds(first, U), :]
                            for u in range(U):
                                nc.vector.tensor_tensor(
                                    scaled[:, half, u, 0:D].rearrange("p (h f) -> p h f", f=HF),
                                    rowbuf[:, half, u, 0:D].rearrange("p (h f) -> p h f", f=HF),
                                    heads[:, bass.ds(first + u, 1), :].rearrange("p a h -> p (a h)")
                                    .unsqueeze(2).to_broadcast([P, HEADS, HF]), ALU.mult)
                            nc.vector.tensor_copy(scaled[:, half, :, D:D + HEADS], exps)
                        matrices.inc(nc.vector.tensor_tensor(
                            carry[0:1, half, :, :], group_keys(g, first, slice(0, 1)),
                            s.before[0:1, bass.ds(first, U)].unsqueeze(2).to_broadcast([1, U, P]),
                            ALU.is_equal), half)

            @block.tensor
            def _(pe):
                with pe.Fori(0, STEPS) as it:
                    for half in range(2):
                        matrices.this(pe, half, it)
                        if heads is None:
                            got.this(pe, half, it)
                        for u in range(U):
                            nc.tensor.matmul(sum_ps[:, u, 0:wide], same[:, half, u, :],
                                             scaled[:, half, u, 0:wide], start=True, stop=False)
                            if u:
                                copied.part(pe, half, it, u)
                            else:
                                copied.one_back(pe, half, it)
                            prev = sums[0:1, half, u - 1, 0:wide] if u else sums[0:1, 1 - half, U - 1, 0:wide]
                            ins = nc.tensor.matmul(sum_ps[:, u, 0:wide], carry[0:1, half, u, :], prev,
                                                   start=False, stop=True)
                            ins.then_inc(used.c[half].sem, 1)

            @block.scalar
            def _(act):
                with act.Fori(0, STEPS) as it:
                    for half in range(2):
                        put.two_back(act, half, it)
                        for u in range(U):
                            used.part(act, half, it, u + 1)
                            ins = nc.scalar.copy(sums[:, half, u, 0:wide], sum_ps[:, u, 0:wide])
                            ins.then_inc(copied.c[half].sem, 1)
        if rows is None:
            st_in.there.up(STEPS)
        st_out.there.up(STEPS)
        for h in (got, put, matrices, used, copied):
            h.up(STEPS)


def weights_pass(g, a):
    nc = g.nc
    g.w_proj = g.sb("w_proj", [P, D + 2 * HEADS])
    g.w_skip = g.sb("w_skip", [P, D])
    g.w1 = g.sb("w1", [P, HID])
    g.w2 = g.sb("w2", [HID + 1, D])
    g.b1 = g.sb("b1", [P, HID])
    g.att = g.sb("att", [P, 2 * D])
    g.att_b = g.sb("att_b", [P, 1])
    g.w_in = g.sb("w_in", [P, 3, 3 * D])
    g.w_hid = g.sb("w_hid", [P, 3 * D])
    g.b_in = g.sb("b_in", [P, 3])
    g.b_hid = g.sb("b_hid", [P, 3])
    g.b_sum = g.sb("b_sum", [P, 3])
    g.minus_half = g.sb("minus_half", [P, NJ])
    ctx, sb, ps = scope(g)
    with ctx:
        a_src, a_tgt = sb("a_src", [P, D]), sb("a_tgt", [P, D])
        prod = sb("prod", [P, 2, D])
        rows_in = sb("rows_in", [P, 3, D])
        rows_hid = sb("rows_hid", [P, 3, D])
        w_step = sb("w_step", [P, 3, D])
        in_t = sb("in_t", [P, 3 * D])
        step_t = sb("step_t", [P, 3 * D])
        t_ps = ps("t_ps", [P, 3, 512])
        c_ps = ps("c_ps", [P, 3, 512])
        loaded, dve, turned, copied = g.sem("w_loaded", "dma"), g.sem("w_dve"), g.sem("w_turned"), g.sem("w_copied")
        with g.block() as block:
            @block.sync
            def _(sp):
                one = lambda v: bcast(v, P)
                n = 0
                loads = [
                    (g.w_proj[:, 0:D], a["L0_gnn_W_proj"]), (g.w_skip[:], a["L0_gnn_W_skip"]),
                    (a_src[:], one(a["L0_gnn_a_src"].rearrange("a h f -> (a h f)"))),
                    (a_tgt[:], one(a["L0_gnn_a_tgt"].rearrange("a h f -> (a h f)"))),
                    (g.w1[:], a["L1_gnn_w1"]), (g.w2[0:HID, :], a["L1_gnn_w2"]),
                    (g.w2[HID:HID + 1, :], a["L1_gnn_b2"].rearrange("(a n) -> a n", a=1)),
                    (g.b1[:], one(a["L1_gnn_b1"])), (g.att[:], one(a["L2_gnn_W_att_w"])),
                    (g.att_b[:], one(a["L2_gnn_W_att_b"])),
                    (rows_in[:], a["L3_gnn_w_ih"].rearrange("(t p) n -> p t n", p=P)),
                    (rows_hid[:], a["L3_gnn_w_hh"].rearrange("(t p) n -> p t n", p=P)),
                    (w_step[:], a["L3_gnn_W"].rearrange("t p n -> p t n")),
                ]
                for to, of in loads:
                    sp.dma_start(to, of).then_inc(loaded.sem, 16)
                with nc.allow_non_contiguous_dma(reason="384 biases, once"):
                    for to, name in ((g.b_in, "L3_gnn_b_ih"), (g.b_hid, "L3_gnn_b_hh")):
                        sp.dma_start(to[:], a[name].rearrange("(t p) -> p t", p=P)).then_inc(loaded.sem, 16)
                sp.wait_ge(loaded.sem, loaded.base + 16 * (len(loads) + 2))
                loaded.up(16 * (len(loads) + 2))
        with g.block() as block:
            @block.vector
            def _(v):
                ch = Chain(v, dve)
                ch.step(nc.vector.memset(g.minus_half[:], -0.5))
                ch.step(nc.vector.tensor_tensor(g.b_sum[:], g.b_in[:], g.b_hid[:], ALU.add))
                ch.step(nc.vector.tensor_tensor(prod[:, 0, :], g.w_proj[:, 0:D], a_src[:], ALU.mult))
                ch.link(nc.vector.tensor_tensor(prod[:, 1, :], g.w_proj[:, 0:D], a_tgt[:], ALU.mult))
                ch.link(nc.vector.reduce_sum(g.w_proj[:, D:D + 2 * HEADS],
                                             prod[:].rearrange("p t (h f) -> p (t h) f", f=HF), AX_X))
                for n, to in enumerate((in_t, g.w_hid, step_t)):
                    v.wait_ge(turned.sem, turned.base + n + 1)
                    nc.vector.tensor_copy(to[:], t_ps[:, n, 0:3 * D]).then_inc(copied.sem, 1)
                for i in range(3):
                    v.wait_ge(turned.sem, turned.base + 4 + i)
                    ch.step(nc.vector.tensor_copy(g.w_in[:, i, :], c_ps[:, i, 0:3 * D]))
                ch.hold()
                ch.finish()

            @block.tensor
            def _(pe):
                for n, of in enumerate((rows_in, rows_hid, w_step)):
                    for t in range(3):
                        last = nc.tensor.transpose(t_ps[:, n, t * D:(t + 1) * D], of[:, t, :], g.ident[:])
                    last.then_inc(turned.sem, 1)
                pe.wait_ge(copied.sem, copied.base + 3)
                for i in range(3):
                    nc.tensor.matmul(c_ps[:, i, 0:3 * D], step_t[:, i * D:(i + 1) * D], in_t[:],
                                     start=True, stop=True).then_inc(turned.sem, 1)
        turned.up(6)
        copied.up(3)


def tile_of(table, width, t):
    return table.rearrange("(t p j) w -> t p (j w)", p=NP_, j=NJ)[bass.ds(t, 1)].rearrange("a p m -> (a p) m")


def flat(ap):
    return ap.rearrange("p j w -> p (j w)")


def tiles(eng):
    with eng.Fori(0, TILES // 2) as it:
        for half in range(2):
            yield it, half


def run_tiles(eng, *steps):
    def at(it, n):
        return it + n // 2, n % 2

    def whole(t):
        for offset, step in steps:
            if 0 <= t + offset < TILES:
                step(*at(0, t + offset))

    whole(-1)
    whole(0)
    with eng.Fori(0, TILES // 2 - 1) as it:
        for n in (1, 2):
            for offset, step in steps:
                step(*at(it, n + offset))
    whole(TILES - 1)
    whole(TILES)


def turn(g, out_ps, tile, width=D):
    for j in range(NJ):
        last = g.nc.tensor.transpose(out_ps[0:width, j * NP_:(j + 1) * NP_], tile[:, j, :], g.ident[0:NP_, 0:NP_])
    return last


class Norm:

    def __init__(self, g, sb):
        self.g = g
        self.stats = sb("ln_stats", [NP_, 2, NJ, 6])
        self.mv = sb("ln_mv", [NP_, 2, NJ, 2])
        self.ve = sb("ln_ve", [NP_, 2, NJ])
        self.rstd = sb("ln_rstd", [NP_, 2, NJ])
        self.stats_there, self.mv_there, self.var_there, self.rstd_there = \
            all_halves(g, "ln_stats", "ln_mv", "ln_var", "ln_rstd")

    def moments(self, v, y, half, it):
        nc = self.g.nc
        for j in range(NJ):
            last = nc.vector.bn_stats(self.stats[:, half, j, :], y[:, j, :])
        self.stats_there.inc(last, half)
        self.stats_there.this(v, half, it)
        gate(self.g, v)
        for j in range(NJ):
            last = nc.vector.bn_aggr(self.mv[:, half, j, :], self.stats[:, half, j, :])
        self.mv_there.inc(last, half)
        self.mv_there.this(v, half, it)
        self.var_there.inc(nc.vector.tensor_scalar(self.ve[:, half, :], self.mv[:, half, :, 1], LN_EPS, None,
                                                   ALU.add), half)

    def power(self, pool, half, it):
        self.var_there.this(pool, half, it)
        self.rstd_there.inc(self.g.nc.gpsimd.tensor_tensor(
            self.rstd[:, half, :], self.ve[:, half, :], self.g.minus_half[0:NP_, :], ALU.pow), half)

    def scale(self, v, out, y, half, it):
        self.rstd_there.this(v, half, it)
        for j in range(NJ):
            last = self.g.nc.vector.tensor_scalar(out[:, j, :], y[:, j, :], self.mv[:, half, j, 0:1],
                                                  self.rstd[:, half, j:j + 1], ALU.subtract, ALU.mult)
        return last

    def up(self):
        for h in (self.stats_there, self.mv_there, self.var_there, self.rstd_there):
            h.up(TILES // 2)


def gat_project_pass(g, x):
    nc = g.nc
    g.proj = g.dram("proj", [N, AW])
    g.tgt_score = g.dram("tgt_score", [N, HEADS])
    W = D + 2 * HEADS
    ctx, sb, ps = scope(g)
    with ctx:
        xin = sb("xin", [NP_, 2, NJ, D])
        x_t = sb("x_t", [P, 2, NB])
        pout = sb("pout", [NP_, 2, NJ, AW])
        sout = sb("sout", [NP_, 2, NJ, HEADS])
        t_ps = ps("t_ps", [P, 2, 512])
        o_ps = ps("o_ps", [NP_, 2, 2, 512])
        loaded, stored = Halves(g, "node_loaded", 16), Halves(g, "node_stored", 32, by_pool=True)
        turned, x_t_there, product, ready = all_halves(g, "node_turned", "node_turned_sb", "node_product", "node_ready")
        with g.block() as block:
            @block.sync
            def _(sp):
                for it, half in tiles(sp):
                    turned.two_back(sp, half, it)
                    loaded.inc(sp.dma_start(flat(xin[:, half]), tile_of(x, D, it * 2 + half)), half)

            @block.tensor
            def _(pe):
                for it, half in tiles(pe):
                    loaded.this(pe, half, it)
                    x_t_there.two_back(pe, half, it)
                    turned.inc(turn(g, t_ps[:, half], xin[:, half]), half)
                    x_t_there.this(pe, half, it)
                    ready.two_back(pe, half, it)
                    for j in range(NJ):
                        last = nc.tensor.matmul(o_ps[:, half, j // 3, (j % 3) * W:(j % 3 + 1) * W],
                                                x_t[:, half, j * NP_:(j + 1) * NP_], g.w_proj[:],
                                                start=True, stop=True)
                    product.inc(last, half)

            @block.scalar
            def _(act):
                for it, half in tiles(act):
                    turned.this(act, half, it)
                    product.two_back(act, half, it)
                    x_t_there.inc(nc.scalar.copy(x_t[:, half, :], t_ps[:, half, 0:NB]), half)

            @block.vector
            def _(v):
                for it, half in tiles(v):
                    product.this(v, half, it)
                    stored.two_back(v, half, it)
                    for b, js in ((0, slice(0, 3)), (1, slice(3, 5))):
                        n = js.stop - js.start
                        o = o_ps[:, half, b, 0:n * W].rearrange("p (j w) -> p j w", w=W)
                        nc.vector.tensor_copy(pout[:, half, js, :], o[:, :, 0:AW])
                        last = nc.vector.tensor_copy(sout[:, half, js, :], o[:, :, AW:W])
                    ready.inc(last, half)

            @block.gpsimd
            def _(pool):
                for it, half in tiles(pool):
                    ready.this(pool, half, it)
                    t = it * 2 + half
                    pool.dma_start(tile_of(g.proj, AW, t), flat(pout[:, half])).then_inc(stored.c[half].sem, 16)
                    pool.dma_start(tile_of(g.tgt_score, HEADS, t), flat(sout[:, half])).then_inc(stored.c[half].sem, 16)
                for half in range(2):
                    stored.two_back(pool, half, TILES // 2)
        for h in (loaded, stored, turned, x_t_there, product, ready):
            h.up(TILES // 2)


def gat_score_pass(g, s, e_sb):
    nc = g.nc
    ctx, sb, ps = scope(g)
    with ctx:
        rowbuf = sb("rowbuf", [P, 2, U, AW])
        tgt = sb("tgt", [P, 2, U, HEADS])
        raw = sb("raw", [P, 2, U, HEADS])
        gmax = sb("gmax", [P, 3])
        st_src, st_key = Stage(g, sb, "gather"), Stage(g, sb, "second")
        got = Halves(g, "score_rows", 16 * U * 2, by_pool=True)
        kept = Halves(g, "score_kept", 16)
        summed, scored = all_halves(g, "score_sum", "score_done")
        with g.block() as block:
            @block.sync
            def _(sp):
                def keep(half, it):
                    got.this(sp, half, it)
                    kept.inc(sp.dma_start(g.rows[bass.ds(it * 2 + half, 1)].rearrange("a p u d -> (a p) u d"),
                                          rowbuf[:, half, :, 0:D]), half)
                with sp.Fori(0, STEPS) as it:
                    for half in range(2):
                        got.two_back(sp, half, it)
                        st_src.load(sp, s.other_i, half, it)
                        st_key.load(sp, s.key_i, half, it)
                        keep(half, it)
                for half in range(2):
                    kept.two_back(sp, half, STEPS)

            @block.gpsimd
            def _(pool):
                with pool.Fori(0, STEPS) as it:
                    for half in range(2):
                        st_src.there.this(pool, half, it)
                        st_key.there.this(pool, half, it)
                        summed.two_back(pool, half, it)
                        kept.two_back(pool, half, it)
                        for ins in gather(pool, st_src, g.proj, lambda u: rowbuf[:, half, u, :], half):
                            ins.then_inc(got.c[half].sem, 16)
                        for ins in gather(pool, st_key, g.tgt_score, lambda u: tgt[:, half, u, :], half):
                            ins.then_inc(got.c[half].sem, 16)

            @block.vector
            def _(v):
                with v.Fori(0, STEPS) as it:
                    for half in range(2):
                        got.this(v, half, it)
                        summed.inc(nc.vector.tensor_tensor(raw[:, half], rowbuf[:, half, :, D:AW], tgt[:, half],
                                                           ALU.add), half)
                        summed.this(v, half, it)
                        scored.inc(nc.vector.scalar_tensor_tensor(
                            e_sb[:, bass.ds(it * (2 * U) + half * U, U), :], raw[:, half], 0.2, raw[:, half],
                            ALU.mult, ALU.max), half)
                        scored.this(v, half, it)
        for h in (st_src.there, st_key.there, got, kept, summed, scored):
            h.up(STEPS)
        dve, maxed, negated, powered = g.sem("max_dve"), g.sem("max_all"), g.sem("max_neg"), g.sem("max_exp")
        dve_base = dve.base
        with g.block() as block:
            @block.vector
            def _(v):
                ch = Chain(v, dve)
                ch.link(nc.vector.memset(e_sb[0:88, CH - 1, :], FAR))
                ch.step(nc.vector.reduce_max(gmax[:, 0:1], e_sb[:].rearrange("p c h -> p (c h)"), AX_X))
                v.wait_ge(maxed.sem, maxed.base + 1)
                nc.vector.tensor_scalar(gmax[:, 2:3], gmax[:, 1:2], -1.0, None, ALU.mult).then_inc(negated.sem, 1)
                ch.finish()

            @block.gpsimd
            def _(pool):
                pool.wait_ge(dve.sem, dve_base + 2)
                nc.gpsimd.partition_all_reduce(gmax[:, 1:2], gmax[:, 0:1], P, RMAX).then_inc(maxed.sem, 1)

            @block.scalar
            def _(act):
                act.wait_ge(negated.sem, negated.base + 1)
                nc.scalar.activation(e_sb[:], e_sb[:], ACT.Exp, bias=gmax[:, 2:3]).then_inc(powered.sem, 1)
                act.wait_ge(powered.sem, powered.base + 1)
        maxed.up(1)
        negated.up(1)
        powered.up(1)


def gat_finish_pass(g, x):
    nc = g.nc
    g.x1 = g.dram("x1", [N, D])
    g.hid_a = g.dram("hid_a", [N, HID])
    ctx, sb, ps = scope(g)
    with ctx:
        xin = sb("xin", [NP_, 2, NJ, D])
        agg = sb("agg", [NP_, 2, NJ, AW])
        x_t = sb("x_t", [P, NB])
        y_t = sb("y_t", [P, NB])
        den = sb("den", [NP_, 2, NJ, HEADS])
        rden = sb("rden", [NP_, 2, NJ, HEADS])
        t = sb("t", [NP_, 2, NJ, D])
        low = sb("low", [NP_, 2, NJ, D])
        y = sb("y", [NP_, 2, NJ, D])
        x1 = sb("x1_sb", [NP_, 2, NJ, D])
        h = sb("h_sb", [NP_, 2, NJ, HID])
        t_ps = ps("t_ps", [P, 2, 512])
        o_ps = ps("o_ps", [NP_, 2, 2, 512])
        h_ps = ps("h_ps", [NP_, 512])
        ln = Norm(g, sb)
        loaded, stored = Halves(g, "node_loaded", 32), Halves(g, "node_stored", 32, by_pool=True)
        names = ("node_turned", "node_turned_sb", "node_product", "node_ready", "fin_t", "fin_exp", "fin_turned",
                 "fin_turned_sb", "fin_product", "fin_h", "fin_sum")
        turned, x_t_there, product, x1_there, t_there, exped, turned1, y_t_there, product1, h_there, summed = \
            all_halves(g, *names)
        dve = g.sem("node_dve")
        with g.block() as block:
            @block.sync
            def _(sp):
                for it, half in tiles(sp):
                    summed.two_back(sp, half, it)
                    turned.two_back(sp, half, it)
                    tt = it * 2 + half
                    sp.dma_start(flat(xin[:, half]), tile_of(x, D, tt)).then_inc(loaded.c[half].sem, 16)
                    sp.dma_start(flat(agg[:, half]), tile_of(g.agg_dst, AW, tt)).then_inc(loaded.c[half].sem, 16)

            @block.tensor
            def _(pe):
                def first(it, half):
                    loaded.this(pe, half, it)
                    x_t_there.one_back(pe, half, it)
                    turned.inc(turn(g, t_ps[:, 0], xin[:, half]), half)
                    x_t_there.this(pe, half, it)
                    t_there.two_back(pe, half, it)
                    for j in range(NJ):
                        last = nc.tensor.matmul(o_ps[:, half, j // 4, (j % 4) * D:(j % 4 + 1) * D],
                                                x_t[:, j * NP_:(j + 1) * NP_], g.w_skip[:], start=True, stop=True)
                    product.inc(last, half)

                def second(it, half):
                    x1_there.this(pe, half, it)
                    y_t_there.one_back(pe, half, it)
                    turned1.inc(turn(g, t_ps[:, 1], x1[:, half]), half)
                    y_t_there.this(pe, half, it)
                    h_there.one_back(pe, half, it)
                    for j in range(NJ):
                        last = nc.tensor.matmul(h_ps[:, j * HID:(j + 1) * HID], y_t[:, j * NP_:(j + 1) * NP_],
                                                g.w1[:], start=True, stop=True)
                    product1.inc(last, half)

                run_tiles(pe, (1, first), (0, second))

            @block.scalar
            def _(act):
                def first(it, half):
                    turned.this(act, half, it)
                    product.one_back(act, half, it)
                    x_t_there.inc(nc.scalar.copy(x_t[:], t_ps[:, 0, 0:NB]), half)
                    t_there.this(act, half, it)
                    exped.inc(nc.scalar.activation(low[:, half], low[:, half], ACT.Exp), half)

                def second(it, half):
                    turned1.this(act, half, it)
                    product1.one_back(act, half, it)
                    y_t_there.inc(nc.scalar.copy(y_t[:], t_ps[:, 1, 0:NB]), half)
                    product1.this(act, half, it)
                    stored.two_back(act, half, it)
                    h_there.inc(nc.scalar.copy(flat(h[:, half]), h_ps[:, 0:NJ * HID]), half)

                run_tiles(act, (1, first), (0, second))

            @block.vector
            def _(v):
                ch = Chain(v, dve, per=2 * 9)
                with v.Fori(0, TILES // 2) as it:
                    ch.start(it)
                    for half in range(2):
                        loaded.this(v, half, it)
                        ch.link(nc.vector.tensor_scalar(den[:, half], agg[:, half, :, D:AW], 1e-16, None, ALU.add))
                        ch.link(nc.vector.reciprocal(rden[:, half], den[:, half]))
                        for j in range(NJ):
                            ch.step(nc.vector.tensor_tensor(
                                t[:, half, j].rearrange("p (h f) -> p h f", f=HF),
                                agg[:, half, j, 0:D].rearrange("p (h f) -> p h f", f=HF),
                                rden[:, half, j].unsqueeze(2).to_broadcast([NP_, HEADS, HF]), ALU.mult))
                        product.this(v, half, it)
                        ch.hold()
                        for js, b in ((slice(0, 4), 0), (slice(4, 5), 1)):
                            n = (js.stop - js.start) * D
                            last = nc.vector.tensor_tensor(flat(t[:, half, js]), flat(t[:, half, js]),
                                                           o_ps[:, half, b, 0:n], ALU.add)
                        ch.link(last)
                        t_there.inc(nc.vector.tensor_scalar(low[:, half], t[:, half], 0.0, None, ALU.min), half)
                        exped.this(v, half, it)
                        ch.link(nc.vector.scalar_tensor_tensor(flat(t[:, half]), flat(t[:, half]), 0.0,
                                                               flat(low[:, half]), ALU.max, ALU.add))
                        nc.vector.scalar_tensor_tensor(flat(y[:, half]), flat(t[:, half]), -1.0,
                                                       flat(xin[:, half]), ALU.add, ALU.add) \
                            .then_inc(summed.c[half].sem, 1)
                        summed.this(v, half, it)
                        ln.moments(v, y[:, half], half, it)
                        stored.two_back(v, half, it)
                        turned1.two_back(v, half, it)
                        x1_there.inc(ln.scale(v, x1[:, half], y[:, half], half, it), half)
                ch.loop_done(TILES // 2)
                ch.finish()

            @block.gpsimd
            def _(pool):
                for it, half in tiles(pool):
                    ln.power(pool, half, it)
                    x1_there.this(pool, half, it)
                    tt = it * 2 + half
                    pool.dma_start(tile_of(g.x1, D, tt), flat(x1[:, half])).then_inc(stored.c[half].sem, 16)
                    h_there.this(pool, half, it)
                    pool.dma_start(tile_of(g.hid_a, HID, tt), flat(h[:, half])).then_inc(stored.c[half].sem, 16)
                for half in range(2):
                    stored.two_back(pool, half, TILES // 2)
        ln.up()
        for h_ in (loaded, stored, turned, x_t_there, product, x1_there, t_there, exped, turned1, y_t_there,
                   product1, h_there, summed):
            h_.up(TILES // 2)


def gcn_hidden_pass(g):
    nc = g.nc
    g.hid_b = g.dram("hid_b", [N, HID])
    ctx, sb, ps = scope(g)
    with ctx:
        agg = sb("agg", [NP_, 2, NJ, HID])
        pre = sb("pre", [NP_, 2, NJ, HID])
        h = sb("h", [NP_, 2, NJ, HID])
        loaded, stored = Halves(g, "node_loaded1", 16), Halves(g, "node_stored1", 16, by_pool=True)
        biased, squashed = all_halves(g, "hid_biased", "hid_squashed")
        with g.block() as block:
            @block.sync
            def _(sp):
                for it, half in tiles(sp):
                    biased.two_back(sp, half, it)
                    loaded.inc(sp.dma_start(flat(agg[:, half]), tile_of(g.agg_hid, HID, it * 2 + half)), half)

            @block.vector
            def _(v):
                for it, half in tiles(v):
                    loaded.this(v, half, it)
                    squashed.two_back(v, half, it)
                    biased.inc(nc.vector.tensor_tensor(
                        pre[:, half], agg[:, half], g.b1[0:NP_, :].unsqueeze(1).to_broadcast([NP_, NJ, HID]),
                        ALU.add), half)

            @block.scalar
            def _(act):
                for it, half in tiles(act):
                    biased.this(act, half, it)
                    stored.two_back(act, half, it)
                    squashed.inc(nc.scalar.activation(flat(h[:, half]), flat(pre[:, half]), ACT.Sigmoid), half)

            @block.gpsimd
            def _(pool):
                for it, half in tiles(pool):
                    squashed.this(pool, half, it)
                    stored.inc(pool.dma_start(tile_of(g.hid_b, HID, it * 2 + half), flat(h[:, half])), half)
                for half in range(2):
                    stored.two_back(pool, half, TILES // 2)
        for h_ in (loaded, stored, biased, squashed):
            h_.up(TILES // 2)


def gcn_finish_pass(g):
    nc = g.nc
    g.x2 = g.dram("x2", [N, D])
    g.node_score = g.dram("node_score", [N, 1])
    ctx, sb, ps = scope(g)
    with ctx:
        xin = sb("xin", [NP_, 2, NJ, D])
        agg = sb("agg", [NP_, 2, NJ, HID])
        a_t = sb("a_t", [HID + 1, 2, NB])
        sig = sb("sig", [NP_, 2, NJ, D])
        y = sb("y", [NP_, 2, NJ, D])
        x2 = sb("x2_sb", [NP_, 2, NJ, D])
        prod = sb("prod", [NP_, 2, NJ, D])
        dot = sb("dot", [NP_, 2, NJ])
        sc = sb("sc", [NP_, 2, NJ])
        t_ps = ps("t_ps", [P, 2, 512])
        o_ps = ps("o_ps", [NP_, 2, 2, 512])
        ln = Norm(g, sb)
        loaded, stored = Halves(g, "node_loaded", 32), Halves(g, "node_stored", 32, by_pool=True)
        turned, a_t_there, product, squashed, summed, x2_there, weighted, dotted, scored = all_halves(
            g, "node_turned", "node_turned_sb", "node_product", "gcn_squashed", "gcn_summed", "gcn_x2", "gcn_weighted",
            "gcn_dotted", "gcn_scored")
        ones = g.sem("gcn_ones")
        with g.block() as block:
            @block.vector
            def _(v):
                nc.vector.memset(a_t[HID:HID + 1, :, :], 1.0).then_inc(ones.sem, 1)
                v.wait_ge(ones.sem, ones.base + 1)
        ones.up(1)
        with g.block() as block:
            @block.sync
            def _(sp):
                for it, half in tiles(sp):
                    summed.two_back(sp, half, it)
                    turned.two_back(sp, half, it)
                    t = it * 2 + half
                    sp.dma_start(flat(xin[:, half]), tile_of(g.x1, D, t)).then_inc(loaded.c[half].sem, 16)
                    sp.dma_start(flat(agg[:, half]), tile_of(g.agg_hid, HID, t)).then_inc(loaded.c[half].sem, 16)

            @block.tensor
            def _(pe):
                def turns(it, half):
                    loaded.this(pe, half, it)
                    a_t_there.two_back(pe, half, it)
                    gate(g, pe)
                    turned.inc(turn(g, t_ps[:, half], agg[:, half], HID), half)

                def products(it, half):
                    a_t_there.this(pe, half, it)
                    squashed.two_back(pe, half, it)
                    for j in range(NJ):
                        last = nc.tensor.matmul(o_ps[:, half, j // 4, (j % 4) * D:(j % 4 + 1) * D],
                                                a_t[:, half, j * NP_:(j + 1) * NP_], g.w2[:], start=True, stop=True)
                    product.inc(last, half)

                run_tiles(pe, (1, turns), (0, products))

            @block.scalar
            def _(act):
                def copies(it, half):
                    turned.this(act, half, it)
                    product.two_back(act, half, it)
                    a_t_there.inc(nc.scalar.copy(a_t[0:HID, half, :], t_ps[0:HID, half, 0:NB]), half)

                def squash(it, half):
                    product.this(act, half, it)
                    summed.two_back(act, half, it)
                    nc.scalar.activation(flat(sig[:, half, 0:4]), o_ps[:, half, 0, 0:4 * D], ACT.Sigmoid)
                    squashed.inc(nc.scalar.activation(sig[:, half, 4], o_ps[:, half, 1, 0:D], ACT.Sigmoid), half)

                run_tiles(act, (1, copies), (0, squash))

            @block.vector
            def _(v):
                for it, half in tiles(v):
                    loaded.this(v, half, it)
                    squashed.this(v, half, it)
                    summed.inc(nc.vector.tensor_tensor(y[:, half], sig[:, half], xin[:, half], ALU.add), half)
                    summed.this(v, half, it)
                    ln.moments(v, y[:, half], half, it)
                    stored.two_back(v, half, it)
                    x2_there.inc(ln.scale(v, x2[:, half], y[:, half], half, it), half)
                    x2_there.this(v, half, it)
                    weighted.inc(nc.vector.tensor_tensor(
                        prod[:, half], x2[:, half], g.att[0:NP_, 0:D].unsqueeze(1).to_broadcast([NP_, NJ, D]),
                        ALU.mult), half)
                    weighted.this(v, half, it)
                    dotted.inc(nc.vector.reduce_sum(dot[:, half], prod[:, half], AX_X), half)
                    dotted.this(v, half, it)
                    scored.inc(nc.vector.tensor_scalar(sc[:, half], dot[:, half], g.att_b[0:NP_, :], None, ALU.add),
                               half)

            @block.gpsimd
            def _(pool):
                def powers(it, half):
                    ln.power(pool, half, it)

                def stores(it, half):
                    x2_there.this(pool, half, it)
                    t = it * 2 + half
                    pool.dma_start(tile_of(g.x2, D, t), flat(x2[:, half])).then_inc(stored.c[half].sem, 16)
                    scored.this(pool, half, it)
                    pool.dma_start(tile_of(g.node_score, 1, t), sc[:, half]).then_inc(stored.c[half].sem, 16)

                run_tiles(pool, (0, powers), (0, stores))
                for half in range(2):
                    stored.two_back(pool, half, TILES // 2)
        ln.up()
        for h in (loaded, stored, turned, a_t_there, product, squashed, summed, x2_there, weighted, dotted, scored):
            h.up(TILES // 2)


def att_score_pass(g, s, edge_attr, score, top):
    nc = g.nc
    ctx, sb, ps = scope(g)
    with ctx:
        rowbuf = sb("rowbuf", [P, 2, U, D])
        node = sb("node", [P, 2, U])
        junk = sb("junk", [P, 2, U, D], BF16)
        dot = sb("dot", [P, 2, U])
        raw = sb("raw", [P, 2, U])
        leaky = sb("leaky", [P, 2, U])
        diag = sb("diag", [P, 2, U, P])
        far = sb("far", [P, 2, U, P])
        full = sb("full", [P, 2, U, P])
        ones = sb("ones", [P, P])
        row_ps = ps("row_ps", [P, 2, 1024])
        st_edge, st_key = Stage(g, sb, "gather"), Stage(g, sb, "second")
        got = Halves(g, "score_rows", 16 * U * 2, by_pool=True)
        kept = Halves(g, "score_kept", 16)
        dotted, summed, scored, diagonal, apart, spread, masked, topped = all_halves(
            g, "att_dotted", "att_summed", "att_scored", "att_diagonal", "att_apart", "att_spread", "att_masked", "att_topped")
        set_up = g.sem("att_ones")
        with g.block() as block:
            @block.vector
            def _(v):
                nc.vector.memset(ones[:], 1.0).then_inc(set_up.sem, 1)
                v.wait_ge(set_up.sem, set_up.base + 1)
        set_up.up(1)
        with g.block() as block:
            @block.sync
            def _(sp):
                with sp.Fori(0, STEPS) as it:
                    for half in range(2):
                        got.two_back(sp, half, it)
                        st_edge.load(sp, s.edge_i, half, it)
                        st_key.load(sp, s.key_i, half, it)
                        got.this(sp, half, it)
                        kept.inc(sp.dma_start(g.rows[bass.ds(it * 2 + half, 1)].rearrange("a p u d -> (a p) u d"),
                                              rowbuf[:, half]), half)
                for half in range(2):
                    kept.two_back(sp, half, STEPS)

            @block.gpsimd
            def _(pool):
                with pool.Fori(0, STEPS) as it:
                    for half in range(2):
                        st_edge.there.this(pool, half, it)
                        st_key.there.this(pool, half, it)
                        summed.two_back(pool, half, it)
                        kept.two_back(pool, half, it)
                        for ins in gather(pool, st_edge, edge_attr, lambda u: rowbuf[:, half, u, :], half):
                            ins.then_inc(got.c[half].sem, 16)
                        for ins in gather(pool, st_key, g.node_score, lambda u: node[:, half, u:u + 1], half):
                            ins.then_inc(got.c[half].sem, 16)

            @block.tensor
            def _(pe):
                with pe.Fori(0, STEPS) as it:
                    for half in range(2):
                        diagonal.this(pe, half, it)
                        masked.two_back(pe, half, it)
                        for u in range(U):
                            last = nc.tensor.matmul(row_ps[:, half, u * P:(u + 1) * P], ones[:],
                                                    diag[:, half, u, :], start=True, stop=True)
                        spread.inc(last, half)

            @block.vector
            def _(v):
                with v.Fori(0, STEPS) as it:
                    for half in range(2):
                        first = it * (2 * U) + half * U
                        got.this(v, half, it)
                        for u in range(U):
                            last = nc.vector.scalar_tensor_tensor(
                                junk[:, half, u, :], rowbuf[:, half, u, :], 1.0, g.att[:, D:2 * D], ALU.mult,
                                ALU.mult, accum_out=dot[:, half, u:u + 1])
                        dotted.inc(last, half)
                        dotted.this(v, half, it)
                        summed.inc(nc.vector.tensor_tensor(raw[:, half], dot[:, half], node[:, half], ALU.add), half)
                        summed.this(v, half, it)
                        scored.inc(nc.vector.scalar_tensor_tensor(leaky[:, half], raw[:, half], 0.2, raw[:, half],
                                                                  ALU.mult, ALU.max), half)
                        scored.this(v, half, it)
                        nc.vector.tensor_copy(score[:, bass.ds(first, U)], leaky[:, half])
                        for u in range(U):
                            last = nc.vector.tensor_scalar(diag[:, half, u, :], g.ident[:], leaky[:, half, u:u + 1],
                                                           None, ALU.mult)
                        diagonal.inc(last, half)
                        for u in range(U):
                            last = nc.vector.tensor_scalar(far[:, half, u, :], chunk_keys(g, first + u),
                                                           s.key[:, bass.ds(first + u, 1)], FAR, ALU.not_equal,
                                                           ALU.mult)
                        apart.inc(last, half)
                        apart.this(v, half, it)
                        spread.this(v, half, it)
                        masked.inc(nc.vector.tensor_tensor(
                            full[:, half].rearrange("p u q -> p (u q)"), far[:, half].rearrange("p u q -> p (u q)"),
                            row_ps[:, half, 0:U * P], ALU.add), half)
                        masked.this(v, half, it)
                        topped.inc(nc.vector.reduce_max(top[:, bass.ds(first, U)], full[:, half], AX_X), half)
                        topped.this(v, half, it)
        for h in (st_edge.there, st_key.there, got, kept, dotted, summed, scored, diagonal, apart,
                  spread, masked, topped):
            h.up(STEPS)


def att_max_pass(g, s, score, top):
    nc = g.nc
    ctx, sb, ps = scope(g)
    with ctx:
        key_first = sb("key_first", [1, CH])
        top_first = sb("top_first", [1, CH])
        whole = sb("whole", [1, CH])
        goes_on = sb("goes_on", [1, 2, CH])
        pen = sb("pen", [1, 2, CH])
        run = sb("run", [1, 2, CH])
        rows = sb("rows", [1, 4, CH])
        wide = sb("wide", [P, 4, CH])
        t1 = sb("t1", [P, 2, CH])
        t2 = sb("t2", [P, 2, CH])
        loaded, dve, spread, powered = g.sem("amax_loaded", "dma"), g.sem("amax_dve"), g.sem("amax_spread"), g.sem("amax_exp")
        with g.block() as block:
            @block.sync
            def _(sp):
                sp.dma_start(key_first[:], s.key_d[P - 1:P, :]).then_inc(loaded.sem, 16)
                sp.dma_start(top_first[:], top[P - 1:P, :]).then_inc(loaded.sem, 16)

            @block.vector
            def _(v):
                ch = Chain(v, dve)
                v.wait_ge(loaded.sem, loaded.base + 32)
                key_last = s.key[0:1, :]
                ch.step(nc.vector.memset(goes_on[:], 0.0))
                ch.step(nc.vector.memset(rows[:], FAR))
                ch.link(nc.vector.tensor_tensor(whole[:], key_first[:], key_last, ALU.is_equal))
                ch.step(nc.vector.tensor_tensor(goes_on[:, 0, :], key_first[:], s.before[:], ALU.is_equal))
                ch.link(nc.vector.tensor_tensor(goes_on[:, 1, 0:CH - 1], key_first[:, 1:CH], key_last[:, 0:CH - 1],
                                                ALU.is_equal))
                for d in range(2):
                    ch.step(nc.vector.tensor_tensor(pen[:, d, :], goes_on[:, d, :], whole[:], ALU.mult))
                ch.hold()
                ch.link(nc.vector.tensor_scalar(pen[:], pen[:], -FAR, FAR, ALU.mult, ALU.add))
                ch.step(nc.vector.tensor_tensor_scan(run[:, 0, :], pen[:, 0, :], top[0:1, :], FAR, ALU.add, ALU.max))
                ch.link(nc.vector.tensor_tensor_scan(run[:, 1, ::-1], pen[:, 1, ::-1], top_first[:, ::-1], FAR,
                                                     ALU.add, ALU.max))
                ch.step(nc.vector.tensor_copy(rows[:, 0, 1:CH], run[:, 0, 0:CH - 1]))
                ch.step(nc.vector.tensor_copy(rows[:, 1, :], s.before[:]))
                ch.step(nc.vector.tensor_copy(rows[:, 2, 0:CH - 1], run[:, 1, 1:CH]))
                ch.link(nc.vector.tensor_copy(rows[:, 3, 0:CH - 1], key_first[:, 1:CH]))
                ch.finish()
        with g.block() as block:
            @block.gpsimd
            def _(pool):
                nc.gpsimd.partition_broadcast(wide[:].rearrange("p a c -> p (a c)"),
                                              rows[:].rearrange("p a c -> p (a c)"), P).then_inc(spread.sem, 1)
                pool.wait_ge(spread.sem, spread.base + 1)
        with g.block() as block:
            @block.vector
            def _(v):
                ch = Chain(v, dve)
                for d in range(2):
                    ch.step(nc.vector.tensor_tensor(t1[:, d, :], s.key[:], wide[:, 2 * d + 1, :], ALU.not_equal))
                ch.hold()
                for d in range(2):
                    ch.step(nc.vector.scalar_tensor_tensor(t2[:, d, :], t1[:, d, :], FAR, wide[:, 2 * d, :],
                                                           ALU.mult, ALU.add))
                ch.hold()
                for d in range(2):
                    ch.link(nc.vector.tensor_tensor(top[:], top[:], t2[:, d, :], ALU.max))
                ch.link(nc.vector.tensor_tensor(score[:], score[:], top[:], ALU.subtract))
                ch.finish()
        with g.block() as block:
            @block.scalar
            def _(act):
                nc.scalar.activation(score[:], score[:], ACT.Exp).then_inc(powered.sem, 1)
                act.wait_ge(powered.sem, powered.base + 1)
        loaded.up(32)
        spread.up(1)
        powered.up(1)


def att_finish_pass(g):
    nc = g.nc
    g.x3 = g.dram("x3", [N, D])
    ctx, sb, ps = scope(g)
    with ctx:
        xin = sb("xin", [NP_, 2, NJ, D])
        agg = sb("agg", [NP_, 2, 2, NJ, AW])
        small = {n: sb(n, [NP_, 2, 2, NJ]) for n in ("none", "mx", "less", "fac", "part", "coef")}
        one = {n: sb(n, [NP_, 2, NJ]) for n in ("both", "den", "empty", "safe", "rden", "keep")}
        first = sb("first", [NP_, 2, NJ, D])
        mean = sb("mean", [NP_, 2, NJ, D])
        gel = sb("gel", [NP_, 2, NJ, D])
        y = sb("y", [NP_, 2, NJ, D])
        x3 = sb("x3_sb", [NP_, 2, NJ, D])
        ln = Norm(g, sb)
        loaded, stored = Halves(g, "node_loaded3", 48), Halves(g, "node_stored1", 16, by_pool=True)
        exped, lessened, meaned, gelued, summed, x3_there = all_halves(
            g, "join_exp", "join_less", "join_mean", "join_gelu", "join_sum", "join_x3")
        steps = all_halves(g, *[f"join_step{n}" for n in range(10)])
        with g.block() as block:
            @block.sync
            def _(sp):
                for it, half in tiles(sp):
                    summed.two_back(sp, half, it)
                    t = it * 2 + half
                    sp.dma_start(flat(xin[:, half]), tile_of(g.x2, D, t)).then_inc(loaded.c[half].sem, 16)
                    sp.dma_start(flat(agg[:, half, 0]), tile_of(g.agg_src, AW, t)).then_inc(loaded.c[half].sem, 16)
                    sp.dma_start(flat(agg[:, half, 1]), tile_of(g.agg_dst, AW, t)).then_inc(loaded.c[half].sem, 16)

            @block.scalar
            def _(act):
                def exps(it, half):
                    lessened.this(act, half, it)
                    exped.inc(nc.scalar.activation(small["fac"][:, half], small["less"][:, half], ACT.Exp), half)

                def gelus(it, half):
                    meaned.this(act, half, it)
                    summed.two_back(act, half, it)
                    gelued.inc(nc.scalar.activation(flat(gel[:, half]), flat(mean[:, half]), ACT.Gelu), half)

                run_tiles(act, (0, exps), (0, gelus))

            @block.vector
            def _(v):
                def factors(it, half):
                    n = iter(steps)

                    def link(ins):
                        h = next(n)
                        h.inc(ins, half)
                        h.this(v, half, it)

                    s = {k: t[:, half] for k, t in small.items()}
                    o = {k: t[:, half] for k, t in one.items()}
                    loaded.this(v, half, it)
                    d, m = agg[:, half, :, :, D], agg[:, half, :, :, D + 1]
                    link(nc.vector.tensor_scalar(s["none"], d, 0.0, FAR, ALU.is_equal, ALU.mult))
                    link(nc.vector.tensor_tensor(s["mx"], m, s["none"], ALU.add))
                    link(nc.vector.tensor_tensor(o["both"], s["mx"][:, 0], s["mx"][:, 1], ALU.max))
                    lessened.inc(nc.vector.tensor_tensor(
                        s["less"], s["mx"], o["both"].unsqueeze(1).to_broadcast([NP_, 2, NJ]), ALU.subtract), half)
                    exped.this(v, half, it)
                    link(nc.vector.tensor_tensor(s["part"], s["fac"], d, ALU.mult))
                    link(nc.vector.tensor_tensor(o["den"], s["part"][:, 0], s["part"][:, 1], ALU.add))
                    link(nc.vector.tensor_scalar(o["empty"], o["den"], 0.0, None, ALU.is_equal))
                    nc.vector.tensor_scalar(o["keep"], o["empty"], 1.0, None, ALU.add)
                    link(nc.vector.tensor_tensor(o["safe"], o["den"], o["empty"], ALU.add))
                    link(nc.vector.reciprocal(o["rden"], o["safe"]))
                    link(nc.vector.tensor_tensor(
                        s["coef"], s["fac"], o["rden"].unsqueeze(1).to_broadcast([NP_, 2, NJ]), ALU.mult))
                    for j in range(NJ):
                        last = nc.vector.tensor_scalar(first[:, half, j], agg[:, half, 0, j, 0:D],
                                                       s["coef"][:, 0, j:j + 1], None, ALU.mult)
                    link(last)
                    for j in range(NJ):
                        last = nc.vector.scalar_tensor_tensor(mean[:, half, j], agg[:, half, 1, j, 0:D],
                                                              s["coef"][:, 1, j:j + 1], first[:, half, j],
                                                              ALU.mult, ALU.add)
                    meaned.inc(last, half)

                def norms(it, half):
                    gelued.this(v, half, it)
                    for j in range(NJ):
                        last = nc.vector.scalar_tensor_tensor(y[:, half, j], xin[:, half, j],
                                                              one["keep"][:, half, j:j + 1], gel[:, half, j],
                                                              ALU.mult, ALU.add)
                    summed.inc(last, half)
                    summed.this(v, half, it)
                    ln.moments(v, y[:, half], half, it)
                    stored.two_back(v, half, it)
                    x3_there.inc(ln.scale(v, x3[:, half], y[:, half], half, it), half)

                run_tiles(v, (1, factors), (0, norms))

            @block.gpsimd
            def _(pool):
                for it, half in tiles(pool):
                    ln.power(pool, half, it)
                    x3_there.this(pool, half, it)
                    stored.inc(pool.dma_start(tile_of(g.x3, D, it * 2 + half), flat(x3[:, half])), half)
                for half in range(2):
                    stored.two_back(pool, half, TILES // 2)
        ln.up()
        for h in (loaded, stored, exped, lessened, meaned, gelued, summed, x3_there, *steps):
            h.up(TILES // 2)


def gru_pass(g, step, h_in, h_out, x3=None):
    nc = g.nc
    final = x3 is not None
    ctx, sb, ps = scope(g)
    with ctx:
        hin = sb("hin", [NP_, 2, NJ, D])
        agg = sb("agg", [NP_, 2, NJ, D])
        xin = sb("xin", [NP_, 2, NJ, D]) if final else None
        h_t = sb("h_t", [P, 2, NB])
        a_t = sb("a_t", [P, 2, NB])
        r = sb("r", [P, 2, NB])
        z = sb("z", [P, 2, NB])
        gated = sb("gated", [P, 2, NB])
        pre = sb("pre", [P, 2, NB])
        new = sb("new", [P, 2, NB])
        diff = sb("diff", [P, 2, NB])
        mixed = sb("mixed", [P, 2, NB])
        h_new = sb("h_new", [P, 2, NB])
        hout = sb("hout", [NP_, 2, NJ, D])
        y = sb("y", [NP_, 2, NJ, D]) if final else None
        turn_ps = ps("turn_ps", [P, 2, 512])
        gate_ps = ps("gate_ps", [P, 4, 512])
        back_ps = ps("back_ps", [NP_, 2, 512])
        ln = Norm(g, sb) if final else None
        loaded, x_loaded = Halves(g, "node_loaded", 32), Halves(g, "gru_x_loaded", 16)
        stored = Halves(g, "node_stored1", 16, by_pool=True)
        a_turned, h_turned, a_there, h_there, r_prod, z_prod, n_prod, i_prod = all_halves(
            g, "gru_a_turned", "gru_h_turned", "gru_a", "gru_h", "gru_r_product", "gru_z_product",
            "gru_n_product", "gru_i_product")
        r_there, z_there, gated_there, pre_there, new_there, diff_there, mixed_there, h_new_there, back, out_there = \
            all_halves(g, "gru_r", "gru_z", "gru_gated", "gru_pre", "gru_new", "gru_diff", "gru_mixed",
                       "gru_h_new", "gru_back", "gru_out")
        summed, = all_halves(g, "gru_summed")
        with g.block() as block:
            @block.sync
            def _(sp):
                def loads(it, half):
                    h_turned.two_back(sp, half, it)
                    t = it * 2 + half
                    sp.dma_start(flat(hin[:, half]), tile_of(h_in, D, t)).then_inc(loaded.c[half].sem, 16)
                    src = g.agg_dst.rearrange("(t p j) w -> t p j w", p=NP_, j=NJ)[bass.ds(t, 1)]
                    sp.dma_start(agg[:, half], src.rearrange("a p j w -> (a p) j w")[:, :, 0:D]) \
                        .then_inc(loaded.c[half].sem, 16)

                def skips(it, half):
                    summed.two_back(sp, half, it)
                    x_loaded.inc(sp.dma_start(flat(xin[:, half]), tile_of(x3, D, it * 2 + half)), half)

                run_tiles(sp, (1, loads), *([(0, skips)] if final else []))

            @block.tensor
            def _(pe):
                def turns(it, half):
                    loaded.this(pe, half, it)
                    a_there.one_back(pe, half, it)
                    a_turned.inc(turn(g, turn_ps[:, 0], agg[:, half]), half)
                    h_there.one_back(pe, half, it)
                    h_turned.inc(turn(g, turn_ps[:, 1], hin[:, half]), half)

                def products(it, half):
                    a_there.this(pe, half, it)
                    h_there.this(pe, half, it)
                    w_in, a, h = g.w_in[:, step], a_t[:, half], h_t[:, half]
                    for b, (free, done) in enumerate(((r_there, r_prod), (z_there, z_prod))):
                        free.one_back(pe, half, it)
                        nc.tensor.matmul(gate_ps[:, b, 0:NB], w_in[:, b * D:(b + 1) * D], a, start=True, stop=False)
                        done.inc(nc.tensor.matmul(gate_ps[:, b, 0:NB], g.w_hid[:, b * D:(b + 1) * D], h,
                                                  start=False, stop=True), half)
                    gated_there.one_back(pe, half, it)
                    n_prod.inc(nc.tensor.matmul(gate_ps[:, 2, 0:NB], g.w_hid[:, 2 * D:3 * D], h, start=True,
                                                stop=True), half)
                    pre_there.one_back(pe, half, it)
                    i_prod.inc(nc.tensor.matmul(gate_ps[:, 3, 0:NB], w_in[:, 2 * D:3 * D], a, start=True,
                                                stop=True), half)

                def backs(it, half):
                    h_new_there.this(pe, half, it)
                    out_there.one_back(pe, half, it)
                    for j in range(NJ):
                        last = nc.tensor.transpose(back_ps[:, j // 4, (j % 4) * D:(j % 4 + 1) * D],
                                                   h_new[:, half, j * NP_:(j + 1) * NP_], g.ident[:])
                    back.inc(last, half)

                run_tiles(pe, (1, turns), (0, products), (-1, backs))

            @block.scalar
            def _(act):
                def copies(it, half):
                    a_turned.this(act, half, it)
                    i_prod.two_back(act, half, it)
                    a_there.inc(nc.scalar.copy(a_t[:, half], turn_ps[:, 0, 0:NB]), half)
                    h_turned.this(act, half, it)
                    diff_there.two_back(act, half, it)
                    h_there.inc(nc.scalar.copy(h_t[:, half], turn_ps[:, 1, 0:NB]), half)

                def gates(it, half):
                    r_prod.this(act, half, it)
                    gated_there.two_back(act, half, it)
                    r_there.inc(nc.scalar.activation(r[:, half], gate_ps[:, 0, 0:NB], ACT.Sigmoid,
                                                     bias=g.b_sum[:, 0:1]), half)
                    z_prod.this(act, half, it)
                    mixed_there.two_back(act, half, it)
                    z_there.inc(nc.scalar.activation(z[:, half], gate_ps[:, 1, 0:NB], ACT.Sigmoid,
                                                     bias=g.b_sum[:, 1:2]), half)
                    pre_there.this(act, half, it)
                    h_new_there.two_back(act, half, it)
                    new_there.inc(nc.scalar.activation(new[:, half], pre[:, half], ACT.Tanh,
                                                       bias=g.b_in[:, 2:3]), half)

                run_tiles(act, (1, copies), (0, gates))

            @block.vector
            def _(v):
                def gates(it, half):
                    n_prod.this(v, half, it)
                    r_there.this(v, half, it)
                    gated_there.inc(nc.vector.scalar_tensor_tensor(
                        gated[:, half], gate_ps[:, 2, 0:NB], g.b_hid[:, 2:3], r[:, half], ALU.add, ALU.mult), half)
                    i_prod.this(v, half, it)
                    gated_there.this(v, half, it)
                    new_there.two_back(v, half, it)
                    pre_there.inc(nc.vector.tensor_tensor(pre[:, half], gated[:, half], gate_ps[:, 3, 0:NB],
                                                          ALU.add), half)

                def mixes(it, half):
                    new_there.this(v, half, it)
                    h_there.this(v, half, it)
                    diff_there.inc(nc.vector.tensor_tensor(diff[:, half], h_t[:, half], new[:, half],
                                                           ALU.subtract), half)
                    z_there.this(v, half, it)
                    diff_there.this(v, half, it)
                    mixed_there.inc(nc.vector.tensor_tensor(mixed[:, half], diff[:, half], z[:, half],
                                                            ALU.mult), half)
                    mixed_there.this(v, half, it)
                    back.two_back(v, half, it)
                    h_new_there.inc(nc.vector.tensor_tensor(h_new[:, half], mixed[:, half], new[:, half],
                                                            ALU.add), half)

                def outs(it, half):
                    back.this(v, half, it)
                    if not final:
                        stored.two_back(v, half, it)
                        nc.vector.tensor_copy(flat(hout[:, half, 0:4]), back_ps[:, 0, 0:4 * D])
                        out_there.inc(nc.vector.tensor_copy(hout[:, half, 4], back_ps[:, 1, 0:D]), half)
                        return
                    x_loaded.this(v, half, it)
                    nc.vector.tensor_tensor(flat(y[:, half, 0:4]), flat(xin[:, half, 0:4]), back_ps[:, 0, 0:4 * D],
                                            ALU.add)
                    out_there.inc(nc.vector.tensor_tensor(y[:, half, 4], xin[:, half, 4], back_ps[:, 1, 0:D],
                                                          ALU.add), half)
                    out_there.this(v, half, it)
                    ln.moments(v, y[:, half], half, it)
                    stored.two_back(v, half, it)
                    summed.inc(ln.scale(v, hout[:, half], y[:, half], half, it), half)

                run_tiles(v, (0, gates), (-1, outs), (0, mixes))

            @block.gpsimd
            def _(pool):
                for it, half in tiles(pool):
                    if final:
                        ln.power(pool, half, it)
                        summed.this(pool, half, it)
                    else:
                        out_there.this(pool, half, it)
                    stored.inc(pool.dma_start(tile_of(h_out, D, it * 2 + half), flat(hout[:, half])), half)
                for half in range(2):
                    stored.two_back(pool, half, TILES // 2)
        if final:
            ln.up()
            summed.up(TILES // 2)
            x_loaded.up(TILES // 2)
        for h in (loaded, stored, a_turned, h_turned, a_there, h_there, r_prod, z_prod, n_prod, i_prod, r_there,
                  z_there, gated_there, pre_there, new_there, diff_there, mixed_there, h_new_there, back, out_there):
            h.up(TILES // 2)


def program(g, a, out):
    constants_pass(g)
    weights_pass(g, a)
    gat_project_pass(g, a["x"])
    sort_pass(g, a["src"], a["dst"], a["edge_weight"])
    g.key_row = g.sb("key_row", [P, EP])
    g.rows = g.dram("rows", [GROUPS, P, U, D])
    dst, src = Side(g, "dst"), Side(g, "src")
    side_pass(g, dst)
    side_pass(g, src)
    key_row_pass(g, dst)

    ctx, sb, ps = scope(g)
    with ctx:
        e_sb = sb("gat_exp", [P, CH, HEADS])
        gat_score_pass(g, dst, e_sb)
        edge_pass(g, dst, rows=g.rows, heads=e_sb, out=g.agg_dst, out_width=AW)
    gat_finish_pass(g, a["x"])

    edge_pass(g, dst, table=g.hid_a, idx=dst.other_i, width=HID, weight=dst.weight, out=g.agg_hid, out_width=HID)
    gcn_hidden_pass(g)
    edge_pass(g, dst, table=g.hid_b, idx=dst.other_i, width=HID, weight=dst.weight, out=g.agg_hid, out_width=HID)
    gcn_finish_pass(g)

    ctx, sb, ps = scope(g)
    with ctx:
        score, top = sb("score", [P, CH]), sb("top", [P, CH])
        for s, table in ((src, g.agg_src), (dst, g.agg_dst)):
            key_row_pass(g, s)
            att_score_pass(g, s, a["edge_attr_128"], score, top)
            att_max_pass(g, s, score, top)
            edge_pass(g, s, rows=g.rows, weight=score, seg_max=top, out=table, out_width=AW)
    att_finish_pass(g)

    h = [g.x3, g.dram("h1", [N, D]), g.dram("h2", [N, D]), out]
    for i in range(3):
        edge_pass(g, dst, table=h[i], idx=dst.other_i, weight=dst.weight, out=g.agg_dst, out_width=AW)
        gru_pass(g, i, h[i], h[i + 1], g.x3 if i == 2 else None)


_INS = ['x', 'src', 'dst', 'edge_attr_128', 'edge_weight', 'L0_gnn_W_proj', 'L0_gnn_W_skip', 'L0_gnn_a_src',
        'L0_gnn_a_tgt', 'L1_gnn_w1', 'L1_gnn_b1', 'L1_gnn_w2', 'L1_gnn_b2', 'L2_gnn_W_att_w', 'L2_gnn_W_att_b',
        'L3_gnn_W', 'L3_gnn_w_ih', 'L3_gnn_w_hh', 'L3_gnn_b_ih', 'L3_gnn_b_hh']


def build(nc, args, out):
    with ExitStack() as ctx:
        program(Net(nc, ctx, args["x"]), args, out)


def kernel(**inputs):
    import numpy as _np
    import concourse.bacc as _bacc
    from concourse import mybir as _mybir
    from concourse.bass_utils import run_bass_kernel_spmd as _run

    nc = _bacc.Bacc("TRN2", target_bir_lowering=False, num_devices=1)
    arrays, args = {}, {}
    for name in _INS:
        a = _np.ascontiguousarray(inputs[name])
        arrays[f"in_{name}_dram"] = a
        args[name] = nc.dram_tensor(f"in_{name}_dram", a.shape, _mybir.dt.from_np(a.dtype), kind="ExternalInput").ap()
    out = nc.dram_tensor("out_0_dram", (N, D), F32, kind="ExternalOutput").ap()
    build(nc, args, out)
    r = _run(nc, [arrays], core_ids=[0])
    return r.results[0]["out_0_dram"]
```

```python
from contextlib import ExitStack, contextmanager

import concourse.bass as bass
from concourse import mybir

F32 = mybir.dt.float32
I32 = mybir.dt.int32
BF16 = mybir.dt.bfloat16
ALU = mybir.AluOpType
ACT = mybir.ActivationFunctionType
AX_X = mybir.AxisListType.X
RMAX = bass.bass_isa.ReduceOp.max

N = 50000
E = 25000
D = 128
HEADS = 8
HF = D // HEADS
HID = 64
P = 128
CH = -(-E // P)
EP = CH * P
SP_P, SP_B = 125, 200
LO = 256
HG = 98
PAD_KEY = 2 * HG * LO - 1
AW = 136
U = 7
GROUPS = CH // U
NJ = 4
NB = P * NJ
TILES = -(-N // NB)
TB = 4
UB = 10
LN_EPS = 1e-5
FAR = -1e30


class Count:

    def __init__(self, sem, kind):
        self.sem, self.base, self.kind = sem, 0, kind

    def up(self, n):
        self.base += n


class Chain:

    def __init__(self, eng, count, per=0):
        self.eng, self.count, self.per = eng, count, per
        self.n, self.iv, self.extra = 0, None, 0

    def start(self, iv):
        self.iv, self.n = iv, 0

    def value(self):
        v = self.count.base + self.extra + self.n
        return v if self.iv is None else self.iv * self.per + v

    def step(self, ins):
        self.n += 1
        ins.then_inc(self.count.sem, 1)
        return ins

    def hold(self):
        self.eng.wait_ge(self.count.sem, self.value())

    def link(self, ins):
        self.step(ins)
        self.hold()

    def loop_done(self, steps):
        assert self.n == self.per, (self.n, self.per)
        self.extra += steps * self.per
        self.n, self.iv = 0, None

    def finish(self):
        self.count.up(self.extra + self.n)


class Net:

    def __init__(self, nc, ctx, some_input):
        self.nc, self.ctx, self.counts, self.passes = nc, ctx, {}, 0
        self.spare = {"": [], "pool_dma": [], "dma": []}
        self.fresh = []
        self.some_input = some_input
        self.raise_buf = self.sb("raise_buf", [P, 64])
        self.passed = ctx.enter_context(nc.semaphore("passed"))

    def sem(self, name, kind=""):
        if name not in self.counts:
            spare = self.spare[kind]
            if not spare:
                spare.append(Count(self.ctx.enter_context(self.nc.semaphore(f"{name}_{self.passes}")), kind))
                self.fresh.append(spare[-1])
            self.counts[name] = spare.pop()
        return self.counts[name]

    @contextmanager
    def block(self):
        fresh, self.fresh, nc = self.fresh, [], self.nc
        if fresh:
            raised = [c for c in fresh if c.kind == ""]
            by_sp = [c for c in fresh if c.kind == "dma"]
            by_pool = [c for c in fresh if c.kind == "pool_dma"]

            def few_bytes(eng, counts, row):
                for n, c in enumerate(counts):
                    eng.dma_start(self.raise_buf[row:row + 1, n:n + 1],
                                  self.some_input[0:1, 0:1]).then_inc(c.sem, 16)
                for c in counts:
                    eng.wait_ge(c.sem, 16)
                    c.base += 16

            with nc.Block() as block:
                @block.sync
                def _(sp):
                    few_bytes(sp, by_sp, 0)

                @block.gpsimd
                def _(pool):
                    for c in raised:
                        pool.sem_inc(c.sem, 1)
                        c.base += 1
                    few_bytes(pool, by_pool, 32)
        with nc.Block() as block:
            yield block

    def end_of_pass(self):
        for count in self.counts.values():
            self.spare[count.kind].append(count)
        self.counts = {}

    def sb(self, name, shape, dt=F32):
        return self.ctx.enter_context(self.nc.sbuf_tensor(name, shape, dt))

    def dram(self, name, shape, dt=F32):
        return self.nc.dram_tensor(name, shape, dt, kind="Internal").ap()


def scope(g):
    nc, ctx = g.nc, ExitStack()
    g.end_of_pass()
    g.passes += 1
    of = f"pass{g.passes}_"

    def sb(name, shape, dt=F32):
        return ctx.enter_context(nc.sbuf_tensor(of + name, shape, dt))

    def ps(name, shape, dt=F32):
        return ctx.enter_context(nc.psum_tensor(of + name, shape, dt))

    return ctx, sb, ps


def gate(g, eng):
    eng.sem_inc(g.passed, 1)


def bcast(row, parts):
    return row.rearrange("(a n) -> a n", a=1).partition_broadcast(parts)


def constants_pass(g):
    nc = g.nc
    made = g.sem("consts_made")
    g.ident = g.sb("ident", [P, P])
    g.iota_lo = g.sb("iota_lo", [P, LO], BF16)
    g.iota_hi = g.sb("iota_hi", [P, 2 * HG], BF16)
    g.iota_p = g.sb("iota_p", [P, 2])
    g.earlier = g.sb("earlier", [P, P])
    g.zero = g.sb("zero", [P, 4 * AW])
    with g.block() as block:
        @block.gpsimd
        def _(pool):
            nc.gpsimd.memset(g.ident[:], 0.0).then_inc(made.sem, 1)
            nc.gpsimd.memset(g.earlier[:], 1.0).then_inc(made.sem, 1)
            nc.gpsimd.memset(g.zero[:], 0.0).then_inc(made.sem, 1)
            nc.gpsimd.iota(g.iota_lo[:], [[1, LO]], base=0, channel_multiplier=0,
                           allow_small_or_imprecise_dtypes=True).then_inc(made.sem, 1)
            nc.gpsimd.iota(g.iota_hi[:], [[1, 2 * HG]], base=0, channel_multiplier=0,
                           allow_small_or_imprecise_dtypes=True).then_inc(made.sem, 1)
            nc.gpsimd.iota(g.iota_p[:], [[HG, 2]], base=0, channel_multiplier=1,
                           allow_small_or_imprecise_dtypes=True).then_inc(made.sem, 1)
            pool.wait_ge(made.sem, made.base + 6)
            nc.gpsimd.affine_select(out=g.ident[:], in_=g.ident[:], compare_op=ALU.not_equal, fill=1.0,
                                    base=0, pattern=[[-1, P]], channel_multiplier=1).then_inc(made.sem, 1)
            nc.gpsimd.affine_select(out=g.earlier[:], in_=g.earlier[:], compare_op=ALU.is_gt, fill=0.0,
                                    base=0, pattern=[[-1, P]], channel_multiplier=1).then_inc(made.sem, 1)
            pool.wait_ge(made.sem, made.base + 8)
    made.up(8)


def sort_pass(g, src, dst, weight):
    nc = g.nc
    keys_in = {"dst": dst, "src": src}
    g.agg_dst = g.dram("agg_dst", [N, AW])
    g.agg_src = g.dram("agg_src", [N, AW])
    g.agg_hid = g.dram("agg_hid", [N, HID])
    g.agg_hid2 = g.dram("agg_hid2", [N, HID])
    tables = {"dst": (g.agg_dst, g.agg_hid), "src": (g.agg_src, g.agg_hid2)}
    g.rec = {k: g.dram(f"rec_{k}", [EP, 4]) for k in keys_in}
    ctx, sb, ps = scope(g)
    with ctx:
        rec = sb("rec", [SP_P, SP_B, 4])
        ints = sb("ints", [SP_P, 2, SP_B], I32)
        hi_lo = sb("hi_lo", [SP_P, 2, SP_B], I32)
        wcol = sb("wcol", [SP_P, SP_B])
        hi_f = sb("hi_f", [SP_P, SP_B])
        lo_f = sb("lo_f", [SP_P, SP_B])
        key_f = sb("key_f", [SP_P, SP_B])
        row = sb("row", [SP_P, E], I32)
        oh_lo = sb("oh_lo", [SP_P, 2, UB, LO], BF16)
        oh_hi = sb("oh_hi", [SP_P, 2, UB, 2 * HG], BF16)
        hi_t = sb("hi_t", [HG, UB, SP_P], I32)
        oh_t = sb("oh_t", [HG, 2, UB, 2, SP_P])
        junk_eq = sb("junk_eq", [SP_P, 2, UB, SP_P], BF16)
        junk_lo = sb("junk_lo", [SP_P, 2, UB, LO], BF16)
        rank = sb("rank", [SP_P, 2, 2, UB])
        pos = sb("pos", [SP_P, 2, UB])
        pos_i = sb("pos_i", [SP_P, 2, UB], I32)
        low_i = sb("low_i", [SP_P, 2, UB], I32)
        high_i = sb("high_i", [SP_P, 2, UB], I32)
        place = sb("place", [SP_P, 2, UB], I32)
        rec_stage = sb("rec_stage", [SP_P, 2, UB, 4])
        hist = sb("hist", [HG, 2, LO])
        scan = sb("scan", [HG, 2, LO])
        tot = sb("tot", [HG, 4])
        offs = sb("offs", [HG, 2])
        ones = sb("ones", [HG, HG])
        later = sb("later", [HG, HG])
        hist_sb = sb("hist_sb", [HG, 2, 2 * LO])
        pad = sb("pad", [88, 4])
        h_ps = ps("h_ps", [HG, 2 * LO])
        look_ps = ps("look_ps", [SP_P, 4, 512])
        off_ps = ps("off_ps", [HG, 512])
        steps = SP_B // UB // 2

        for key in ("dst", "src"):
            key_in = keys_in[key]
            ki = 1 if key == "dst" else 0
            out = g.rec[key]
            loaded, dve, prep = g.sem("sort_loaded", "dma"), g.sem("sort_dve"), g.sem("sort_prep")
            padded, numbered, summed = g.sem("sort_padded", "dma"), g.sem("sort_numbered"), g.sem("sort_summed")
            snap, counted_b = g.sem("sort_snapped"), g.sem("sort_counted_block")
            looked = [g.sem(f"sort_looked{h}") for h in range(2)]
            ranked = [g.sem(f"sort_ranked{h}") for h in range(2)]
            placed = [g.sem(f"sort_placed{h}") for h in range(2)]
            scattered = [g.sem(f"sort_scattered{h}", "pool_dma") for h in range(2)]
            onehots = [g.sem(f"sort_onehots{h}") for h in range(2)]
            counted = [g.sem(f"sort_counted{h}") for h in range(2)]
            zeroed = Ring(g, "tables_zeroed", 2, 32, "dma")
            with g.block() as block:
                @block.sync
                def _(sp):
                    v = lambda a: a.rearrange("(p b) -> p b", b=SP_B)
                    sp.dma_start(ints[:, 0, :], v(src)).then_inc(loaded.sem, 16)
                    sp.dma_start(ints[:, 1, :], v(dst)).then_inc(loaded.sem, 16)
                    sp.dma_start(wcol[:], v(weight)).then_inc(loaded.sem, 16)
                    sp.dma_start(row[:], bcast(key_in, SP_P)).then_inc(loaded.sem, 16)
                    sp.wait_ge(prep.sem, prep.base + 1)
                    sp.dma_start(out.rearrange("(q c) k -> q c k", c=CH)[0:88, CH - 1, :],
                                 pad[:]).then_inc(padded.sem, 16)
                    sp.wait_ge(padded.sem, padded.base + 16)

                @block.vector
                def _(v):
                    ch = Chain(v, dve)
                    ch.step(nc.vector.memset(ones[:], 1.0))
                    ch.step(nc.vector.memset(pad[:], 0.0))
                    ch.link(nc.vector.tensor_scalar(later[:], g.earlier[0:HG, 0:HG], -1.0, 1.0, ALU.mult, ALU.add))
                    ch.step(nc.vector.tensor_tensor(later[:], later[:], g.ident[0:HG, 0:HG], ALU.subtract))
                    nc.vector.memset(pad[:, ki:ki + 1], float(PAD_KEY)).then_inc(prep.sem, 1)
                    v.wait_ge(loaded.sem, loaded.base + 64)
                    ch.step(nc.vector.tensor_copy(rec[:, :, 0], ints[:, 0, :]))
                    ch.step(nc.vector.tensor_copy(rec[:, :, 1], ints[:, 1, :]))
                    ch.step(nc.vector.tensor_copy(rec[:, :, 2], wcol[:]))
                    ch.step(nc.vector.tensor_scalar(hi_lo[:, 0, :], ints[:, ki, :], 8, None, ALU.logical_shift_right))
                    ch.link(nc.vector.tensor_scalar(hi_lo[:, 1, :], ints[:, ki, :], LO - 1, None, ALU.bitwise_and))
                    ch.step(nc.vector.tensor_copy(hi_f[:], hi_lo[:, 0, :]))
                    ch.step(nc.vector.tensor_copy(key_f[:], ints[:, ki, :]))
                    ch.link(nc.vector.tensor_copy(lo_f[:], hi_lo[:, 1, :]))
                    ch.finish()

                @block.gpsimd
                def _(pool):
                    nc.gpsimd.iota(rec[:, :, 3], [[1, SP_B]], base=0, channel_multiplier=SP_B,
                                   allow_small_or_imprecise_dtypes=True).then_inc(numbered.sem, 1)
                    pool.wait_ge(numbered.sem, numbered.base + 1)
            loaded.up(64)
            padded.up(16)
            prep.up(1)
            numbered.up(1)

            def onehots_of(par, b, i):
                nc.vector.tensor_scalar(oh_lo[:, par, b, :], g.iota_lo[0:SP_P, :],
                                        lo_f[:, bass.ds(i, 1)], None, ALU.is_equal)
                return nc.vector.tensor_scalar(oh_hi[:, par, b, :], g.iota_hi[0:SP_P, :],
                                               hi_f[:, bass.ds(i, 1)], None, ALU.is_equal)

            def count(par, b):
                for h in range(2):
                    last = nc.tensor.matmul(h_ps[:, h * LO:(h + 1) * LO], oh_hi[:, par, b, h * HG:(h + 1) * HG],
                                            oh_lo[:, par, b, :], start=False, stop=True, skip_group_check=True)
                return last

            with g.block() as block:
                @block.vector
                def _(v):
                    with v.Fori(0, steps) as it:
                        for par in range(2):
                            v.wait_ge(counted[par].sem, it + counted[par].base)
                            for b in range(UB):
                                last = onehots_of(par, b, it * (2 * UB) + (par * UB + b))
                            last.then_inc(onehots[par].sem, 1)

                @block.tensor
                def _(pe):
                    nc.tensor.matmul(h_ps[:, :], g.zero[:, 0:HG], g.zero[:, 0:2 * LO], start=True, stop=True)
                    with pe.Fori(0, steps) as it:
                        for par in range(2):
                            pe.wait_ge(onehots[par].sem, it + (onehots[par].base + 1))
                            for b in range(UB):
                                last = count(par, b)
                            last.then_inc(counted[par].sem, 1)
            for h in range(2):
                onehots[h].up(steps)
                counted[h].up(steps)

            with g.block() as block:
                @block.vector
                def _(v):
                    ch = Chain(v, dve)
                    ch.step(nc.vector.memset(tot[:], 0.0))
                    ch.link(nc.vector.tensor_copy(hist[:].rearrange("p a b -> p (a b)"), h_ps[:]))
                    for h in range(2):
                        ch.step(nc.vector.tensor_tensor_scan(scan[:, h, :], hist[:, h, :], g.zero[0:HG, 0:LO],
                                                             0.0, ALU.add, ALU.add))
                    ch.hold()
                    ch.step(nc.vector.tensor_copy(tot[:, 0:2], scan[:, :, LO - 1]))
                    ch.step(nc.vector.tensor_copy(tot[:, 3:4], scan[:, 0, LO - 1:LO]))
                    ch.link(nc.vector.tensor_tensor(hist[:], scan[:], hist[:], ALU.subtract))
                    ch.finish()
            with g.block() as block:
                @block.tensor
                def _(pe):
                    nc.tensor.matmul(off_ps[:, 0:2], later[:], tot[:, 0:2], start=True, stop=False)
                    nc.tensor.matmul(off_ps[:, 0:2], ones[:], tot[:, 2:4], start=False,
                                     stop=True).then_inc(summed.sem, 1)
                    pe.wait_ge(summed.sem, summed.base + 3)
                    nc.tensor.matmul(h_ps[:, :], g.ident[0:HG, 0:HG],
                                     hist[:].rearrange("p a b -> p (a b)"), start=True,
                                     stop=True).then_inc(summed.sem, 1)
                    pe.wait_ge(summed.sem, summed.base + 4)

                @block.vector
                def _(v):
                    v.wait_ge(summed.sem, summed.base + 1)
                    for h in range(2):
                        nc.vector.tensor_scalar(hist[:, h, :], hist[:, h, :], off_ps[:, h:h + 1], None,
                                                ALU.add).then_inc(summed.sem, 1)
            summed.up(4)

            with g.block() as block:
                @block.sync
                def _(sp):
                    def zeros(tile):
                        zeroed.slot_free(sp, tile)
                        wide, narrow = tables[key]
                        store(sp, zeroed, tile, (wide, g.zero[:]), (narrow, g.zero[:, 0:NJ * HID]))

                    run_tiles(sp, (0, zeros))
                    zeroed.all(sp)

                @block.scalar
                def _(act):
                    with act.Fori(0, SP_B // 2) as it:
                        for p2 in range(2):
                            act.wait_ge(counted_b.sem, it * 2 + (counted_b.base + p2))
                            act.wait_ge(looked[p2].sem, it + looked[p2].base)
                            nc.scalar.copy(hist_sb[:, p2, :], h_ps[:]).then_inc(snap.sem, 1)

                @block.tensor
                def _(pe):
                    with pe.Fori(0, SP_B // (2 * UB)) as it:
                        for par in range(2):
                            pe.wait_ge(onehots[par].sem, it + (onehots[par].base + 1))
                            for b in range(UB):
                                k = par * UB + b
                                p2 = b % 2
                                pe.wait_ge(snap.sem, it * (2 * UB) + (snap.base + k + 1))
                                count(par, b).then_inc(counted_b.sem, 1)
                                pe.wait_ge(ranked[p2].sem, it * UB + (ranked[p2].base + k // 2))
                                for h in range(2):
                                    last = nc.tensor.matmul(look_ps[:, p2, 0:LO], oh_t[:, par, b, h, :],
                                                            hist_sb[:, p2, h * LO:(h + 1) * LO],
                                                            start=(h == 0), stop=(h == 1))
                                last.then_inc(looked[p2].sem, 1)

                @block.vector
                def _(v):
                    ch = Chain(v, dve, per=2 * 6)
                    with v.Fori(0, SP_B // (2 * UB)) as it:
                        ch.start(it)
                        for par in range(2):
                            rv = row[:].rearrange("p (a b) -> p b a", b=SP_B)
                            blocks = bass.ds(it * (2 * UB) + par * UB, UB)
                            for p2 in range(2):
                                v.wait_ge(looked[p2].sem, it * UB + (looked[p2].base + (par * UB) // 2))
                            ch.link(nc.vector.tensor_scalar(hi_t[:], rv[0:HG, blocks, :], 8, None,
                                                            ALU.logical_shift_right))
                            for h in range(2):
                                nc.vector.tensor_scalar(oh_t[:, par, :, h, :], hi_t[:], g.iota_p[0:HG, h:h + 1],
                                                        None, ALU.is_equal)
                            for b in range(UB):
                                i = it * (2 * UB) + (par * UB + b)
                                last = onehots_of(par, b, i)
                            last.then_inc(onehots[par].sem, 1)
                            for b in range(UB):
                                i = it * (2 * UB) + (par * UB + b)
                                nc.vector.scalar_tensor_tensor(
                                    junk_eq[:, par, b, :], rv[:, bass.ds(i, 1), :].rearrange("p a b -> p (a b)"),
                                    key_f[:, bass.ds(i, 1)],
                                    g.earlier[0:SP_P, 0:SP_P], ALU.is_equal, ALU.mult,
                                    accum_out=rank[:, par, 0, b:b + 1])
                            for b in range(UB):
                                i = it * (2 * UB) + (par * UB + b)
                                p2 = b % 2
                                v.wait_ge(looked[p2].sem, it * UB + (looked[p2].base + (par * UB + b) // 2 + 1))
                                nc.vector.scalar_tensor_tensor(
                                    junk_lo[:, par, b, :], g.iota_lo[0:SP_P, :], lo_f[:, bass.ds(i, 1)],
                                    look_ps[:, p2, 0:LO], ALU.is_equal, ALU.mult,
                                    accum_out=rank[:, par, 1, b:b + 1]).then_inc(ranked[p2].sem, 1)
                            for p2 in range(2):
                                v.wait_ge(ranked[p2].sem, it * UB + (ranked[p2].base + (par + 1) * UB // 2))
                            v.wait_ge(scattered[par].sem, it * (16 * UB) + scattered[par].base)
                            ch.step(nc.vector.tensor_copy(rec_stage[:, par, :, :], rec[:, blocks, :]))
                            ch.link(nc.vector.tensor_tensor(pos_i[:, par, :], rank[:, par, 0, :],
                                                            rank[:, par, 1, :], ALU.add))
                            ch.step(nc.vector.tensor_scalar(low_i[:, par, :], pos_i[:, par, :], P - 1, None,
                                                            ALU.bitwise_and))
                            ch.link(nc.vector.tensor_scalar(high_i[:, par, :], pos_i[:, par, :], 7, None,
                                                            ALU.logical_shift_right))
                            ch.link(nc.vector.tensor_scalar(pos[:, par, :], low_i[:, par, :], -float(CH),
                                                            float((P - 1) * CH), ALU.mult, ALU.add))
                            nc.vector.tensor_tensor(place[:, par, :], pos[:, par, :],
                                                    high_i[:, par, :], ALU.add).then_inc(placed[par].sem, 1)
                    ch.loop_done(SP_B // (2 * UB))
                    ch.finish()

                @block.gpsimd
                def _(pool):
                    bound = pool.to_reg(EP - 1)
                    with pool.Fori(0, SP_B // (2 * UB)) as it:
                        for par in range(2):
                            pool.wait_ge(placed[par].sem, it + (placed[par].base + 1))
                            gate(g, pool)
                            for b in range(UB):
                                pool.indirect_dma_start(
                                    out=out, out_offset=bass.IndirectOffsetOnAxis(ap=place[:, par, b:b + 1], axis=0),
                                    in_=rec_stage[:, par, b, :], in_offset=None, bounds_check=bound,
                                    oob_is_err=False).then_inc(scattered[par].sem, 16)
                    for par in range(2):
                        pool.wait_ge(scattered[par].sem, scattered[par].base + 16 * SP_B // 2)
            zeroed.up()
            snap.up(SP_B)
            counted_b.up(SP_B)
            for h in range(2):
                onehots[h].up(steps)
                looked[h].up(SP_B // 2)
                ranked[h].up(SP_B // 2)
                placed[h].up(steps)
                scattered[h].up(16 * SP_B // 2)


class Halves:

    def __init__(self, g, name, k=1, by_pool=False):
        kind = "" if k % 16 else ("pool_dma" if by_pool else "dma")
        self.c = [g.sem(f"{name}{h}", kind) for h in range(2)]
        self.g, self.k = g, k

    def wait(self, eng, half, value):
        eng.wait_ge(self.c[half].sem, value)
        if eng in (self.g.nc.gpsimd, self.g.nc.sync):
            gate(self.g, eng)

    def inc(self, ins, half):
        return ins.then_inc(self.c[half].sem, self.k)

    def this(self, eng, half, it):
        self.wait(eng, half, it * self.k + (self.c[half].base + self.k))

    def part(self, eng, half, it, n):
        self.wait(eng, half, it * self.k + (self.c[half].base + n))

    def two_back(self, eng, half, it):
        self.wait(eng, half, it * self.k + self.c[half].base)

    def one_back(self, eng, half, it):
        self.wait(eng, 1 - half, it * self.k + (self.c[1 - half].base + self.k * half))

    def up(self, tiles):
        for c in self.c:
            c.up(self.k * tiles)


def all_halves(g, *names, k=1):
    return [Halves(g, n, k) for n in names]


class Side:

    def __init__(self, g, name):
        self.name = name
        self.rec = g.rec[name]
        self.key = g.sb(f"{name}_key", [P, CH])
        self.weight = g.sb(f"{name}_weight", [P, CH])
        self.before = g.sb(f"{name}_before", [1, CH])
        self.other_i = g.sb(f"{name}_other_i", [P, CH], I32)
        self.edge_i = g.sb(f"{name}_edge_i", [P, CH], I32)
        self.key_i = g.sb(f"{name}_key_i", [P, CH], I32)
        self.last_i = g.sb(f"{name}_last_i", [P, CH], I32)
        self.key_d = g.dram(f"{name}_key_d", [P, CH])
        self.rows = g.dram(f"{name}_rows", [P, CH, D])


def side_pass(g, s):
    nc = g.nc
    kc = 1 if s.name == "dst" else 0
    ctx, sb, ps = scope(g)
    with ctx:
        rec = sb("side_rec", [P, CH, 4])
        after = sb("side_after", [P, CH])
        tmp = sb("side_tmp", [P, CH])
        tmp2 = sb("side_tmp2", [P, CH])
        loaded, dve, keyed, wrote = g.sem("side_loaded", "dma"), g.sem("side_dve"), g.sem("side_keyed"), g.sem("side_wrote", "dma")
        shifted = g.sem("side_shifted", "dma")
        with g.block() as block:
            @block.sync
            def _(sp):
                sp.dma_start(rec[:], s.rec.rearrange("(q c) k -> q c k", c=CH)).then_inc(loaded.sem, 16)
                sp.wait_ge(keyed.sem, keyed.base + 1)
                sp.dma_start(s.key_d, s.key[:]).then_inc(wrote.sem, 16)
                sp.wait_ge(wrote.sem, wrote.base + 16)
                sp.dma_start(after[1:P, :], s.key_d[0:P - 1, :]).then_inc(shifted.sem, 16)
                sp.dma_start(after[0:1, 0:CH - 1], s.key_d[P - 1:P, 1:CH]).then_inc(shifted.sem, 16)
                sp.dma_start(s.before[0:1, 1:CH], s.key_d[0:1, 0:CH - 1]).then_inc(shifted.sem, 16)
                sp.wait_ge(shifted.sem, shifted.base + 48)

            @block.vector
            def _(v):
                ch = Chain(v, dve)
                ch.step(nc.vector.memset(after[0:1, CH - 1:CH], -1.0))
                ch.step(nc.vector.memset(s.before[0:1, 0:1], -1.0))
                v.wait_ge(loaded.sem, loaded.base + 16)
                nc.vector.tensor_copy(s.key[:], rec[:, :, kc]).then_inc(keyed.sem, 1)
                ch.step(nc.vector.tensor_copy(s.weight[:], rec[:, :, 2]))
                ch.step(nc.vector.tensor_copy(s.other_i[:], rec[:, :, 0]))
                ch.step(nc.vector.tensor_copy(s.edge_i[:], rec[:, :, 3]))
                v.wait_ge(keyed.sem, keyed.base + 1)
                ch.step(nc.vector.tensor_scalar(s.key_i[:], s.key[:], float(N - 1), None, ALU.min))
                v.wait_ge(shifted.sem, shifted.base + 48)
                ch.link(nc.vector.tensor_tensor(tmp[:], s.key[:], after[:], ALU.is_equal))
                ch.link(nc.vector.tensor_scalar(tmp2[:], tmp[:], float(4 * N), None, ALU.mult))
                ch.link(nc.vector.tensor_tensor(s.last_i[:], tmp2[:], s.key[:], ALU.add))
                ch.finish()
        loaded.up(16)
        keyed.up(1)
        wrote.up(16)
        shifted.up(48)


def load_key_row(g, eng, s, loaded):
    eng.dma_start(g.key_row[:], bcast(s.key_d.rearrange("q c -> (q c)"), P)).then_inc(loaded.sem, 16)


def key_row_pass(g, s):
    loaded = g.sem("key_row_loaded", "dma")
    with g.block() as block:
        @block.sync
        def _(sp):
            load_key_row(g, sp, s, loaded)
            sp.wait_ge(loaded.sem, loaded.base + 16)
    loaded.up(16)


def chunk_keys(g, c, parts=slice(0, P)):
    return g.key_row[parts, :].rearrange("p (q c) -> p c q", c=CH)[:, bass.ds(c, 1), :].rearrange("p a q -> p (a q)")


def group_keys(g, c, parts=slice(0, P)):
    return g.key_row[parts, :].rearrange("p (q c) -> p c q", c=CH)[:, bass.ds(c, U), :]


class Stage:

    def __init__(self, g, sb, name):
        self.buf = sb(f"stage_{name}", [P, 2, U], I32)
        self.there = Halves(g, f"staged_{name}", 16)

    def load(self, sp, idx, half, it):
        self.there.inc(sp.dma_start(self.buf[:, half, :], idx[:, bass.ds(it * (2 * U) + half * U, U)]), half)


def gather(pool, stage, table, out, half):
    for u in range(U):
        last = pool.indirect_dma_start(out=out(u), out_offset=None, in_=table,
                                       in_offset=bass.IndirectOffsetOnAxis(ap=stage.buf[:, half, u:u + 1], axis=0))
        yield last


STEPS = GROUPS // 2


def edge_pass(g, s, table=None, idx=None, rows=None, width=D, weight=None, heads=None, seg_max=None,
              squash=None, out=None, out_width=None):
    nc = g.nc
    wide = D + HEADS if heads is not None else (D + 1 if seg_max is not None else width)
    ctx, sb, ps = scope(g)
    with ctx:
        rowbuf = sb("rowbuf", [P, 2, U, AW])
        same = sb("same", [P, 2, U, P])
        carry = sb("carry", [1, 2, U, P])
        sums = sb("sums", [P, 2, U, out_width])
        made = heads is not None or squash is not None
        scaled = sb("scaled", [P, 2, U, AW]) if made else rowbuf
        pre = sb("pre", [P, 2, U, width]) if squash is not None else None
        sum_ps = ps("sum_ps", [P, U, 512])
        st_in = Stage(g, sb, "gather")
        st_out = Stage(g, sb, "scatter")
        got = Halves(g, "edge_rows", 16 * U if rows is None else 16, by_pool=rows is None)
        put = Halves(g, "edge_put", 16 * U, by_pool=True)
        matrices, = all_halves(g, "edge_matrices")
        biased, squashed = all_halves(g, "edge_biased", "edge_squashed") if squash is not None else (None, None)
        used, copied = all_halves(g, "edge_used", "edge_copied", k=U)
        cleared, dve = g.sem("edge_cleared"), g.sem("edge_dve")

        with g.block() as block:
            @block.vector
            def _(v):
                nc.vector.memset(sums[:], 0.0).then_inc(cleared.sem, 1)
                nc.vector.memset(rowbuf[:], 1.0).then_inc(cleared.sem, 1)
                v.wait_ge(cleared.sem, cleared.base + 2)
        cleared.up(2)

        with g.block() as block:
            @block.sync
            def _(sp):
                with sp.Fori(0, STEPS) as it:
                    for half in range(2):
                        if rows is None:
                            got.two_back(sp, half, it)
                            st_in.load(sp, idx, half, it)
                        else:
                            used.two_back(sp, half, it)
                            got.inc(sp.dma_start(rowbuf[:, half, :, 0:D],
                                                 rows[:, bass.ds(it * (2 * U) + half * U, U), :]),
                                    half)
                        put.two_back(sp, half, it)
                        st_out.load(sp, s.last_i, half, it)

            @block.gpsimd
            def _(pool):
                bound = pool.to_reg(N - 1)

                def gathers(half, it):
                    st_in.there.this(pool, half, it)
                    used.two_back(pool, half, it)
                    for ins in gather(pool, st_in, table, lambda u: rowbuf[:, half, u, 0:width], half):
                        ins.then_inc(got.c[half].sem, 16)

                def scatters(half, it):
                    st_out.there.this(pool, half, it)
                    copied.this(pool, half, it)
                    if seg_max is not None:
                        matrices.this(pool, half, it)
                    for u in range(U):
                        pool.indirect_dma_start(
                            out=out, out_offset=bass.IndirectOffsetOnAxis(ap=st_out.buf[:, half, u:u + 1], axis=0),
                            in_=sums[:, half, u, :], in_offset=None, bounds_check=bound,
                            oob_is_err=False).then_inc(put.c[half].sem, 16)

                if rows is None:
                    gathers(0, 0)
                with pool.Fori(0, STEPS - 1) as it:
                    for half in range(2):
                        if rows is None:
                            gathers(1 - half, it + half)
                        scatters(half, it)
                if rows is None:
                    gathers(1, STEPS - 1)
                scatters(0, STEPS - 1)
                scatters(1, STEPS - 1)
                for half in range(2):
                    put.two_back(pool, half, STEPS)

            @block.vector
            def _(v):
                with v.Fori(0, STEPS) as it:
                    for half in range(2):
                        first = it * (2 * U) + half * U
                        used.two_back(v, half, it)
                        for u in range(U):
                            args = (None, ALU.is_equal) if weight is None else \
                                (weight[:, bass.ds(first + u, 1)], ALU.is_equal, ALU.mult)
                            nc.vector.tensor_scalar(same[:, half, u, :], chunk_keys(g, first + u),
                                                    s.key[:, bass.ds(first + u, 1)], *args)
                        if seg_max is not None:
                            put.two_back(v, half, it)
                            nc.vector.tensor_copy(sums[:, half, :, D + 1], seg_max[:, bass.ds(first, U)])
                        if squash is not None:
                            got.this(v, half, it)
                            squashed.two_back(v, half, it)
                            biased.inc(nc.vector.tensor_tensor(
                                pre[:, half], rowbuf[:, half, :, 0:width],
                                squash.unsqueeze(1).to_broadcast([P, U, width]), ALU.add), half)
                        if heads is not None:
                            got.this(v, half, it)
                            exps = heads[:, bass.ds(first, U), :]
                            for u in range(U):
                                nc.vector.tensor_tensor(
                                    scaled[:, half, u, 0:D].rearrange("p (h f) -> p h f", f=HF),
                                    rowbuf[:, half, u, 0:D].rearrange("p (h f) -> p h f", f=HF),
                                    heads[:, bass.ds(first + u, 1), :].rearrange("p a h -> p (a h)")
                                    .unsqueeze(2).to_broadcast([P, HEADS, HF]), ALU.mult)
                            nc.vector.tensor_copy(scaled[:, half, :, D:D + HEADS], exps)
                        matrices.inc(nc.vector.tensor_tensor(
                            carry[0:1, half, :, :], group_keys(g, first, slice(0, 1)),
                            s.before[0:1, bass.ds(first, U)].unsqueeze(2).to_broadcast([1, U, P]),
                            ALU.is_equal), half)

            @block.tensor
            def _(pe):
                with pe.Fori(0, STEPS) as it:
                    for half in range(2):
                        matrices.this(pe, half, it)
                        if squash is not None:
                            squashed.this(pe, half, it)
                        elif heads is None:
                            got.this(pe, half, it)

                        def product(u):
                            nc.tensor.matmul(sum_ps[:, u, 0:wide], same[:, half, u, :],
                                             scaled[:, half, u, 0:wide], start=True, stop=False)

                        product(0)
                        for u in range(U):
                            if u + 1 < U:
                                product(u + 1)
                            if u:
                                copied.part(pe, half, it, u)
                            else:
                                copied.one_back(pe, half, it)
                            prev = sums[0:1, half, u - 1, 0:wide] if u else sums[0:1, 1 - half, U - 1, 0:wide]
                            ins = nc.tensor.matmul(sum_ps[:, u, 0:wide], carry[0:1, half, u, :], prev,
                                                   start=False, stop=True)
                            ins.then_inc(used.c[half].sem, 1)

            @block.scalar
            def _(act):
                with act.Fori(0, STEPS) as it:
                    for half in range(2):
                        if squash is not None:
                            biased.this(act, half, it)
                            used.two_back(act, half, it)
                            squashed.inc(nc.scalar.activation(scaled[:, half, :, 0:width], pre[:, half],
                                                              ACT.Sigmoid), half)
                        put.two_back(act, half, it)
                        for u in range(U):
                            used.part(act, half, it, u + 1)
                            ins = nc.scalar.copy(sums[:, half, u, 0:wide], sum_ps[:, u, 0:wide])
                            ins.then_inc(copied.c[half].sem, 1)
        if rows is None:
            st_in.there.up(STEPS)
        st_out.there.up(STEPS)
        for h in (got, put, matrices, used, copied, *((biased, squashed) if squash is not None else ())):
            h.up(STEPS)


def weights_pass(g, a):
    nc = g.nc
    g.w_proj = g.sb("w_proj", [P, D + 2 * HEADS])
    g.w_skip = g.sb("w_skip", [P, D])
    g.w1 = g.sb("w1", [P, HID])
    g.w2 = g.sb("w2", [HID + 1, D])
    g.b1 = g.sb("b1", [P, HID])
    g.att = g.sb("att", [P, 2 * D])
    g.att_b = g.sb("att_b", [P, 1])
    g.w_in = g.sb("w_in", [P, 3, 3 * D])
    g.w_hid = g.sb("w_hid", [P, 3 * D])
    g.b_in = g.sb("b_in", [P, 3])
    g.b_hid = g.sb("b_hid", [P, 3])
    g.b_sum = g.sb("b_sum", [P, 3])
    g.minus_half = g.sb("minus_half", [P, NJ])
    ctx, sb, ps = scope(g)
    with ctx:
        a_src, a_tgt = sb("a_src", [P, D]), sb("a_tgt", [P, D])
        prod = sb("prod", [P, 2, D])
        rows_in = sb("rows_in", [P, 3, D])
        rows_hid = sb("rows_hid", [P, 3, D])
        w_step = sb("w_step", [P, 3, D])
        in_t = sb("in_t", [P, 3 * D])
        step_t = sb("step_t", [P, 3 * D])
        t_ps = ps("t_ps", [P, 3, 512])
        c_ps = ps("c_ps", [P, 3, 512])
        loaded, dve, turned, copied = g.sem("w_loaded", "dma"), g.sem("w_dve"), g.sem("w_turned"), g.sem("w_copied")
        with g.block() as block:
            @block.sync
            def _(sp):
                one = lambda v: bcast(v, P)
                n = 0
                loads = [
                    (g.w_proj[:, 0:D], a["L0_gnn_W_proj"]), (g.w_skip[:], a["L0_gnn_W_skip"]),
                    (a_src[:], one(a["L0_gnn_a_src"].rearrange("a h f -> (a h f)"))),
                    (a_tgt[:], one(a["L0_gnn_a_tgt"].rearrange("a h f -> (a h f)"))),
                    (g.w1[:], a["L1_gnn_w1"]), (g.w2[0:HID, :], a["L1_gnn_w2"]),
                    (g.w2[HID:HID + 1, :], a["L1_gnn_b2"].rearrange("(a n) -> a n", a=1)),
                    (g.b1[:], one(a["L1_gnn_b1"])), (g.att[:], one(a["L2_gnn_W_att_w"])),
                    (g.att_b[:], one(a["L2_gnn_W_att_b"])),
                    (rows_in[:], a["L3_gnn_w_ih"].rearrange("(t p) n -> p t n", p=P)),
                    (rows_hid[:], a["L3_gnn_w_hh"].rearrange("(t p) n -> p t n", p=P)),
                    (w_step[:], a["L3_gnn_W"].rearrange("t p n -> p t n")),
                ]
                for to, of in loads:
                    sp.dma_start(to, of).then_inc(loaded.sem, 16)
                with nc.allow_non_contiguous_dma(reason="384 biases, once"):
                    for to, name in ((g.b_in, "L3_gnn_b_ih"), (g.b_hid, "L3_gnn_b_hh")):
                        sp.dma_start(to[:], a[name].rearrange("(t p) -> p t", p=P)).then_inc(loaded.sem, 16)
                sp.wait_ge(loaded.sem, loaded.base + 16 * (len(loads) + 2))
                loaded.up(16 * (len(loads) + 2))
        with g.block() as block:
            @block.vector
            def _(v):
                ch = Chain(v, dve)
                ch.step(nc.vector.memset(g.minus_half[:], -0.5))
                ch.step(nc.vector.tensor_tensor(g.b_sum[:], g.b_in[:], g.b_hid[:], ALU.add))
                ch.step(nc.vector.tensor_tensor(prod[:, 0, :], g.w_proj[:, 0:D], a_src[:], ALU.mult))
                ch.link(nc.vector.tensor_tensor(prod[:, 1, :], g.w_proj[:, 0:D], a_tgt[:], ALU.mult))
                ch.link(nc.vector.reduce_sum(g.w_proj[:, D:D + 2 * HEADS],
                                             prod[:].rearrange("p t (h f) -> p (t h) f", f=HF), AX_X))
                for n, to in enumerate((in_t, g.w_hid, step_t)):
                    v.wait_ge(turned.sem, turned.base + n + 1)
                    nc.vector.tensor_copy(to[:], t_ps[:, n, 0:3 * D]).then_inc(copied.sem, 1)
                for i in range(3):
                    v.wait_ge(turned.sem, turned.base + 4 + i)
                    ch.step(nc.vector.tensor_copy(g.w_in[:, i, :], c_ps[:, i, 0:3 * D]))
                ch.hold()
                ch.finish()

            @block.tensor
            def _(pe):
                for n, of in enumerate((rows_in, rows_hid, w_step)):
                    for t in range(3):
                        last = nc.tensor.transpose(t_ps[:, n, t * D:(t + 1) * D], of[:, t, :], g.ident[:])
                    last.then_inc(turned.sem, 1)
                pe.wait_ge(copied.sem, copied.base + 3)
                for i in range(3):
                    nc.tensor.matmul(c_ps[:, i, 0:3 * D], step_t[:, i * D:(i + 1) * D], in_t[:],
                                     start=True, stop=True).then_inc(turned.sem, 1)
        turned.up(6)
        copied.up(3)


class Tile:

    def __init__(self, it, n):
        self.it, self.n = it + n // TB, n % TB
        self.t = self.it * TB + self.n
        self.known = isinstance(self.t, int)

    def back(self, m=1):
        return Tile(self.it, self.n - m)

    def slot(self, slots=2):
        return self.n % slots

    def lap(self, slots):
        return self.it * (TB // slots) + self.n // slots

    @property
    def first_node(self):
        return min(self.t * NB, N - NB) if self.known else self.t * NB

    @property
    def is_last(self):
        return self.known and self.t == TILES - 1


class Ring:

    def __init__(self, g, name, slots=2, k=1, kind=""):
        self.c = [g.sem(f"{name}{n}", kind) for n in range(slots)]
        self.g, self.k, self.slots = g, k, slots

    def wait(self, eng, tile, laps):
        c = self.c[tile.slot(self.slots)]
        eng.wait_ge(c.sem, (tile.lap(self.slots) + laps) * self.k + c.base)
        if eng in (self.g.nc.gpsimd, self.g.nc.sync):
            gate(self.g, eng)

    def inc(self, ins, tile, by=1):
        return ins.then_inc(self.c[tile.slot(self.slots)].sem, by)

    def this(self, eng, tile):
        self.wait(eng, tile, 1)

    def slot_free(self, eng, tile):
        self.wait(eng, tile, 0)

    def one_back(self, eng, tile):
        if not (tile.known and tile.t == 0):
            self.wait(eng, tile.back(), 1)

    def four_back(self, eng, tile):
        if not (tile.known and tile.t < 4):
            self.wait(eng, tile.back(4), 1)

    def all(self, eng):
        for n in range(self.slots):
            self.wait(eng, Tile(0, n), -(-(TILES - n) // self.slots))

    def up(self):
        for n, c in enumerate(self.c):
            c.up(self.k * -(-(TILES - n) // self.slots))


def rings(g, *names):
    return [Ring(g, n) for n in names]


def run_tiles(eng, *steps):
    offsets = [offset for offset, _ in steps]

    def whole(time):
        for offset, step in steps:
            if 0 <= time + offset < TILES:
                step(Tile(0, time + offset))

    start = max(0, -min(offsets))
    laps = (TILES - 2 - max(offsets) - start + 1) // TB
    for time in range(-max(offsets), start):
        whole(time)
    with eng.Fori(0, laps) as it:
        for n in range(TB):
            for offset, step in steps:
                step(Tile(it, start + offset + n))
    for time in range(start + laps * TB, TILES - min(offsets)):
        whole(time)


def tile_of(table, tile):
    return table[bass.ds(tile.first_node, NB), :].rearrange("(p j) w -> p (j w)", j=NJ)


def flat(ap):
    return ap.rearrange("p j w -> p (j w)")


def turn(g, out_ps, tile, width=D):
    for j in range(NJ):
        last = g.nc.tensor.transpose(out_ps[0:width, j * P:(j + 1) * P], tile[:, j, :], g.ident[:])
    return last


class Norm:

    def __init__(self, g, sb):
        self.g = g
        self.stats = sb("ln_stats", [P, 2, NJ, 6])
        self.mv = sb("ln_mv", [P, 2, NJ, 2])
        self.ve = sb("ln_ve", [P, 2, NJ])
        self.minus = sb("ln_minus", [P, 2, NJ])
        self.rstd = sb("ln_rstd", [P, 2, NJ])
        self.shift = sb("ln_shift", [P, 2, NJ])
        self.stats_there, self.mv_there, self.var_there, self.rstd_there, self.shift_there, self.done = rings(
            g, "ln_stats", "ln_mv", "ln_var", "ln_rstd", "ln_shift", "ln_done")

    def moments(self, v, y, tile):
        nc, h = self.g.nc, tile.slot()
        for j in range(NJ):
            last = nc.vector.bn_stats(self.stats[:, h, j, :], y[:, h, j, :])
        self.stats_there.inc(last, tile)
        self.stats_there.this(v, tile)
        gate(self.g, v)
        for j in range(NJ):
            last = nc.vector.bn_aggr(self.mv[:, h, j, :], self.stats[:, h, j, :])
        self.mv_there.inc(last, tile)
        self.mv_there.this(v, tile)
        self.shift_there.slot_free(v, tile)
        nc.vector.tensor_scalar(self.minus[:, h, :], self.mv[:, h, :, 0], -1.0, None, ALU.mult)
        self.var_there.inc(nc.vector.tensor_scalar(self.ve[:, h, :], self.mv[:, h, :, 1], LN_EPS, None,
                                                   ALU.add), tile)

    def power(self, pool, tile):
        nc, h = self.g.nc, tile.slot()
        self.var_there.this(pool, tile)
        self.done.slot_free(pool, tile)
        self.rstd_there.inc(nc.gpsimd.tensor_tensor(self.rstd[:, h, :], self.ve[:, h, :],
                                                    self.g.minus_half[:], ALU.pow), tile)
        self.rstd_there.this(pool, tile)
        self.shift_there.inc(nc.gpsimd.tensor_tensor(self.shift[:, h, :], self.minus[:, h, :],
                                                     self.rstd[:, h, :], ALU.mult), tile)

    def scale(self, act, out, y, tile):
        self.shift_there.this(act, tile)
        h = tile.slot()
        for j in range(NJ):
            last = self.g.nc.scalar.activation(out[:, h, j, :], y[:, h, j, :], ACT.Identity,
                                               bias=self.shift[:, h, j:j + 1], scale=self.rstd[:, h, j:j + 1])
        self.done.inc(last, tile)

    def scale_by_dve(self, v, out, y, tile):
        self.shift_there.this(v, tile)
        h = tile.slot()
        for j in range(NJ):
            last = self.g.nc.vector.tensor_scalar(out[:, h, j, :], y[:, h, j, :], self.rstd[:, h, j:j + 1],
                                                  self.shift[:, h, j:j + 1], ALU.mult, ALU.add)
        self.done.inc(last, tile)

    def up(self):
        for r in (self.stats_there, self.mv_there, self.var_there, self.rstd_there, self.shift_there, self.done):
            r.up()


def store(sp, stored, tile, *pairs):
    if tile.is_last:
        stored.one_back(sp, tile)
    for table, buf in pairs:
        stored.inc(sp.dma_start(tile_of(table, tile), buf), tile, 16)


class Prefetch:

    def __init__(self, g, sb, side, edge_attr):
        self.g, self.side, self.edge_attr = g, side, edge_attr
        self.idx = sb("pre_idx", [P, 2, 2], I32)
        self.rows = sb("pre_rows", [P, 2, 2, D])
        self.there = Ring(g, "pre_there", 2, 32, "pool_dma")
        self.kept = Ring(g, "pre_kept", 2, 16, "dma")
        self.staged = Ring(g, "pre_staged")

    def gather(self, pool, tile):
        h = tile.slot()
        self.there.slot_free(pool, tile)
        self.staged.inc(self.g.nc.gpsimd.tensor_copy(self.idx[:, h, :], self.side.edge_i[:, bass.ds(tile.t * 2, 2)]),
                        tile)
        self.kept.slot_free(pool, tile)
        self.staged.this(pool, tile)
        for u in range(2):
            self.there.inc(pool.indirect_dma_start(
                out=self.rows[:, h, u, :], out_offset=None, in_=self.edge_attr,
                in_offset=bass.IndirectOffsetOnAxis(ap=self.idx[:, h, u:u + 1], axis=0)), tile, 16)

    def keep(self, sp, tile):
        self.there.this(sp, tile)
        self.kept.inc(sp.dma_start(self.side.rows[:, bass.ds(tile.t * 2, 2), :], self.rows[:, tile.slot()]),
                      tile, 16)

    def up(self):
        for r in (self.there, self.kept, self.staged):
            r.up()


def gat_project_pass(g, x):
    nc = g.nc
    g.proj = g.dram("proj", [N, AW])
    g.tgt_score = g.dram("tgt_score", [N, HEADS])
    W = D + 2 * HEADS
    ctx, sb, ps = scope(g)
    with ctx:
        xin = sb("xin", [P, 4, NJ, D])
        x_t = sb("x_t", [P, 2, NB])
        pout = sb("pout", [P, 2, NJ, AW])
        sout = sb("sout", [P, 2, NJ, HEADS])
        t_ps = ps("t_ps", [P, 2, 512])
        o_ps = ps("o_ps", [P, 2, 2, 512])
        loaded = Ring(g, "node_loaded", 4, 16, "dma")
        stored = Ring(g, "node_stored", 2, 32, "dma")
        turned, x_t_there, product, ready = rings(g, "node_turned", "node_turned_sb", "node_product", "node_ready")
        with g.block() as block:
            @block.sync
            def _(sp):
                def loads(tile):
                    turned.four_back(sp, tile)
                    loaded.inc(sp.dma_start(flat(xin[:, tile.slot(4)]), tile_of(x, tile)), tile, 16)

                def stores(tile):
                    ready.this(sp, tile)
                    store(sp, stored, tile, (g.proj, flat(pout[:, tile.slot()])),
                          (g.tgt_score, flat(sout[:, tile.slot()])))

                run_tiles(sp, (3, loads), (-1, stores))
                stored.all(sp)

            @block.tensor
            def _(pe):
                def turns(tile):
                    loaded.this(pe, tile)
                    x_t_there.slot_free(pe, tile)
                    turned.inc(turn(g, t_ps[:, tile.slot()], xin[:, tile.slot(4)]), tile)

                def products(tile):
                    h = tile.slot()
                    x_t_there.this(pe, tile)
                    ready.slot_free(pe, tile)
                    for j in range(NJ):
                        last = nc.tensor.matmul(o_ps[:, h, j // 2, (j % 2) * W:(j % 2 + 1) * W],
                                                x_t[:, h, j * P:(j + 1) * P], g.w_proj[:], start=True, stop=True)
                    product.inc(last, tile)

                run_tiles(pe, (1, turns), (0, products))

            @block.scalar
            def _(act):
                def copies(tile):
                    turned.this(act, tile)
                    product.slot_free(act, tile)
                    x_t_there.inc(nc.scalar.copy(x_t[:, tile.slot(), :], t_ps[:, tile.slot(), :]), tile)

                run_tiles(act, (0, copies))

            @block.vector
            def _(v):
                def outs(tile):
                    h = tile.slot()
                    product.this(v, tile)
                    stored.slot_free(v, tile)
                    for b in range(2):
                        o = o_ps[:, h, b, 0:2 * W].rearrange("p (j w) -> p j w", w=W)
                        nc.vector.tensor_copy(pout[:, h, 2 * b:2 * b + 2, :], o[:, :, 0:AW])
                        last = nc.vector.tensor_copy(sout[:, h, 2 * b:2 * b + 2, :], o[:, :, AW:W])
                    ready.inc(last, tile)

                run_tiles(v, (0, outs))
        for r in (loaded, stored, turned, x_t_there, product, ready):
            r.up()


def gat_score_pass(g, s, e_sb):
    nc = g.nc
    ctx, sb, ps = scope(g)
    with ctx:
        rowbuf = sb("rowbuf", [P, 2, U, AW])
        tgt = sb("tgt", [P, 2, U, HEADS])
        raw = sb("raw", [P, 2, U, HEADS])
        gmax = sb("gmax", [P, 3])
        st_src, st_key = Stage(g, sb, "gather"), Stage(g, sb, "second")
        got = Halves(g, "score_rows", 16 * U * 2, by_pool=True)
        kept = Halves(g, "score_kept", 16)
        summed, scored = all_halves(g, "score_sum", "score_done")
        keys = g.sem("key_row_loaded", "dma")
        with g.block() as block:
            @block.scalar
            def _(act):
                load_key_row(g, act, s, keys)
                act.wait_ge(keys.sem, keys.base + 16)

            @block.sync
            def _(sp):
                def keep(half, it):
                    got.this(sp, half, it)
                    kept.inc(sp.dma_start(g.rows[:, bass.ds(it * (2 * U) + half * U, U), :],
                                          rowbuf[:, half, :, 0:D]), half)

                def stage(half, it):
                    got.two_back(sp, half, it)
                    st_src.load(sp, s.other_i, half, it)
                    st_key.load(sp, s.key_i, half, it)

                stage(0, 0)
                with sp.Fori(0, STEPS - 1) as it:
                    for half in range(2):
                        stage(1 - half, it + half)
                        keep(half, it)
                stage(1, STEPS - 1)
                keep(0, STEPS - 1)
                keep(1, STEPS - 1)
                for half in range(2):
                    kept.two_back(sp, half, STEPS)

            @block.gpsimd
            def _(pool):
                with pool.Fori(0, STEPS) as it:
                    for half in range(2):
                        st_src.there.this(pool, half, it)
                        st_key.there.this(pool, half, it)
                        summed.two_back(pool, half, it)
                        kept.two_back(pool, half, it)
                        for ins in gather(pool, st_src, g.proj, lambda u: rowbuf[:, half, u, :], half):
                            ins.then_inc(got.c[half].sem, 16)
                        for ins in gather(pool, st_key, g.tgt_score, lambda u: tgt[:, half, u, :], half):
                            ins.then_inc(got.c[half].sem, 16)

            @block.vector
            def _(v):
                with v.Fori(0, STEPS) as it:
                    for half in range(2):
                        got.this(v, half, it)
                        summed.inc(nc.vector.tensor_tensor(raw[:, half], rowbuf[:, half, :, D:AW], tgt[:, half],
                                                           ALU.add), half)
                        summed.this(v, half, it)
                        scored.inc(nc.vector.scalar_tensor_tensor(
                            e_sb[:, bass.ds(it * (2 * U) + half * U, U), :], raw[:, half], 0.2, raw[:, half],
                            ALU.mult, ALU.max), half)
                        scored.this(v, half, it)
        keys.up(16)
        for h in (st_src.there, st_key.there, got, kept, summed, scored):
            h.up(STEPS)
        dve, maxed, negated, powered = g.sem("max_dve"), g.sem("max_all"), g.sem("max_neg"), g.sem("max_exp")
        dve_base = dve.base
        with g.block() as block:
            @block.vector
            def _(v):
                ch = Chain(v, dve)
                ch.link(nc.vector.memset(e_sb[0:88, CH - 1, :], FAR))
                ch.step(nc.vector.reduce_max(gmax[:, 0:1], e_sb[:].rearrange("p c h -> p (c h)"), AX_X))
                v.wait_ge(maxed.sem, maxed.base + 1)
                nc.vector.tensor_scalar(gmax[:, 2:3], gmax[:, 1:2], -1.0, None, ALU.mult).then_inc(negated.sem, 1)
                ch.finish()

            @block.gpsimd
            def _(pool):
                pool.wait_ge(dve.sem, dve_base + 2)
                nc.gpsimd.partition_all_reduce(gmax[:, 1:2], gmax[:, 0:1], P, RMAX).then_inc(maxed.sem, 1)

            @block.scalar
            def _(act):
                act.wait_ge(negated.sem, negated.base + 1)
                nc.scalar.activation(e_sb[:], e_sb[:], ACT.Exp, bias=gmax[:, 2:3]).then_inc(powered.sem, 1)
                act.wait_ge(powered.sem, powered.base + 1)
        maxed.up(1)
        negated.up(1)
        powered.up(1)


def gat_finish_pass(g, x, side, edge_attr):
    nc = g.nc
    g.x1 = g.dram("x1", [N, D])
    g.hid_a = g.dram("hid_a", [N, HID])
    ctx, sb, ps = scope(g)
    with ctx:
        xin = sb("xin", [P, 4, NJ, D])
        agg = sb("agg", [P, 4, NJ, AW])
        x_t = sb("x_t", [P, 2, NB])
        y_t = sb("y_t", [P, 2, NB])
        den = sb("den", [P, 2, NJ, HEADS])
        rden = sb("rden", [P, 2, NJ, HEADS])
        mean = sb("mean", [P, 2, NJ, D])
        t = sb("t", [P, 2, NJ, D])
        power = sb("power", [P, 2, NJ, D])
        low = sb("low", [P, 2, NJ, D])
        y = sb("y", [P, 2, NJ, D])
        x1 = sb("x1_sb", [P, 2, NJ, D])
        h = sb("h_sb", [P, 2, NJ, HID])
        t_ps = ps("t_ps", [P, 2, 512])
        o_ps = ps("o_ps", [P, 2, 512])
        y_ps = ps("y_ps", [P, 2, 512])
        h_ps = ps("h_ps", [P, 2, 512])
        ln = Norm(g, sb)
        pre = Prefetch(g, sb, side, edge_attr)
        loaded = Ring(g, "node_loaded", 4, 32, "dma")
        x1_stored, h_stored = Ring(g, "x1_stored", 2, 16, "dma"), Ring(g, "hid_stored", 2, 16, "dma")
        turned, x_t_there, product, den_there, rden_there, mean_there, t_there, exped, low_there, summed = rings(
            g, "node_turned", "node_turned_sb", "node_product", "fin_den", "fin_rden", "fin_mean", "fin_t",
            "fin_exp", "fin_low", "fin_sum")
        turned1, y_t_there, product1, h_there = rings(g, "fin_turned", "fin_turned_sb", "fin_product", "fin_h")
        with g.block() as block:
            @block.sync
            def _(sp):
                def loads(tile):
                    turned.four_back(sp, tile)
                    summed.four_back(sp, tile)
                    loaded.inc(sp.dma_start(flat(xin[:, tile.slot(4)]), tile_of(x, tile)), tile, 16)
                    loaded.inc(sp.dma_start(flat(agg[:, tile.slot(4)]), tile_of(g.agg_dst, tile)), tile, 16)

                def store_x1(tile):
                    ln.done.this(sp, tile)
                    store(sp, x1_stored, tile, (g.x1, flat(x1[:, tile.slot()])))

                def store_h(tile):
                    h_there.this(sp, tile)
                    store(sp, h_stored, tile, (g.hid_a, flat(h[:, tile.slot()])))

                run_tiles(sp, (3, loads), (-1, lambda tile: pre.keep(sp, tile)), (-2, store_x1), (-4, store_h))
                for r in (x1_stored, h_stored, pre.kept):
                    r.all(sp)

            @block.tensor
            def _(pe):
                def turns(tile):
                    loaded.this(pe, tile)
                    x_t_there.slot_free(pe, tile)
                    turned.inc(turn(g, t_ps[:, tile.slot()], xin[:, tile.slot(4)]), tile)

                def products(tile):
                    s = tile.slot()
                    x_t_there.this(pe, tile)
                    t_there.slot_free(pe, tile)
                    for j in range(NJ):
                        last = nc.tensor.matmul(o_ps[:, s, j * D:(j + 1) * D], x_t[:, s, j * P:(j + 1) * P],
                                                g.w_skip[:], start=True, stop=True)
                    product.inc(last, tile)

                def turns_x1(tile):
                    ln.done.this(pe, tile)
                    y_t_there.slot_free(pe, tile)
                    turned1.inc(turn(g, y_ps[:, tile.slot()], x1[:, tile.slot()]), tile)

                def products_x1(tile):
                    s = tile.slot()
                    y_t_there.this(pe, tile)
                    h_there.slot_free(pe, tile)
                    for j in range(NJ):
                        last = nc.tensor.matmul(h_ps[:, s, j * HID:(j + 1) * HID], y_t[:, s, j * P:(j + 1) * P],
                                                g.w1[:], start=True, stop=True)
                    product1.inc(last, tile)

                run_tiles(pe, (2, turns), (1, products), (-2, turns_x1), (-3, products_x1))

            @block.scalar
            def _(act):
                def copy_x(tile):
                    turned.this(act, tile)
                    product.slot_free(act, tile)
                    x_t_there.inc(nc.scalar.copy(x_t[:, tile.slot()], t_ps[:, tile.slot()]), tile)

                def exps(tile):
                    t_there.this(act, tile)
                    low_there.slot_free(act, tile)
                    exped.inc(nc.scalar.activation(power[:, tile.slot()], t[:, tile.slot()], ACT.Exp), tile)

                def scales(tile):
                    x1_stored.slot_free(act, tile)
                    turned1.slot_free(act, tile)
                    ln.scale(act, x1, y, tile)

                def copy_x1(tile):
                    turned1.this(act, tile)
                    product1.slot_free(act, tile)
                    y_t_there.inc(nc.scalar.copy(y_t[:, tile.slot()], y_ps[:, tile.slot()]), tile)

                def copy_h(tile):
                    product1.this(act, tile)
                    h_stored.slot_free(act, tile)
                    h_there.inc(nc.scalar.copy(flat(h[:, tile.slot()]), h_ps[:, tile.slot(), 0:NJ * HID]), tile)

                run_tiles(act, (2, copy_x), (-2, copy_x1), (-3, copy_h), (-1, scales), (1, exps))

            @block.vector
            def _(v):
                def outs(tile):
                    s, s4 = tile.slot(), tile.slot(4)
                    loaded.this(v, tile)
                    den_there.inc(nc.vector.tensor_scalar(den[:, s], agg[:, s4, :, D:AW], 1e-16, None, ALU.add), tile)
                    den_there.this(v, tile)
                    rden_there.inc(nc.vector.reciprocal(rden[:, s], den[:, s]), tile)
                    rden_there.this(v, tile)
                    for j in range(NJ):
                        last = nc.vector.tensor_tensor(
                            mean[:, s, j].rearrange("p (h f) -> p h f", f=HF),
                            agg[:, s4, j, 0:D].rearrange("p (h f) -> p h f", f=HF),
                            rden[:, s, j].unsqueeze(2).to_broadcast([P, HEADS, HF]), ALU.mult)
                    mean_there.inc(last, tile)
                    mean_there.this(v, tile)
                    product.this(v, tile)
                    exped.slot_free(v, tile)
                    t_there.inc(nc.vector.tensor_tensor(flat(t[:, s]), flat(mean[:, s]), o_ps[:, s], ALU.add), tile)

                def sums(tile):
                    s = tile.slot()
                    exped.this(v, tile)
                    low_there.inc(nc.vector.scalar_tensor_tensor(
                        flat(low[:, s]), flat(power[:, s]), 1.0, flat(xin[:, tile.slot(4)]), ALU.min, ALU.add), tile)
                    low_there.this(v, tile)
                    ln.done.slot_free(v, tile)
                    summed.inc(nc.vector.scalar_tensor_tensor(flat(y[:, s]), flat(t[:, s]), 0.0, flat(low[:, s]),
                                                              ALU.max, ALU.add), tile)
                    summed.this(v, tile)
                    ln.moments(v, y, tile)

                run_tiles(v, (1, outs), (0, sums))

            @block.gpsimd
            def _(pool):
                run_tiles(pool, (0, lambda tile: ln.power(pool, tile)), (0, lambda tile: pre.gather(pool, tile)))
        for r in (ln, pre, loaded, x1_stored, h_stored, turned, x_t_there, product, den_there, rden_there, mean_there,
                  t_there, exped, low_there, summed, turned1, y_t_there, product1, h_there):
            r.up()


def gcn_finish_pass(g, side, edge_attr, next_side):
    nc = g.nc
    g.x2 = g.dram("x2", [N, D])
    g.node_score = g.dram("node_score", [N, 1])
    ctx, sb, ps = scope(g)
    with ctx:
        xin = sb("xin", [P, 4, NJ, D])
        agg = sb("agg", [P, 4, NJ, HID])
        a_t = sb("a_t", [HID + 1, 2, NB])
        sig = sb("sig", [P, 2, NJ, D])
        y = sb("y", [P, 2, NJ, D])
        x2 = sb("x2_sb", [P, 2, NJ, D])
        junk = sb("junk", [P, 2, NJ, D], BF16)
        dot = sb("dot", [P, 2, NJ])
        sc = sb("sc", [P, 2, NJ])
        t_ps = ps("t_ps", [P, 2, 512])
        o_ps = ps("o_ps", [P, 2, 512])
        ln = Norm(g, sb)
        pre = Prefetch(g, sb, side, edge_attr)
        loaded = Ring(g, "node_loaded", 4, 32, "dma")
        x2_stored, sc_stored = Ring(g, "x2_stored", 2, 16, "dma"), Ring(g, "score_stored", 2, 16, "dma")
        turned, a_t_there, product, squashed, summed, dotted, scored = rings(
            g, "node_turned", "node_turned_sb", "node_product", "gcn_squashed", "gcn_summed", "gcn_dotted", "gcn_scored")
        ones, keys = g.sem("gcn_ones"), g.sem("key_row_loaded", "dma")
        with g.block() as block:
            @block.vector
            def _(v):
                nc.vector.memset(a_t[HID:HID + 1, :, :], 1.0).then_inc(ones.sem, 1)
                v.wait_ge(ones.sem, ones.base + 1)
        ones.up(1)
        with g.block() as block:
            @block.sync
            def _(sp):
                def loads(tile):
                    summed.four_back(sp, tile)
                    turned.four_back(sp, tile)
                    loaded.inc(sp.dma_start(flat(xin[:, tile.slot(4)]), tile_of(g.x1, tile)), tile, 16)
                    loaded.inc(sp.dma_start(flat(agg[:, tile.slot(4)]), tile_of(g.agg_hid2, tile)), tile, 16)

                def store_x2(tile):
                    ln.done.this(sp, tile)
                    store(sp, x2_stored, tile, (g.x2, flat(x2[:, tile.slot()])))

                def store_scores(tile):
                    scored.this(sp, tile)
                    store(sp, sc_stored, tile, (g.node_score, sc[:, tile.slot()]))

                load_key_row(g, sp, next_side, keys)
                run_tiles(sp, (3, loads), (-1, lambda tile: pre.keep(sp, tile)), (-2, store_x2), (-3, store_scores))
                sp.wait_ge(keys.sem, keys.base + 16)
                for r in (x2_stored, sc_stored, pre.kept):
                    r.all(sp)

            @block.tensor
            def _(pe):
                def turns(tile):
                    loaded.this(pe, tile)
                    a_t_there.slot_free(pe, tile)
                    gate(g, pe)
                    turned.inc(turn(g, t_ps[:, tile.slot()], agg[:, tile.slot(4)], HID), tile)

                def products(tile):
                    s = tile.slot()
                    a_t_there.this(pe, tile)
                    squashed.slot_free(pe, tile)
                    for j in range(NJ):
                        last = nc.tensor.matmul(o_ps[:, s, j * D:(j + 1) * D], a_t[:, s, j * P:(j + 1) * P],
                                                g.w2[:], start=True, stop=True)
                    product.inc(last, tile)

                run_tiles(pe, (2, turns), (1, products))

            @block.scalar
            def _(act):
                def copies(tile):
                    turned.this(act, tile)
                    product.slot_free(act, tile)
                    a_t_there.inc(nc.scalar.copy(a_t[0:HID, tile.slot(), :], t_ps[0:HID, tile.slot(), :]), tile)

                def squash(tile):
                    product.this(act, tile)
                    summed.slot_free(act, tile)
                    squashed.inc(nc.scalar.activation(flat(sig[:, tile.slot()]), o_ps[:, tile.slot()],
                                                      ACT.Sigmoid), tile)

                def scales(tile):
                    x2_stored.slot_free(act, tile)
                    dotted.slot_free(act, tile)
                    ln.scale(act, x2, y, tile)

                run_tiles(act, (2, copies), (0, squash), (-1, scales))

            @block.vector
            def _(v):
                def sums(tile):
                    s = tile.slot()
                    loaded.this(v, tile)
                    squashed.this(v, tile)
                    ln.done.slot_free(v, tile)
                    summed.inc(nc.vector.tensor_tensor(y[:, s], sig[:, s], xin[:, tile.slot(4)], ALU.add), tile)
                    summed.this(v, tile)
                    ln.moments(v, y, tile)

                def scores(tile):
                    s = tile.slot()
                    ln.done.this(v, tile)
                    for j in range(NJ):
                        last = nc.vector.scalar_tensor_tensor(junk[:, s, j], x2[:, s, j], 1.0, g.att[:, 0:D],
                                                              ALU.mult, ALU.mult, accum_out=dot[:, s, j:j + 1])
                    dotted.inc(last, tile)
                    dotted.this(v, tile)
                    sc_stored.slot_free(v, tile)
                    scored.inc(nc.vector.tensor_scalar(sc[:, s], dot[:, s], g.att_b[:], None, ALU.add), tile)

                run_tiles(v, (0, sums), (-2, scores))

            @block.gpsimd
            def _(pool):
                run_tiles(pool, (0, lambda tile: ln.power(pool, tile)), (0, lambda tile: pre.gather(pool, tile)))
        keys.up(16)
        for r in (ln, pre, loaded, x2_stored, sc_stored, turned, a_t_there, product, squashed, summed, dotted, scored):
            r.up()


def att_score_pass(g, s, score, top):
    nc = g.nc
    ctx, sb, ps = scope(g)
    with ctx:
        rowbuf = sb("rowbuf", [P, 2, U, D])
        node = sb("node", [P, 2, U])
        junk = sb("junk", [P, 2, U, D], BF16)
        dot = sb("dot", [P, 2, U])
        raw = sb("raw", [P, 2, U])
        leaky = sb("leaky", [P, 2, U])
        diag = sb("diag", [P, 2, U, P])
        far = sb("far", [P, 2, U, P])
        full = sb("full", [P, 2, U, P])
        ones = sb("ones", [P, P])
        row_ps = ps("row_ps", [P, 2, 1024])
        st_key = Stage(g, sb, "second")
        loaded = Halves(g, "score_rows", 16)
        got = Halves(g, "score_nodes", 16 * U, by_pool=True)
        dotted, summed, scored, diagonal, apart, spread, masked, topped = all_halves(
            g, "att_dotted", "att_summed", "att_scored", "att_diagonal", "att_apart", "att_spread", "att_masked", "att_topped")
        set_up = g.sem("att_ones")
        with g.block() as block:
            @block.vector
            def _(v):
                nc.vector.memset(ones[:], 1.0).then_inc(set_up.sem, 1)
                v.wait_ge(set_up.sem, set_up.base + 1)
        set_up.up(1)
        with g.block() as block:
            @block.sync
            def _(sp):
                with sp.Fori(0, STEPS) as it:
                    for half in range(2):
                        got.two_back(sp, half, it)
                        st_key.load(sp, s.key_i, half, it)
                        dotted.two_back(sp, half, it)
                        loaded.inc(sp.dma_start(rowbuf[:, half],
                                                s.rows[:, bass.ds(it * (2 * U) + half * U, U), :]), half)

            @block.gpsimd
            def _(pool):
                with pool.Fori(0, STEPS) as it:
                    for half in range(2):
                        st_key.there.this(pool, half, it)
                        summed.two_back(pool, half, it)
                        for ins in gather(pool, st_key, g.node_score, lambda u: node[:, half, u:u + 1], half):
                            ins.then_inc(got.c[half].sem, 16)

            @block.tensor
            def _(pe):
                with pe.Fori(0, STEPS) as it:
                    for half in range(2):
                        diagonal.this(pe, half, it)
                        masked.two_back(pe, half, it)
                        for u in range(U):
                            last = nc.tensor.matmul(row_ps[:, half, u * P:(u + 1) * P], ones[:],
                                                    diag[:, half, u, :], start=True, stop=True)
                        spread.inc(last, half)

            @block.vector
            def _(v):
                def scores(half, it):
                    first = it * (2 * U) + half * U
                    loaded.this(v, half, it)
                    for u in range(U):
                        last = nc.vector.scalar_tensor_tensor(
                            junk[:, half, u, :], rowbuf[:, half, u, :], 1.0, g.att[:, D:2 * D], ALU.mult,
                            ALU.mult, accum_out=dot[:, half, u:u + 1])
                    dotted.inc(last, half)
                    dotted.this(v, half, it)
                    got.this(v, half, it)
                    summed.inc(nc.vector.tensor_tensor(raw[:, half], dot[:, half], node[:, half], ALU.add), half)
                    summed.this(v, half, it)
                    scored.inc(nc.vector.scalar_tensor_tensor(leaky[:, half], raw[:, half], 0.2, raw[:, half],
                                                              ALU.mult, ALU.max), half)
                    scored.this(v, half, it)
                    nc.vector.tensor_copy(score[:, bass.ds(first, U)], leaky[:, half])
                    for u in range(U):
                        last = nc.vector.tensor_scalar(diag[:, half, u, :], g.ident[:], leaky[:, half, u:u + 1],
                                                       None, ALU.mult)
                    diagonal.inc(last, half)
                    for u in range(U):
                        last = nc.vector.tensor_scalar(far[:, half, u, :], chunk_keys(g, first + u),
                                                       s.key[:, bass.ds(first + u, 1)], FAR, ALU.not_equal,
                                                       ALU.mult)
                    apart.inc(last, half)

                def tops(half, it):
                    first = it * (2 * U) + half * U
                    apart.this(v, half, it)
                    spread.this(v, half, it)
                    masked.inc(nc.vector.tensor_tensor(
                        full[:, half].rearrange("p u q -> p (u q)"), far[:, half].rearrange("p u q -> p (u q)"),
                        row_ps[:, half, 0:U * P], ALU.add), half)
                    masked.this(v, half, it)
                    topped.inc(nc.vector.reduce_max(top[:, bass.ds(first, U)], full[:, half], AX_X), half)

                scores(0, 0)
                with v.Fori(0, STEPS - 1) as it:
                    for half in range(2):
                        scores(1 - half, it + half)
                        tops(half, it)
                scores(1, STEPS - 1)
                tops(0, STEPS - 1)
                tops(1, STEPS - 1)
                for half in range(2):
                    topped.two_back(v, half, STEPS)
        for h in (st_key.there, loaded, got, dotted, summed, scored, diagonal, apart,
                  spread, masked, topped):
            h.up(STEPS)


def att_max_pass(g, s, score, top):
    nc = g.nc
    ctx, sb, ps = scope(g)
    with ctx:
        key_first = sb("key_first", [1, CH])
        top_first = sb("top_first", [1, CH])
        whole = sb("whole", [1, CH])
        goes_on = sb("goes_on", [1, 2, CH])
        pen = sb("pen", [1, 2, CH])
        run = sb("run", [1, 2, CH])
        rows = sb("rows", [1, 4, CH])
        wide = sb("wide", [P, 4, CH])
        t1 = sb("t1", [P, 2, CH])
        t2 = sb("t2", [P, 2, CH])
        loaded, dve, spread, powered = g.sem("amax_loaded", "dma"), g.sem("amax_dve"), g.sem("amax_spread"), g.sem("amax_exp")
        with g.block() as block:
            @block.sync
            def _(sp):
                sp.dma_start(key_first[:], s.key_d[P - 1:P, :]).then_inc(loaded.sem, 16)
                sp.dma_start(top_first[:], top[P - 1:P, :]).then_inc(loaded.sem, 16)

            @block.vector
            def _(v):
                ch = Chain(v, dve)
                v.wait_ge(loaded.sem, loaded.base + 32)
                key_last = s.key[0:1, :]
                ch.step(nc.vector.memset(goes_on[:], 0.0))
                ch.step(nc.vector.memset(rows[:], FAR))
                ch.link(nc.vector.tensor_tensor(whole[:], key_first[:], key_last, ALU.is_equal))
                ch.step(nc.vector.tensor_tensor(goes_on[:, 0, :], key_first[:], s.before[:], ALU.is_equal))
                ch.link(nc.vector.tensor_tensor(goes_on[:, 1, 0:CH - 1], key_first[:, 1:CH], key_last[:, 0:CH - 1],
                                                ALU.is_equal))
                for d in range(2):
                    ch.step(nc.vector.tensor_tensor(pen[:, d, :], goes_on[:, d, :], whole[:], ALU.mult))
                ch.hold()
                ch.link(nc.vector.tensor_scalar(pen[:], pen[:], -FAR, FAR, ALU.mult, ALU.add))
                ch.step(nc.vector.tensor_tensor_scan(run[:, 0, :], pen[:, 0, :], top[0:1, :], FAR, ALU.add, ALU.max))
                ch.link(nc.vector.tensor_tensor_scan(run[:, 1, ::-1], pen[:, 1, ::-1], top_first[:, ::-1], FAR,
                                                     ALU.add, ALU.max))
                ch.step(nc.vector.tensor_copy(rows[:, 0, 1:CH], run[:, 0, 0:CH - 1]))
                ch.step(nc.vector.tensor_copy(rows[:, 1, :], s.before[:]))
                ch.step(nc.vector.tensor_copy(rows[:, 2, 0:CH - 1], run[:, 1, 1:CH]))
                ch.link(nc.vector.tensor_copy(rows[:, 3, 0:CH - 1], key_first[:, 1:CH]))
                ch.finish()
        with g.block() as block:
            @block.gpsimd
            def _(pool):
                nc.gpsimd.partition_broadcast(wide[:].rearrange("p a c -> p (a c)"),
                                              rows[:].rearrange("p a c -> p (a c)"), P).then_inc(spread.sem, 1)
                pool.wait_ge(spread.sem, spread.base + 1)
        with g.block() as block:
            @block.vector
            def _(v):
                ch = Chain(v, dve)
                for d in range(2):
                    ch.step(nc.vector.tensor_tensor(t1[:, d, :], s.key[:], wide[:, 2 * d + 1, :], ALU.not_equal))
                ch.hold()
                for d in range(2):
                    ch.step(nc.vector.scalar_tensor_tensor(t2[:, d, :], t1[:, d, :], FAR, wide[:, 2 * d, :],
                                                           ALU.mult, ALU.add))
                ch.hold()
                for d in range(2):
                    ch.link(nc.vector.tensor_tensor(top[:], top[:], t2[:, d, :], ALU.max))
                ch.link(nc.vector.tensor_tensor(score[:], score[:], top[:], ALU.subtract))
                ch.finish()
        with g.block() as block:
            @block.scalar
            def _(act):
                nc.scalar.activation(score[:], score[:], ACT.Exp).then_inc(powered.sem, 1)
                act.wait_ge(powered.sem, powered.base + 1)
        loaded.up(32)
        spread.up(1)
        powered.up(1)


def att_finish_pass(g):
    nc = g.nc
    g.x3 = g.dram("x3", [N, D])
    ctx, sb, ps = scope(g)
    with ctx:
        xin = sb("xin", [P, 4, NJ, D])
        agg = sb("agg", [P, 4, 2, NJ, AW])
        none, mx, less, fac, part, coef = [sb(n, [P, 2, 2, NJ]) for n in ("none", "mx", "less", "fac", "part", "coef")]
        both, den, empty, safe, rden, keep = [sb(n, [P, 2, NJ])
                                              for n in ("both", "den", "empty", "safe", "rden", "keep")]
        first = sb("first", [P, 2, NJ, D])
        mean = sb("mean", [P, 2, NJ, D])
        gel = sb("gel", [P, 2, NJ, D])
        y = sb("y", [P, 2, NJ, D])
        x3 = sb("x3_sb", [P, 2, NJ, D])
        ln = Norm(g, sb)
        loaded, stored = Ring(g, "node_loaded", 4, 32, "dma"), Ring(g, "node_stored", 2, 16, "dma")
        x_loaded = Ring(g, "node_x_loaded", 4, 16, "dma")
        none_there, mx_there, both_there, less_there, exped, part_there, den_there, empty_there, safe_there = rings(
            g, "join_none", "join_mx", "join_both", "join_less", "join_exp", "join_part", "join_den", "join_empty",
            "join_safe")
        rden_there, coef_there, first_there, mean_there, gelued, summed = rings(
            g, "join_rden", "join_coef", "join_first", "join_mean", "join_gelu", "join_sum")
        with g.block() as block:
            @block.sync
            def _(sp):
                def loads(tile):
                    mean_there.four_back(sp, tile)
                    s = tile.slot(4)
                    loaded.inc(sp.dma_start(flat(agg[:, s, 0]), tile_of(g.agg_src, tile)), tile, 16)
                    loaded.inc(sp.dma_start(flat(agg[:, s, 1]), tile_of(g.agg_dst, tile)), tile, 16)

                def skips(tile):
                    summed.four_back(sp, tile)
                    x_loaded.inc(sp.dma_start(flat(xin[:, tile.slot(4)]), tile_of(g.x2, tile)), tile, 16)

                def stores(tile):
                    ln.done.this(sp, tile)
                    store(sp, stored, tile, (g.x3, flat(x3[:, tile.slot()])))

                run_tiles(sp, (3, loads), (2, skips), (-3, stores))
                stored.all(sp)

            @block.scalar
            def _(act):
                def exps(tile):
                    less_there.this(act, tile)
                    coef_there.slot_free(act, tile)
                    exped.inc(nc.scalar.activation(fac[:, tile.slot()], less[:, tile.slot()], ACT.Exp), tile)

                def gelus(tile):
                    mean_there.this(act, tile)
                    summed.slot_free(act, tile)
                    gelued.inc(nc.scalar.activation(flat(gel[:, tile.slot()]), flat(mean[:, tile.slot()]),
                                                    ACT.Gelu), tile)

                def scales(tile):
                    stored.slot_free(act, tile)
                    ln.scale(act, x3, y, tile)

                run_tiles(act, (2, exps), (-2, scales), (0, gelus))

            @block.vector
            def _(v):
                def done(ring, ins, tile):
                    ring.inc(ins, tile)
                    ring.this(v, tile)

                def maxima(tile):
                    s, s4 = tile.slot(), tile.slot(4)
                    loaded.this(v, tile)
                    done(none_there, nc.vector.tensor_scalar(none[:, s], agg[:, s4, :, :, D], 0.0, FAR, ALU.is_equal,
                                                             ALU.mult), tile)
                    done(mx_there, nc.vector.tensor_tensor(mx[:, s], agg[:, s4, :, :, D + 1], none[:, s], ALU.add),
                         tile)
                    done(both_there, nc.vector.tensor_tensor(both[:, s], mx[:, s, 0], mx[:, s, 1], ALU.max), tile)
                    exped.slot_free(v, tile)
                    less_there.inc(nc.vector.tensor_tensor(
                        less[:, s], mx[:, s], both[:, s].unsqueeze(1).to_broadcast([P, 2, NJ]), ALU.subtract), tile)

                def means(tile):
                    s, s4 = tile.slot(), tile.slot(4)
                    exped.this(v, tile)
                    done(part_there, nc.vector.tensor_tensor(part[:, s], fac[:, s], agg[:, s4, :, :, D], ALU.mult),
                         tile)
                    done(den_there, nc.vector.tensor_tensor(den[:, s], part[:, s, 0], part[:, s, 1], ALU.add), tile)
                    done(empty_there, nc.vector.tensor_scalar(empty[:, s], den[:, s], 0.0, None, ALU.is_equal), tile)
                    nc.vector.tensor_scalar(keep[:, s], empty[:, s], 1.0, None, ALU.add)
                    done(safe_there, nc.vector.tensor_tensor(safe[:, s], den[:, s], empty[:, s], ALU.add), tile)
                    done(rden_there, nc.vector.reciprocal(rden[:, s], safe[:, s]), tile)
                    done(coef_there, nc.vector.tensor_tensor(
                        coef[:, s], fac[:, s], rden[:, s].unsqueeze(1).to_broadcast([P, 2, NJ]), ALU.mult), tile)
                    for j in range(NJ):
                        last = nc.vector.tensor_scalar(first[:, s, j], agg[:, s4, 0, j, 0:D], coef[:, s, 0, j:j + 1],
                                                       None, ALU.mult)
                    done(first_there, last, tile)
                    gelued.slot_free(v, tile)
                    for j in range(NJ):
                        last = nc.vector.scalar_tensor_tensor(mean[:, s, j], agg[:, s4, 1, j, 0:D],
                                                              coef[:, s, 1, j:j + 1], first[:, s, j],
                                                              ALU.mult, ALU.add)
                    mean_there.inc(last, tile)

                def sums(tile):
                    s = tile.slot()
                    x_loaded.this(v, tile)
                    gelued.this(v, tile)
                    ln.done.slot_free(v, tile)
                    for j in range(NJ):
                        last = nc.vector.scalar_tensor_tensor(y[:, s, j], xin[:, tile.slot(4), j],
                                                              keep[:, s, j:j + 1], gel[:, s, j], ALU.mult, ALU.add)
                    summed.inc(last, tile)
                    summed.this(v, tile)
                    ln.moments(v, y, tile)

                run_tiles(v, (2, maxima), (-1, sums), (1, means))

            @block.gpsimd
            def _(pool):
                run_tiles(pool, (-1, lambda tile: ln.power(pool, tile)))
        for r in (ln, loaded, x_loaded, stored, none_there, mx_there, both_there, less_there, exped, part_there, den_there,
                  empty_there, safe_there, rden_there, coef_there, first_there, mean_there, gelued, summed):
            r.up()


def gru_pass(g, step, h_in, h_out, x3=None):
    nc = g.nc
    final = x3 is not None
    ctx, sb, ps = scope(g)
    with ctx:
        hin = sb("hin", [P, 4, NJ, D])
        agg = sb("agg", [P, 4, NJ, AW])
        xin = sb("xin", [P, 4, NJ, D]) if final else None
        h_t, a_t, r, z, gated, pre, new, diff, mixed, h_new = [
            sb(n, [P, 2, NB]) for n in ("h_t", "a_t", "r", "z", "gated", "pre", "new", "diff", "mixed", "h_new")]
        hout = sb("hout", [P, 2, NJ, D])
        y = sb("y", [P, 2, NJ, D]) if final else None
        turn_ps = ps("turn_ps", [P, 2, 512])
        gate_ps = ps("gate_ps", [P, 4, 512])
        back_ps = ps("back_ps", [P, 2, 512])
        ln = Norm(g, sb) if final else None
        loaded, stored = Ring(g, "node_loaded", 4, 32, "dma"), Ring(g, "node_stored", 2, 16, "dma")
        x_loaded = Ring(g, "gru_x_loaded", 4, 16, "dma") if final else None
        a_turned, h_turned, a_there, h_there, r_prod, z_prod, n_prod, i_prod = rings(
            g, "gru_a_turned", "gru_h_turned", "gru_a", "gru_h", "gru_r_product", "gru_z_product",
            "gru_n_product", "gru_i_product")
        r_there, z_there, gated_there, pre_there, new_there, diff_there, mixed_there, h_new_there, back, out_there = \
            rings(g, "gru_r", "gru_z", "gru_gated", "gru_pre", "gru_new", "gru_diff", "gru_mixed", "gru_h_new",
                  "gru_back", "gru_out")
        with g.block() as block:
            @block.sync
            def _(sp):
                def loads(tile):
                    h_turned.four_back(sp, tile)
                    s = tile.slot(4)
                    loaded.inc(sp.dma_start(flat(hin[:, s]), tile_of(h_in, tile)), tile, 16)
                    loaded.inc(sp.dma_start(flat(agg[:, s]), tile_of(g.agg_dst, tile)), tile, 16)

                def skips(tile):
                    out_there.four_back(sp, tile)
                    x_loaded.inc(sp.dma_start(flat(xin[:, tile.slot(4)]), tile_of(x3, tile)), tile, 16)

                def stores(tile):
                    (ln.done if final else out_there).this(sp, tile)
                    store(sp, stored, tile, (h_out, flat(hout[:, tile.slot()])))

                run_tiles(sp, (3, loads), *([(1, skips), (-3, stores)] if final else [(-2, stores)]))
                stored.all(sp)

            @block.tensor
            def _(pe):
                def turns(tile):
                    s = tile.slot(4)
                    loaded.this(pe, tile)
                    a_there.one_back(pe, tile)
                    a_turned.inc(turn(g, turn_ps[:, 0], agg[:, s, :, 0:D]), tile)
                    h_there.one_back(pe, tile)
                    h_turned.inc(turn(g, turn_ps[:, 1], hin[:, s]), tile)

                def products(tile):
                    a_there.this(pe, tile)
                    h_there.this(pe, tile)
                    w_in, a, h = g.w_in[:, step], a_t[:, tile.slot()], h_t[:, tile.slot()]
                    for b, (free, done) in enumerate(((r_there, r_prod), (z_there, z_prod))):
                        free.one_back(pe, tile)
                        nc.tensor.matmul(gate_ps[:, b], w_in[:, b * D:(b + 1) * D], a, start=True, stop=False)
                        done.inc(nc.tensor.matmul(gate_ps[:, b], g.w_hid[:, b * D:(b + 1) * D], h,
                                                  start=False, stop=True), tile)
                    gated_there.one_back(pe, tile)
                    n_prod.inc(nc.tensor.matmul(gate_ps[:, 2], g.w_hid[:, 2 * D:3 * D], h, start=True,
                                                stop=True), tile)
                    pre_there.one_back(pe, tile)
                    i_prod.inc(nc.tensor.matmul(gate_ps[:, 3], w_in[:, 2 * D:3 * D], a, start=True,
                                                stop=True), tile)

                def backs(tile):
                    s = tile.slot()
                    h_new_there.this(pe, tile)
                    out_there.slot_free(pe, tile)
                    for j in range(NJ):
                        last = nc.tensor.transpose(back_ps[:, s, j * D:(j + 1) * D],
                                                   h_new[:, s, j * P:(j + 1) * P], g.ident[:])
                    back.inc(last, tile)

                run_tiles(pe, (1, turns), (0, products), (-1, backs))

            @block.scalar
            def _(act):
                def copies(tile):
                    s = tile.slot()
                    a_turned.this(act, tile)
                    i_prod.slot_free(act, tile)
                    a_there.inc(nc.scalar.copy(a_t[:, s], turn_ps[:, 0]), tile)
                    h_turned.this(act, tile)
                    diff_there.slot_free(act, tile)
                    h_there.inc(nc.scalar.copy(h_t[:, s], turn_ps[:, 1]), tile)

                def gates(tile):
                    s = tile.slot()
                    r_prod.this(act, tile)
                    gated_there.slot_free(act, tile)
                    r_there.inc(nc.scalar.activation(r[:, s], gate_ps[:, 0], ACT.Sigmoid,
                                                     bias=g.b_sum[:, 0:1]), tile)
                    z_prod.this(act, tile)
                    mixed_there.slot_free(act, tile)
                    z_there.inc(nc.scalar.activation(z[:, s], gate_ps[:, 1], ACT.Sigmoid,
                                                     bias=g.b_sum[:, 1:2]), tile)
                    pre_there.this(act, tile)
                    h_new_there.slot_free(act, tile)
                    new_there.inc(nc.scalar.activation(new[:, s], pre[:, s], ACT.Tanh,
                                                       bias=g.b_in[:, 2:3]), tile)

                run_tiles(act, (1, copies), (0, gates))

            @block.vector
            def _(v):
                def gates(tile):
                    s = tile.slot()
                    n_prod.this(v, tile)
                    r_there.this(v, tile)
                    gated_there.inc(nc.vector.scalar_tensor_tensor(
                        gated[:, s], gate_ps[:, 2], g.b_hid[:, 2:3], r[:, s], ALU.add, ALU.mult), tile)
                    i_prod.this(v, tile)
                    gated_there.this(v, tile)
                    new_there.slot_free(v, tile)
                    pre_there.inc(nc.vector.tensor_tensor(pre[:, s], gated[:, s], gate_ps[:, 3], ALU.add), tile)

                def mixes(tile):
                    s = tile.slot()
                    new_there.this(v, tile)
                    h_there.this(v, tile)
                    diff_there.inc(nc.vector.tensor_tensor(diff[:, s], h_t[:, s], new[:, s], ALU.subtract), tile)
                    z_there.this(v, tile)
                    diff_there.this(v, tile)
                    mixed_there.inc(nc.vector.tensor_tensor(mixed[:, s], diff[:, s], z[:, s], ALU.mult), tile)
                    mixed_there.this(v, tile)
                    back.slot_free(v, tile)
                    h_new_there.inc(nc.vector.tensor_tensor(h_new[:, s], mixed[:, s], new[:, s], ALU.add), tile)

                def outs(tile):
                    s = tile.slot()
                    back.this(v, tile)
                    stored.slot_free(v, tile)
                    out_there.inc(nc.vector.tensor_copy(flat(hout[:, s]), back_ps[:, s]), tile)

                def norms(tile):
                    s = tile.slot()
                    back.this(v, tile)
                    x_loaded.this(v, tile)
                    ln.done.slot_free(v, tile)
                    out_there.inc(nc.vector.tensor_tensor(flat(y[:, s]), flat(xin[:, tile.slot(4)]), back_ps[:, s],
                                                          ALU.add), tile)
                    out_there.this(v, tile)
                    ln.moments(v, y, tile)

                def scales(tile):
                    stored.slot_free(v, tile)
                    ln.scale_by_dve(v, hout, y, tile)

                run_tiles(v, (0, gates), *([(-2, scales), (-1, norms)] if final else [(-1, outs)]), (0, mixes))

            if final:
                @block.gpsimd
                def _(pool):
                    run_tiles(pool, (-1, lambda tile: ln.power(pool, tile)))
        for h in (*((ln, x_loaded) if final else ()), loaded, stored, a_turned, h_turned, a_there, h_there, r_prod,
                  z_prod, n_prod, i_prod, r_there, z_there, gated_there, pre_there, new_there, diff_there,
                  mixed_there, h_new_there, back, out_there):
            h.up()


def program(g, a, out):
    constants_pass(g)
    weights_pass(g, a)
    gat_project_pass(g, a["x"])
    sort_pass(g, a["src"], a["dst"], a["edge_weight"])
    g.key_row = g.sb("key_row", [P, EP])
    g.rows = g.dram("rows", [P, CH, D])
    dst, src = Side(g, "dst"), Side(g, "src")
    side_pass(g, dst)
    side_pass(g, src)

    ctx, sb, ps = scope(g)
    with ctx:
        e_sb = sb("gat_exp", [P, CH, HEADS])
        gat_score_pass(g, dst, e_sb)
        edge_pass(g, dst, rows=g.rows, heads=e_sb, out=g.agg_dst, out_width=AW)
    gat_finish_pass(g, a["x"], src, a["edge_attr_128"])

    edge_pass(g, dst, table=g.hid_a, idx=dst.other_i, width=HID, weight=dst.weight, out=g.agg_hid, out_width=HID)
    edge_pass(g, dst, table=g.agg_hid, idx=dst.other_i, width=HID, weight=dst.weight, squash=g.b1[:],
              out=g.agg_hid2, out_width=HID)
    gcn_finish_pass(g, dst, a["edge_attr_128"], src)

    ctx, sb, ps = scope(g)
    with ctx:
        score, top = sb("score", [P, CH]), sb("top", [P, CH])
        for s, table in ((src, g.agg_src), (dst, g.agg_dst)):
            if s is dst:
                key_row_pass(g, s)
            att_score_pass(g, s, score, top)
            att_max_pass(g, s, score, top)
            edge_pass(g, s, rows=s.rows, weight=score, seg_max=top, out=table, out_width=AW)
    att_finish_pass(g)

    h = [g.x3, g.dram("h1", [N, D]), g.dram("h2", [N, D]), out]
    for i in range(3):
        edge_pass(g, dst, table=h[i], idx=dst.other_i, weight=dst.weight, out=g.agg_dst, out_width=AW)
        gru_pass(g, i, h[i], h[i + 1], g.x3 if i == 2 else None)


_INS = ['x', 'src', 'dst', 'edge_attr_128', 'edge_weight', 'L0_gnn_W_proj', 'L0_gnn_W_skip', 'L0_gnn_a_src',
        'L0_gnn_a_tgt', 'L1_gnn_w1', 'L1_gnn_b1', 'L1_gnn_w2', 'L1_gnn_b2', 'L2_gnn_W_att_w', 'L2_gnn_W_att_b',
        'L3_gnn_W', 'L3_gnn_w_ih', 'L3_gnn_w_hh', 'L3_gnn_b_ih', 'L3_gnn_b_hh']


def build(nc, args, out):
    with ExitStack() as ctx:
        program(Net(nc, ctx, args["x"]), args, out)


def kernel(**inputs):
    import numpy as _np
    import concourse.bacc as _bacc
    from concourse import mybir as _mybir
    from concourse.bass_utils import run_bass_kernel_spmd as _run

    nc = _bacc.Bacc("TRN2", target_bir_lowering=False, num_devices=1)
    arrays, args = {}, {}
    for name in _INS:
        a = _np.ascontiguousarray(inputs[name])
        arrays[f"in_{name}_dram"] = a
        args[name] = nc.dram_tensor(f"in_{name}_dram", a.shape, _mybir.dt.from_np(a.dtype), kind="ExternalInput").ap()
    out = nc.dram_tensor("out_0_dram", (N, D), F32, kind="ExternalOutput").ap()
    build(nc, args, out)
    r = _run(nc, [arrays], core_ids=[0])
    return r.results[0]["out_0_dram"]
```

```python
from contextlib import ExitStack, contextmanager

import concourse.bass as bass
from concourse import mybir

F32 = mybir.dt.float32
I32 = mybir.dt.int32
BF16 = mybir.dt.bfloat16
ALU = mybir.AluOpType
ACT = mybir.ActivationFunctionType
AX_X = mybir.AxisListType.X
RMAX = bass.bass_isa.ReduceOp.max

N = 50000
E = 25000
D = 128
HEADS = 8
HF = D // HEADS
HID = 64
P = 128
CH = -(-E // P)
EP = CH * P
SP_P, SP_B = 125, 200
LO = 256
HG = 98
PAD_KEY = 2 * HG * LO - 1
AW = 136
U = 7
GROUPS = CH // U
NJ = 4
NB = P * NJ
TILES = -(-N // NB)
TB = 4
UB = 10
LN_EPS = 1e-5
FAR = -1e30


class Count:

    def __init__(self, sem, kind):
        self.sem, self.base, self.kind = sem, 0, kind

    def up(self, n):
        self.base += n


class Chain:

    def __init__(self, eng, count, per=0):
        self.eng, self.count, self.per = eng, count, per
        self.n, self.iv, self.extra = 0, None, 0

    def start(self, iv):
        self.iv, self.n = iv, 0

    def value(self):
        v = self.count.base + self.extra + self.n
        return v if self.iv is None else self.iv * self.per + v

    def step(self, ins):
        self.n += 1
        ins.then_inc(self.count.sem, 1)
        return ins

    def hold(self):
        self.eng.wait_ge(self.count.sem, self.value())

    def link(self, ins):
        self.step(ins)
        self.hold()

    def loop_done(self, steps):
        assert self.n == self.per, (self.n, self.per)
        self.extra += steps * self.per
        self.n, self.iv = 0, None

    def finish(self):
        self.count.up(self.extra + self.n)


class Net:

    def __init__(self, nc, ctx, some_input):
        self.nc, self.ctx, self.counts, self.passes = nc, ctx, {}, 0
        self.spare = {"": [], "pool_dma": [], "dma": []}
        self.fresh = []
        self.some_input = some_input
        self.raise_buf = self.sb("raise_buf", [P, 64])
        self.passed = ctx.enter_context(nc.semaphore("passed"))

    def sem(self, name, kind=""):
        if name not in self.counts:
            spare = self.spare[kind]
            if not spare:
                spare.append(Count(self.ctx.enter_context(self.nc.semaphore(f"{name}_{self.passes}")), kind))
                self.fresh.append(spare[-1])
            self.counts[name] = spare.pop()
        return self.counts[name]

    @contextmanager
    def block(self):
        fresh, self.fresh, nc = self.fresh, [], self.nc
        if fresh:
            raised = [c for c in fresh if c.kind == ""]
            by_sp = [c for c in fresh if c.kind == "dma"]
            by_pool = [c for c in fresh if c.kind == "pool_dma"]

            def few_bytes(eng, counts, row):
                for n, c in enumerate(counts):
                    eng.dma_start(self.raise_buf[row:row + 1, n:n + 1],
                                  self.some_input[0:1, 0:1]).then_inc(c.sem, 16)
                for c in counts:
                    eng.wait_ge(c.sem, 16)
                    c.base += 16

            with nc.Block() as block:
                @block.sync
                def _(sp):
                    few_bytes(sp, by_sp, 0)

                @block.gpsimd
                def _(pool):
                    for c in raised:
                        pool.sem_inc(c.sem, 1)
                        c.base += 1
                    few_bytes(pool, by_pool, 32)
        with nc.Block() as block:
            yield block

    def end_of_pass(self):
        for count in self.counts.values():
            self.spare[count.kind].append(count)
        self.counts = {}

    def sb(self, name, shape, dt=F32):
        return self.ctx.enter_context(self.nc.sbuf_tensor(name, shape, dt))

    def dram(self, name, shape, dt=F32):
        return self.nc.dram_tensor(name, shape, dt, kind="Internal").ap()


def scope(g):
    nc, ctx = g.nc, ExitStack()
    g.end_of_pass()
    g.passes += 1
    of = f"pass{g.passes}_"

    def sb(name, shape, dt=F32):
        return ctx.enter_context(nc.sbuf_tensor(of + name, shape, dt))

    def ps(name, shape, dt=F32):
        return ctx.enter_context(nc.psum_tensor(of + name, shape, dt))

    return ctx, sb, ps


def gate(g, eng):
    eng.sem_inc(g.passed, 1)


def bcast(row, parts):
    return row.rearrange("(a n) -> a n", a=1).partition_broadcast(parts)


def constants_pass(g):
    nc = g.nc
    made = g.sem("consts_made")
    g.ident = g.sb("ident", [P, P])
    g.iota_lo = g.sb("iota_lo", [P, LO], BF16)
    g.iota_hi = g.sb("iota_hi", [P, 2 * HG], BF16)
    g.iota_p = g.sb("iota_p", [P, 2])
    g.earlier = g.sb("earlier", [P, P])
    g.zero = g.sb("zero", [P, 4 * AW])
    with g.block() as block:
        @block.gpsimd
        def _(pool):
            nc.gpsimd.memset(g.ident[:], 0.0).then_inc(made.sem, 1)
            nc.gpsimd.memset(g.earlier[:], 1.0).then_inc(made.sem, 1)
            nc.gpsimd.memset(g.zero[:], 0.0).then_inc(made.sem, 1)
            nc.gpsimd.iota(g.iota_lo[:], [[1, LO]], base=0, channel_multiplier=0,
                           allow_small_or_imprecise_dtypes=True).then_inc(made.sem, 1)
            nc.gpsimd.iota(g.iota_hi[:], [[1, 2 * HG]], base=0, channel_multiplier=0,
                           allow_small_or_imprecise_dtypes=True).then_inc(made.sem, 1)
            nc.gpsimd.iota(g.iota_p[:], [[HG, 2]], base=0, channel_multiplier=1,
                           allow_small_or_imprecise_dtypes=True).then_inc(made.sem, 1)
            pool.wait_ge(made.sem, made.base + 6)
            nc.gpsimd.affine_select(out=g.ident[:], in_=g.ident[:], compare_op=ALU.not_equal, fill=1.0,
                                    base=0, pattern=[[-1, P]], channel_multiplier=1).then_inc(made.sem, 1)
            nc.gpsimd.affine_select(out=g.earlier[:], in_=g.earlier[:], compare_op=ALU.is_gt, fill=0.0,
                                    base=0, pattern=[[-1, P]], channel_multiplier=1).then_inc(made.sem, 1)
            pool.wait_ge(made.sem, made.base + 8)
    made.up(8)


def sort_pass(g, src, dst, weight):
    nc = g.nc
    KEYS = ("dst", "src")
    column = (1, 0)
    g.rec = {k: g.dram(f"rec_{k}", [EP, 4]) for k in KEYS}
    g.agg_dst = g.dram("agg_dst", [N, AW])
    g.agg_src = g.dram("agg_src", [N, AW])
    g.agg_hid = g.dram("agg_hid", [N, HID])
    g.agg_hid2 = g.dram("agg_hid2", [N, HID])
    HB = SP_B // 2
    steps = SP_B // UB // 2
    zero_rows = N // (2 * steps)
    zero_parts = zero_rows // (4 * SP_P)
    ctx, sb, ps = scope(g)
    with ctx:
        ints = sb("ints", [HB, 2, 2, SP_P], I32)
        by_block = sb("by_block", [HB, 3, 2, SP_P])
        rec = sb("rec", [SP_P, SP_B, 4])
        key_i = sb("key_i", [SP_P, 2, SP_B], I32)
        hi_i = sb("hi_i", [SP_P, 2, SP_B], I32)
        lo_i = sb("lo_i", [SP_P, 2, SP_B], I32)
        hi_f = sb("hi_f", [SP_P, 2, SP_B])
        lo_f = sb("lo_f", [SP_P, 2, SP_B])
        key_f = sb("key_f", [SP_P, 2, SP_B])
        row = sb("row", [SP_P, 2, 2, UB, SP_P], I32)
        oh_lo = sb("oh_lo", [SP_P, 2, 2, UB, LO], BF16)
        oh_hi = sb("oh_hi", [SP_P, 2, 2, UB, 2 * HG], BF16)
        hi_t = sb("hi_t", [HG, 2, UB, SP_P], I32)
        oh_t = sb("oh_t", [HG, 2, 2, UB, 2, SP_P])
        junk_eq = sb("junk_eq", [SP_P, 2, 2, UB, SP_P], BF16)
        junk_lo = sb("junk_lo", [SP_P, 2, 2, UB, LO], BF16)
        rank = sb("rank", [SP_P, 2, 2, 2, UB])
        pos = sb("pos", [SP_P, 2, 2, UB])
        pos_i = sb("pos_i", [SP_P, 2, 2, UB], I32)
        low_i = sb("low_i", [SP_P, 2, 2, UB], I32)
        high_i = sb("high_i", [SP_P, 2, 2, UB], I32)
        place = sb("place", [SP_P, 2, 2, UB], I32)
        rec_stage = sb("rec_stage", [SP_P, 2, UB, 4])
        hist = sb("hist", [HG, 2, 2, LO])
        scan = sb("scan", [HG, 2, 2, LO])
        tot = sb("tot", [HG, 2, 4])
        ones = sb("ones", [HG, HG])
        later = sb("later", [HG, HG])
        hist_sb = sb("hist_sb", [HG, 2, 2, 2 * LO])
        pad = sb("pad", [88, 2, 4])
        h_ps = ps("h_ps", [HG, 2, 2 * LO])
        look_ps = ps("look_ps", [SP_P, 2, 2, 512])
        off_ps = ps("off_ps", [HG, 2, 512])
        loaded, dve, prep = g.sem("sort_loaded", "dma"), g.sem("sort_dve"), g.sem("sort_prep")
        padded, numbered, summed = g.sem("sort_padded", "dma"), g.sem("sort_numbered"), g.sem("sort_summed")
        turned = g.sem("sort_turned")

        def of_both(name, kind=""):
            return [[g.sem(f"{name}_{key}{h}", kind) for h in range(2)] for key in KEYS]

        looked, ranked, placed, onehots, counted = [of_both(n) for n in (
            "sort_looked", "sort_ranked", "sort_placed", "sort_onehots", "sort_counted")]
        scattered = of_both("sort_scattered", "pool_dma")
        snap, counted_b = [[g.sem(f"{n}_{key}") for key in KEYS] for n in ("sort_snapped", "sort_counted_block")]
        rows_there = Halves(g, "sort_rows", 16 * 2)
        rows_used, pos_there, split_there, low_there, *spread = all_halves(
            g, "sort_rows_used", "sort_position", "sort_position_split", "sort_position_low", "sort_hi_dst",
            "sort_hi_src")
        zeroed = Halves(g, "sort_zeroed", 16 * 4 * zero_parts)

        with g.block() as block:
            @block.sync
            def _(sp):
                v = lambda a: a.rearrange("(h b p) -> b h p", h=2, b=HB)
                sp.dma_start(ints[:, 0], v(src)).then_inc(loaded.sem, 16)
                sp.dma_start(ints[:, 1], v(dst)).then_inc(loaded.sem, 16)
                sp.dma_start(by_block[:, 2], v(weight)).then_inc(loaded.sem, 16)
                sp.wait_ge(prep.sem, prep.base + 1)
                for k, key in enumerate(KEYS):
                    sp.dma_start(g.rec[key].rearrange("(q c) k -> q c k", c=CH)[0:88, CH - 1, :],
                                 pad[:, k, :]).then_inc(padded.sem, 16)
                sp.wait_ge(padded.sem, padded.base + 32)

            @block.vector
            def _(v):
                ch = Chain(v, dve)
                ch.step(nc.vector.memset(ones[:], 1.0))
                ch.step(nc.vector.memset(pad[:], 0.0))
                ch.link(nc.vector.tensor_scalar(later[:], g.earlier[0:HG, 0:HG], -1.0, 1.0, ALU.mult, ALU.add))
                ch.step(nc.vector.tensor_tensor(later[:], later[:], g.ident[0:HG, 0:HG], ALU.subtract))
                for k in range(2):
                    last = nc.vector.memset(pad[:, k, column[k]:column[k] + 1], float(PAD_KEY))
                last.then_inc(prep.sem, 1)
                v.wait_ge(loaded.sem, loaded.base + 48)
                nc.vector.tensor_copy(by_block[:, 0:2], ints[:]).then_inc(prep.sem, 1)
                v.wait_ge(turned.sem, turned.base + 1)
                for a in range(3):
                    ch.step(nc.vector.tensor_copy(rec[:, :, a], look_ps[:, a // 2, a % 2, 0:SP_B]))
                for k in range(2):
                    keys = look_ps[:, column[k] // 2, column[k] % 2, 0:SP_B]
                    ch.step(nc.vector.tensor_copy(key_i[:, k, :], keys))
                    ch.link(nc.vector.tensor_copy(key_f[:, k, :], keys))
                ch.step(nc.vector.tensor_scalar(hi_i[:], key_i[:], 8, None, ALU.logical_shift_right))
                ch.link(nc.vector.tensor_scalar(lo_i[:], key_i[:], LO - 1, None, ALU.bitwise_and))
                ch.step(nc.vector.tensor_copy(hi_f[:], hi_i[:]))
                ch.link(nc.vector.tensor_copy(lo_f[:], lo_i[:]))
                ch.finish()

            @block.tensor
            def _(pe):
                pe.wait_ge(prep.sem, prep.base + 2)
                for a in range(3):
                    for h in range(2):
                        last = nc.tensor.transpose(look_ps[:, a // 2, a % 2, h * HB:(h + 1) * HB],
                                                   by_block[:, a, h, :], g.ident[0:HB, 0:HB])
                last.then_inc(turned.sem, 1)

            @block.gpsimd
            def _(pool):
                nc.gpsimd.iota(rec[:, :, 3], [[SP_P, SP_B]], base=0, channel_multiplier=1,
                               allow_small_or_imprecise_dtypes=True).then_inc(numbered.sem, 1)
                pool.wait_ge(numbered.sem, numbered.base + 1)
        loaded.up(48)
        padded.up(32)
        prep.up(2)
        numbered.up(1)
        turned.up(1)

        def onehots_of(k, par, b, i):
            nc.vector.tensor_scalar(oh_lo[:, k, par, b, :], g.iota_lo[0:SP_P, :],
                                    lo_f[:, k, bass.ds(i, 1)], None, ALU.is_equal)
            return nc.vector.tensor_scalar(oh_hi[:, k, par, b, :], g.iota_hi[0:SP_P, :],
                                           hi_f[:, k, bass.ds(i, 1)], None, ALU.is_equal)

        def count(k, par, b):
            for h in range(2):
                last = nc.tensor.matmul(h_ps[:, k, h * LO:(h + 1) * LO], oh_hi[:, k, par, b, h * HG:(h + 1) * HG],
                                        oh_lo[:, k, par, b, :], start=False, stop=True, skip_group_check=True)
            return last

        with g.block() as block:
            @block.vector
            def _(v):
                with v.Fori(0, steps) as it:
                    for par in range(2):
                        for k in range(2):
                            v.wait_ge(counted[k][par].sem, it + counted[k][par].base)
                            for b in range(UB):
                                last = onehots_of(k, par, b, it * (2 * UB) + (par * UB + b))
                            last.then_inc(onehots[k][par].sem, 1)

            @block.tensor
            def _(pe):
                for k in range(2):
                    nc.tensor.matmul(h_ps[:, k, :], g.zero[:, 0:HG], g.zero[:, 0:2 * LO], start=True, stop=True)
                with pe.Fori(0, steps) as it:
                    for par in range(2):
                        for k in range(2):
                            pe.wait_ge(onehots[k][par].sem, it + (onehots[k][par].base + 1))
                            for b in range(UB):
                                last = count(k, par, b)
                            last.then_inc(counted[k][par].sem, 1)
        for k in range(2):
            for h in range(2):
                onehots[k][h].up(steps)
                counted[k][h].up(steps)

        with g.block() as block:
            @block.vector
            def _(v):
                ch = Chain(v, dve)
                ch.step(nc.vector.memset(tot[:], 0.0))
                ch.link(nc.vector.tensor_copy(hist[:].rearrange("p k a b -> p (k a b)"),
                                              h_ps[:].rearrange("p k b -> p (k b)")))
                for k in range(2):
                    for h in range(2):
                        ch.step(nc.vector.tensor_tensor_scan(scan[:, k, h, :], hist[:, k, h, :],
                                                             g.zero[0:HG, 0:LO], 0.0, ALU.add, ALU.add))
                ch.hold()
                for k in range(2):
                    ch.step(nc.vector.tensor_copy(tot[:, k, 0:2], scan[:, k, :, LO - 1]))
                    ch.step(nc.vector.tensor_copy(tot[:, k, 3:4], scan[:, k, 0, LO - 1:LO]))
                ch.link(nc.vector.tensor_tensor(hist[:], scan[:], hist[:], ALU.subtract))
                ch.finish()
        with g.block() as block:
            @block.tensor
            def _(pe):
                for k in range(2):
                    nc.tensor.matmul(off_ps[:, k, 0:2], later[:], tot[:, k, 0:2], start=True, stop=False)
                    nc.tensor.matmul(off_ps[:, k, 0:2], ones[:], tot[:, k, 2:4], start=False,
                                     stop=True).then_inc(summed.sem, 1)
                pe.wait_ge(summed.sem, summed.base + 6)
                for k in range(2):
                    nc.tensor.matmul(h_ps[:, k, :], g.ident[0:HG, 0:HG],
                                     hist[:, k].rearrange("p a b -> p (a b)"), start=True,
                                     stop=True).then_inc(summed.sem, 1)
                pe.wait_ge(summed.sem, summed.base + 8)

            @block.vector
            def _(v):
                v.wait_ge(summed.sem, summed.base + 2)
                for k in range(2):
                    for h in range(2):
                        nc.vector.tensor_scalar(hist[:, k, h, :], hist[:, k, h, :], off_ps[:, k, h:h + 1], None,
                                                ALU.add).then_inc(summed.sem, 1)
        summed.up(8)

        with g.block() as block:
            @block.sync
            def _(sp):
                with sp.Fori(0, steps) as it:
                    for par in range(2):
                        rows_used.two_back(sp, par, it)
                        for k, keys in enumerate((dst, src)):
                            edges = keys[bass.ds(it * (2 * UB * SP_P) + par * UB * SP_P, UB * SP_P)]
                            sp.dma_start(
                                row[:, par, k].rearrange("p b a -> p (b a)"),
                                bcast(edges, SP_P)).then_inc(rows_there.c[par].sem, 16)
                        zeroed.two_back(sp, par, it)
                        for table, width in ((g.agg_dst, AW), (g.agg_src, AW), (g.agg_hid, HID), (g.agg_hid2, HID)):
                            for n in range(zero_parts):
                                first = it * (2 * zero_rows) + par * zero_rows + n * 4 * SP_P
                                sp.dma_start(table[bass.ds(first, 4 * SP_P), :].rearrange("(p j) w -> p (j w)", j=4),
                                             g.zero[0:SP_P, 0:4 * width]).then_inc(zeroed.c[par].sem, 16)
                for par in range(2):
                    zeroed.two_back(sp, par, steps)

            @block.scalar
            def _(act):
                with act.Fori(0, HB) as it:
                    for p2 in range(2):
                        for k in range(2):
                            act.wait_ge(counted_b[k].sem, it * 2 + (counted_b[k].base + p2))
                            act.wait_ge(looked[k][p2].sem, it + looked[k][p2].base)
                            nc.scalar.copy(hist_sb[:, k, p2, :], h_ps[:, k, :]).then_inc(snap[k].sem, 1)

            @block.tensor
            def _(pe):
                with pe.Fori(0, steps) as it:
                    for par in range(2):
                        for k in range(2):
                            pe.wait_ge(onehots[k][par].sem, it + (onehots[k][par].base + 1))
                        for b in range(UB):
                            n = par * UB + b
                            p2 = b % 2
                            for k in range(2):
                                pe.wait_ge(snap[k].sem, it * (2 * UB) + (snap[k].base + n + 1))
                                count(k, par, b).then_inc(counted_b[k].sem, 1)
                            for k in range(2):
                                pe.wait_ge(ranked[k][p2].sem, it * UB + (ranked[k][p2].base + n // 2))
                                for h in range(2):
                                    last = nc.tensor.matmul(look_ps[:, k, p2, 0:LO], oh_t[:, k, par, b, h, :],
                                                            hist_sb[:, k, p2, h * LO:(h + 1) * LO],
                                                            start=(h == 0), stop=(h == 1))
                                last.then_inc(looked[k][p2].sem, 1)

            @block.vector
            def _(v):
                def spread_hi(k, par, it, first_step):
                    if not first_step:
                        for p2 in range(2):
                            v.wait_ge(looked[k][p2].sem, it * UB + (looked[k][p2].base + (par - 1) * UB // 2))
                    spread[k].inc(nc.vector.tensor_scalar(hi_t[:, k], row[0:HG, par, k], 8, None,
                                                          ALU.logical_shift_right), par)
                    spread[k].this(v, par, it)
                    for h in range(2):
                        nc.vector.tensor_scalar(oh_t[:, k, par, :, h, :], hi_t[:, k], g.iota_p[0:HG, h:h + 1],
                                                None, ALU.is_equal)

                def prepare(b, par, it, first_step=False):
                    if b == 0:
                        rows_there.this(v, par, it)
                    if b % (UB // 2) == 0:
                        spread_hi(b // (UB // 2), par, it, first_step)
                    i = it * (2 * UB) + (par * UB + b)
                    for k in range(2):
                        last = nc.vector.scalar_tensor_tensor(
                            junk_eq[:, k, par, b, :], row[:, par, k, b, :], key_f[:, k, bass.ds(i, 1)],
                            g.earlier[0:SP_P, 0:SP_P], ALU.is_equal, ALU.mult,
                            accum_out=rank[:, k, par, 0, b:b + 1])
                    if b == UB - 1:
                        rows_used.inc(last, par)
                    for k in range(2):
                        last = onehots_of(k, par, b, i)
                        if b == UB - 1:
                            last.then_inc(onehots[k][par].sem, 1)

                def look_up(b, par, it):
                    p2 = b % 2
                    for k in range(2):
                        v.wait_ge(looked[k][p2].sem, it * UB + (looked[k][p2].base + (par * UB + b) // 2 + 1))
                        nc.vector.scalar_tensor_tensor(
                            junk_lo[:, k, par, b, :], g.iota_lo[0:SP_P, :],
                            lo_f[:, k, bass.ds(it * (2 * UB) + (par * UB + b), 1)],
                            look_ps[:, k, p2, 0:LO], ALU.is_equal, ALU.mult,
                            accum_out=rank[:, k, par, 1, b:b + 1]).then_inc(ranked[k][p2].sem, 1)

                def places(par, it):
                    for k in range(2):
                        for p2 in range(2):
                            v.wait_ge(ranked[k][p2].sem, it * UB + (ranked[k][p2].base + (par + 1) * UB // 2))
                        v.wait_ge(scattered[k][par].sem, it * (16 * UB) + scattered[k][par].base)
                    nc.vector.tensor_copy(rec_stage[:, par], rec[:, bass.ds(it * (2 * UB) + par * UB, UB), :])
                    pos_there.inc(nc.vector.tensor_tensor(pos_i[:, :, par, :], rank[:, :, par, 0, :],
                                                          rank[:, :, par, 1, :], ALU.add), par)
                    pos_there.this(v, par, it)
                    nc.vector.tensor_scalar(low_i[:, :, par, :], pos_i[:, :, par, :], P - 1, None, ALU.bitwise_and)
                    split_there.inc(nc.vector.tensor_scalar(high_i[:, :, par, :], pos_i[:, :, par, :], 7, None,
                                                            ALU.logical_shift_right), par)
                    split_there.this(v, par, it)
                    low_there.inc(nc.vector.tensor_scalar(pos[:, :, par, :], low_i[:, :, par, :], -float(CH),
                                                          float((P - 1) * CH), ALU.mult, ALU.add), par)
                    low_there.this(v, par, it)
                    for k in range(2):
                        nc.vector.tensor_tensor(place[:, k, par, :], pos[:, k, par, :], high_i[:, k, par, :],
                                                ALU.add).then_inc(placed[k][par].sem, 1)

                for b in range(UB):
                    prepare(b, 0, 0, first_step=True)
                with v.Fori(0, steps - 1) as it:
                    for par in range(2):
                        for b in range(UB):
                            prepare(b, 1 - par, it + par)
                            look_up(b, par, it)
                        places(par, it)
                for b in range(UB):
                    prepare(b, 1, steps - 1)
                    look_up(b, 0, steps - 1)
                places(0, steps - 1)
                for b in range(UB):
                    look_up(b, 1, steps - 1)
                places(1, steps - 1)

            @block.gpsimd
            def _(pool):
                bound = pool.to_reg(EP - 1)
                with pool.Fori(0, steps) as it:
                    for par in range(2):
                        for k, key in enumerate(KEYS):
                            pool.wait_ge(placed[k][par].sem, it + (placed[k][par].base + 1))
                            gate(g, pool)
                            for b in range(UB):
                                pool.indirect_dma_start(
                                    out=g.rec[key],
                                    out_offset=bass.IndirectOffsetOnAxis(ap=place[:, k, par, b:b + 1], axis=0),
                                    in_=rec_stage[:, par, b, :], in_offset=None, bounds_check=bound,
                                    oob_is_err=False).then_inc(scattered[k][par].sem, 16)
                for k in range(2):
                    for par in range(2):
                        pool.wait_ge(scattered[k][par].sem, scattered[k][par].base + 16 * HB)
        for h in (rows_there, rows_used, zeroed, pos_there, split_there, low_there, *spread):
            h.up(steps)
        for k in range(2):
            snap[k].up(SP_B)
            counted_b[k].up(SP_B)
            for h in range(2):
                onehots[k][h].up(steps)
                looked[k][h].up(HB)
                ranked[k][h].up(HB)
                placed[k][h].up(steps)
                scattered[k][h].up(16 * HB)


class Halves:

    def __init__(self, g, name, k=1, by_pool=False):
        kind = "" if k % 16 else ("pool_dma" if by_pool else "dma")
        self.c = [g.sem(f"{name}{h}", kind) for h in range(2)]
        self.g, self.k = g, k

    def wait(self, eng, half, value):
        eng.wait_ge(self.c[half].sem, value)
        if eng in (self.g.nc.gpsimd, self.g.nc.sync):
            gate(self.g, eng)

    def inc(self, ins, half):
        return ins.then_inc(self.c[half].sem, self.k)

    def this(self, eng, half, it):
        self.wait(eng, half, it * self.k + (self.c[half].base + self.k))

    def part(self, eng, half, it, n):
        self.wait(eng, half, it * self.k + (self.c[half].base + n))

    def two_back(self, eng, half, it):
        self.wait(eng, half, it * self.k + self.c[half].base)

    def one_back(self, eng, half, it):
        self.wait(eng, 1 - half, it * self.k + (self.c[1 - half].base + self.k * half))

    def up(self, tiles):
        for c in self.c:
            c.up(self.k * tiles)


def all_halves(g, *names, k=1):
    return [Halves(g, n, k) for n in names]


class Side:

    def __init__(self, g, name):
        self.name = name
        self.rec = g.rec[name]
        self.key = g.sb(f"{name}_key", [P, CH])
        self.weight = g.sb(f"{name}_weight", [P, CH])
        self.before = g.sb(f"{name}_before", [1, CH])
        self.other_i = g.sb(f"{name}_other_i", [P, CH], I32)
        self.edge_i = g.sb(f"{name}_edge_i", [P, CH], I32)
        self.key_i = g.sb(f"{name}_key_i", [P, CH], I32)
        self.last_i = g.sb(f"{name}_last_i", [P, CH], I32)
        self.key_d = g.dram(f"{name}_key_d", [P, CH])
        self.rows = g.dram(f"{name}_rows", [P, CH, D])


def side_pass(g, s):
    nc = g.nc
    kc = 1 if s.name == "dst" else 0
    ctx, sb, ps = scope(g)
    with ctx:
        rec = sb("side_rec", [P, CH, 4])
        after = sb("side_after", [P, CH])
        tmp = sb("side_tmp", [P, CH])
        tmp2 = sb("side_tmp2", [P, CH])
        loaded, dve, keyed, wrote = g.sem("side_loaded", "dma"), g.sem("side_dve"), g.sem("side_keyed"), g.sem("side_wrote", "dma")
        shifted = g.sem("side_shifted", "dma")
        with g.block() as block:
            @block.sync
            def _(sp):
                sp.dma_start(rec[:], s.rec.rearrange("(q c) k -> q c k", c=CH)).then_inc(loaded.sem, 16)
                sp.wait_ge(keyed.sem, keyed.base + 1)
                sp.dma_start(s.key_d, s.key[:]).then_inc(wrote.sem, 16)
                sp.wait_ge(wrote.sem, wrote.base + 16)
                sp.dma_start(after[1:P, :], s.key_d[0:P - 1, :]).then_inc(shifted.sem, 16)
                sp.dma_start(after[0:1, 0:CH - 1], s.key_d[P - 1:P, 1:CH]).then_inc(shifted.sem, 16)
                sp.dma_start(s.before[0:1, 1:CH], s.key_d[0:1, 0:CH - 1]).then_inc(shifted.sem, 16)
                sp.wait_ge(shifted.sem, shifted.base + 48)

            @block.vector
            def _(v):
                ch = Chain(v, dve)
                ch.step(nc.vector.memset(after[0:1, CH - 1:CH], -1.0))
                ch.step(nc.vector.memset(s.before[0:1, 0:1], -1.0))
                v.wait_ge(loaded.sem, loaded.base + 16)
                nc.vector.tensor_copy(s.key[:], rec[:, :, kc]).then_inc(keyed.sem, 1)
                ch.step(nc.vector.tensor_copy(s.weight[:], rec[:, :, 2]))
                ch.step(nc.vector.tensor_copy(s.other_i[:], rec[:, :, 0]))
                ch.step(nc.vector.tensor_copy(s.edge_i[:], rec[:, :, 3]))
                v.wait_ge(keyed.sem, keyed.base + 1)
                ch.step(nc.vector.tensor_scalar(s.key_i[:], s.key[:], float(N - 1), None, ALU.min))
                v.wait_ge(shifted.sem, shifted.base + 48)
                ch.link(nc.vector.tensor_tensor(tmp[:], s.key[:], after[:], ALU.is_equal))
                ch.link(nc.vector.tensor_scalar(tmp2[:], tmp[:], float(4 * N), None, ALU.mult))
                ch.link(nc.vector.tensor_tensor(s.last_i[:], tmp2[:], s.key[:], ALU.add))
                ch.finish()
        loaded.up(16)
        keyed.up(1)
        wrote.up(16)
        shifted.up(48)


def load_key_row(g, eng, s, loaded):
    eng.dma_start(g.key_row[:], bcast(s.key_d.rearrange("q c -> (q c)"), P)).then_inc(loaded.sem, 16)


def key_row_pass(g, s):
    loaded = g.sem("key_row_loaded", "dma")
    with g.block() as block:
        @block.sync
        def _(sp):
            load_key_row(g, sp, s, loaded)
            sp.wait_ge(loaded.sem, loaded.base + 16)
    loaded.up(16)


def chunk_keys(g, c, parts=slice(0, P)):
    return g.key_row[parts, :].rearrange("p (q c) -> p c q", c=CH)[:, bass.ds(c, 1), :].rearrange("p a q -> p (a q)")


def group_keys(g, c, parts=slice(0, P)):
    return g.key_row[parts, :].rearrange("p (q c) -> p c q", c=CH)[:, bass.ds(c, U), :]


class Stage:

    def __init__(self, g, sb, name):
        self.buf = sb(f"stage_{name}", [P, 2, U], I32)
        self.there = Halves(g, f"staged_{name}", 16)

    def load(self, sp, idx, half, it):
        self.there.inc(sp.dma_start(self.buf[:, half, :], idx[:, bass.ds(it * (2 * U) + half * U, U)]), half)


def gather(pool, stage, table, out, half):
    for u in range(U):
        last = pool.indirect_dma_start(out=out(u), out_offset=None, in_=table,
                                       in_offset=bass.IndirectOffsetOnAxis(ap=stage.buf[:, half, u:u + 1], axis=0))
        yield last


STEPS = GROUPS // 2


def edge_pass(g, s, table=None, idx=None, rows=None, width=D, weight=None, heads=None, seg_max=None,
              squash=None, out=None, out_width=None):
    nc = g.nc
    wide = D + HEADS if heads is not None else (D + 1 if seg_max is not None else width)
    ctx, sb, ps = scope(g)
    with ctx:
        rowbuf = sb("rowbuf", [P, 2, U, AW])
        same = sb("same", [P, 2, U, P])
        carry = sb("carry", [1, 2, U, P])
        sums = sb("sums", [P, 2, U, out_width])
        made = heads is not None or squash is not None
        scaled = sb("scaled", [P, 2, U, AW]) if made else rowbuf
        pre = sb("pre", [P, 2, U, width]) if squash is not None else None
        sum_ps = ps("sum_ps", [P, U, 512])
        st_in = Stage(g, sb, "gather")
        st_out = Stage(g, sb, "scatter")
        got = Halves(g, "edge_rows", 16 * U if rows is None else 16, by_pool=rows is None)
        put = Halves(g, "edge_put", 16 * U, by_pool=True)
        matrices, = all_halves(g, "edge_matrices")
        biased, squashed = all_halves(g, "edge_biased", "edge_squashed") if squash is not None else (None, None)
        used, copied = all_halves(g, "edge_used", "edge_copied", k=U)
        cleared, dve = g.sem("edge_cleared"), g.sem("edge_dve")

        with g.block() as block:
            @block.vector
            def _(v):
                nc.vector.memset(sums[:], 0.0).then_inc(cleared.sem, 1)
                nc.vector.memset(rowbuf[:], 1.0).then_inc(cleared.sem, 1)
                v.wait_ge(cleared.sem, cleared.base + 2)
        cleared.up(2)

        with g.block() as block:
            @block.sync
            def _(sp):
                with sp.Fori(0, STEPS) as it:
                    for half in range(2):
                        if rows is None:
                            got.two_back(sp, half, it)
                            st_in.load(sp, idx, half, it)
                        else:
                            used.two_back(sp, half, it)
                            got.inc(sp.dma_start(rowbuf[:, half, :, 0:D],
                                                 rows[:, bass.ds(it * (2 * U) + half * U, U), :]),
                                    half)
                        put.two_back(sp, half, it)
                        st_out.load(sp, s.last_i, half, it)

            @block.gpsimd
            def _(pool):
                bound = pool.to_reg(N - 1)

                def gathers(half, it):
                    st_in.there.this(pool, half, it)
                    used.two_back(pool, half, it)
                    for ins in gather(pool, st_in, table, lambda u: rowbuf[:, half, u, 0:width], half):
                        ins.then_inc(got.c[half].sem, 16)

                def scatters(half, it):
                    st_out.there.this(pool, half, it)
                    copied.this(pool, half, it)
                    if seg_max is not None:
                        matrices.this(pool, half, it)
                    for u in range(U):
                        pool.indirect_dma_start(
                            out=out, out_offset=bass.IndirectOffsetOnAxis(ap=st_out.buf[:, half, u:u + 1], axis=0),
                            in_=sums[:, half, u, :], in_offset=None, bounds_check=bound,
                            oob_is_err=False).then_inc(put.c[half].sem, 16)

                if rows is None:
                    gathers(0, 0)
                with pool.Fori(0, STEPS - 1) as it:
                    for half in range(2):
                        if rows is None:
                            gathers(1 - half, it + half)
                        scatters(half, it)
                if rows is None:
                    gathers(1, STEPS - 1)
                scatters(0, STEPS - 1)
                scatters(1, STEPS - 1)
                for half in range(2):
                    put.two_back(pool, half, STEPS)

            @block.vector
            def _(v):
                with v.Fori(0, STEPS) as it:
                    for half in range(2):
                        first = it * (2 * U) + half * U
                        used.two_back(v, half, it)
                        for u in range(U):
                            args = (None, ALU.is_equal) if weight is None else \
                                (weight[:, bass.ds(first + u, 1)], ALU.is_equal, ALU.mult)
                            nc.vector.tensor_scalar(same[:, half, u, :], chunk_keys(g, first + u),
                                                    s.key[:, bass.ds(first + u, 1)], *args)
                        if seg_max is not None:
                            put.two_back(v, half, it)
                            nc.vector.tensor_copy(sums[:, half, :, D + 1], seg_max[:, bass.ds(first, U)])
                        if squash is not None:
                            got.this(v, half, it)
                            squashed.two_back(v, half, it)
                            biased.inc(nc.vector.tensor_tensor(
                                pre[:, half], rowbuf[:, half, :, 0:width],
                                squash.unsqueeze(1).to_broadcast([P, U, width]), ALU.add), half)
                        if heads is not None:
                            got.this(v, half, it)
                            exps = heads[:, bass.ds(first, U), :]
                            for u in range(U):
                                nc.vector.tensor_tensor(
                                    scaled[:, half, u, 0:D].rearrange("p (h f) -> p h f", f=HF),
                                    rowbuf[:, half, u, 0:D].rearrange("p (h f) -> p h f", f=HF),
                                    heads[:, bass.ds(first + u, 1), :].rearrange("p a h -> p (a h)")
                                    .unsqueeze(2).to_broadcast([P, HEADS, HF]), ALU.mult)
                            nc.vector.tensor_copy(scaled[:, half, :, D:D + HEADS], exps)
                        matrices.inc(nc.vector.tensor_tensor(
                            carry[0:1, half, :, :], group_keys(g, first, slice(0, 1)),
                            s.before[0:1, bass.ds(first, U)].unsqueeze(2).to_broadcast([1, U, P]),
                            ALU.is_equal), half)

            @block.tensor
            def _(pe):
                with pe.Fori(0, STEPS) as it:
                    for half in range(2):
                        matrices.this(pe, half, it)
                        if squash is not None:
                            squashed.this(pe, half, it)
                        elif heads is None:
                            got.this(pe, half, it)

                        def product(u):
                            nc.tensor.matmul(sum_ps[:, u, 0:wide], same[:, half, u, :],
                                             scaled[:, half, u, 0:wide], start=True, stop=False)

                        product(0)
                        for u in range(U):
                            if u + 1 < U:
                                product(u + 1)
                            if u:
                                copied.part(pe, half, it, u)
                            else:
                                copied.one_back(pe, half, it)
                            prev = sums[0:1, half, u - 1, 0:wide] if u else sums[0:1, 1 - half, U - 1, 0:wide]
                            ins = nc.tensor.matmul(sum_ps[:, u, 0:wide], carry[0:1, half, u, :], prev,
                                                   start=False, stop=True)
                            ins.then_inc(used.c[half].sem, 1)

            @block.scalar
            def _(act):
                with act.Fori(0, STEPS) as it:
                    for half in range(2):
                        if squash is not None:
                            biased.this(act, half, it)
                            used.two_back(act, half, it)
                            squashed.inc(nc.scalar.activation(scaled[:, half, :, 0:width], pre[:, half],
                                                              ACT.Sigmoid), half)
                        put.two_back(act, half, it)
                        for u in range(U):
                            used.part(act, half, it, u + 1)
                            ins = nc.scalar.copy(sums[:, half, u, 0:wide], sum_ps[:, u, 0:wide])
                            ins.then_inc(copied.c[half].sem, 1)
        if rows is None:
            st_in.there.up(STEPS)
        st_out.there.up(STEPS)
        for h in (got, put, matrices, used, copied, *((biased, squashed) if squash is not None else ())):
            h.up(STEPS)


def weights_pass(g, a):
    nc = g.nc
    g.w_proj = g.sb("w_proj", [P, D + 2 * HEADS])
    g.w_skip = g.sb("w_skip", [P, D])
    g.w1 = g.sb("w1", [P, HID])
    g.w2 = g.sb("w2", [HID + 1, D])
    g.b1 = g.sb("b1", [P, HID])
    g.att = g.sb("att", [P, 2 * D])
    g.att_b = g.sb("att_b", [P, 1])
    g.w_in = g.sb("w_in", [P, 3, 3 * D])
    g.w_hid = g.sb("w_hid", [P, 3 * D])
    g.b_in = g.sb("b_in", [P, 3])
    g.b_hid = g.sb("b_hid", [P, 3])
    g.b_sum = g.sb("b_sum", [P, 3])
    g.minus_half = g.sb("minus_half", [P, NJ])
    ctx, sb, ps = scope(g)
    with ctx:
        a_src, a_tgt = sb("a_src", [P, D]), sb("a_tgt", [P, D])
        prod = sb("prod", [P, 2, D])
        rows_in = sb("rows_in", [P, 3, D])
        rows_hid = sb("rows_hid", [P, 3, D])
        w_step = sb("w_step", [P, 3, D])
        in_t = sb("in_t", [P, 3 * D])
        step_t = sb("step_t", [P, 3 * D])
        t_ps = ps("t_ps", [P, 3, 512])
        c_ps = ps("c_ps", [P, 3, 512])
        loaded, dve, turned, copied = g.sem("w_loaded", "dma"), g.sem("w_dve"), g.sem("w_turned"), g.sem("w_copied")
        with g.block() as block:
            @block.sync
            def _(sp):
                one = lambda v: bcast(v, P)
                n = 0
                loads = [
                    (g.w_proj[:, 0:D], a["L0_gnn_W_proj"]), (g.w_skip[:], a["L0_gnn_W_skip"]),
                    (a_src[:], one(a["L0_gnn_a_src"].rearrange("a h f -> (a h f)"))),
                    (a_tgt[:], one(a["L0_gnn_a_tgt"].rearrange("a h f -> (a h f)"))),
                    (g.w1[:], a["L1_gnn_w1"]), (g.w2[0:HID, :], a["L1_gnn_w2"]),
                    (g.w2[HID:HID + 1, :], a["L1_gnn_b2"].rearrange("(a n) -> a n", a=1)),
                    (g.b1[:], one(a["L1_gnn_b1"])), (g.att[:], one(a["L2_gnn_W_att_w"])),
                    (g.att_b[:], one(a["L2_gnn_W_att_b"])),
                    (rows_in[:], a["L3_gnn_w_ih"].rearrange("(t p) n -> p t n", p=P)),
                    (rows_hid[:], a["L3_gnn_w_hh"].rearrange("(t p) n -> p t n", p=P)),
                    (w_step[:], a["L3_gnn_W"].rearrange("t p n -> p t n")),
                ]
                for to, of in loads:
                    sp.dma_start(to, of).then_inc(loaded.sem, 16)
                with nc.allow_non_contiguous_dma(reason="384 biases, once"):
                    for to, name in ((g.b_in, "L3_gnn_b_ih"), (g.b_hid, "L3_gnn_b_hh")):
                        sp.dma_start(to[:], a[name].rearrange("(t p) -> p t", p=P)).then_inc(loaded.sem, 16)
                sp.wait_ge(loaded.sem, loaded.base + 16 * (len(loads) + 2))
                loaded.up(16 * (len(loads) + 2))
        with g.block() as block:
            @block.vector
            def _(v):
                ch = Chain(v, dve)
                ch.step(nc.vector.memset(g.minus_half[:], -0.5))
                ch.step(nc.vector.tensor_tensor(g.b_sum[:], g.b_in[:], g.b_hid[:], ALU.add))
                ch.step(nc.vector.tensor_tensor(prod[:, 0, :], g.w_proj[:, 0:D], a_src[:], ALU.mult))
                ch.link(nc.vector.tensor_tensor(prod[:, 1, :], g.w_proj[:, 0:D], a_tgt[:], ALU.mult))
                ch.link(nc.vector.reduce_sum(g.w_proj[:, D:D + 2 * HEADS],
                                             prod[:].rearrange("p t (h f) -> p (t h) f", f=HF), AX_X))
                for n, to in enumerate((in_t, g.w_hid, step_t)):
                    v.wait_ge(turned.sem, turned.base + n + 1)
                    nc.vector.tensor_copy(to[:], t_ps[:, n, 0:3 * D]).then_inc(copied.sem, 1)
                for i in range(3):
                    v.wait_ge(turned.sem, turned.base + 4 + i)
                    ch.step(nc.vector.tensor_copy(g.w_in[:, i, :], c_ps[:, i, 0:3 * D]))
                ch.hold()
                ch.finish()

            @block.tensor
            def _(pe):
                for n, of in enumerate((rows_in, rows_hid, w_step)):
                    for t in range(3):
                        last = nc.tensor.transpose(t_ps[:, n, t * D:(t + 1) * D], of[:, t, :], g.ident[:])
                    last.then_inc(turned.sem, 1)
                pe.wait_ge(copied.sem, copied.base + 3)
                for i in range(3):
                    nc.tensor.matmul(c_ps[:, i, 0:3 * D], step_t[:, i * D:(i + 1) * D], in_t[:],
                                     start=True, stop=True).then_inc(turned.sem, 1)
        turned.up(6)
        copied.up(3)


class Tile:

    def __init__(self, it, n):
        self.it, self.n = it + n // TB, n % TB
        self.t = self.it * TB + self.n
        self.known = isinstance(self.t, int)

    def back(self, m=1):
        return Tile(self.it, self.n - m)

    def slot(self, slots=2):
        return self.n % slots

    def lap(self, slots):
        return self.it * (TB // slots) + self.n // slots

    @property
    def first_node(self):
        return min(self.t * NB, N - NB) if self.known else self.t * NB

    @property
    def is_last(self):
        return self.known and self.t == TILES - 1


class Ring:

    def __init__(self, g, name, slots=2, k=1, kind=""):
        self.c = [g.sem(f"{name}{n}", kind) for n in range(slots)]
        self.g, self.k, self.slots = g, k, slots

    def wait(self, eng, tile, laps):
        c = self.c[tile.slot(self.slots)]
        eng.wait_ge(c.sem, (tile.lap(self.slots) + laps) * self.k + c.base)
        if eng in (self.g.nc.gpsimd, self.g.nc.sync):
            gate(self.g, eng)

    def inc(self, ins, tile, by=1):
        return ins.then_inc(self.c[tile.slot(self.slots)].sem, by)

    def this(self, eng, tile):
        self.wait(eng, tile, 1)

    def slot_free(self, eng, tile):
        self.wait(eng, tile, 0)

    def one_back(self, eng, tile):
        if not (tile.known and tile.t == 0):
            self.wait(eng, tile.back(), 1)

    def four_back(self, eng, tile):
        if not (tile.known and tile.t < 4):
            self.wait(eng, tile.back(4), 1)

    def all(self, eng):
        for n in range(self.slots):
            self.wait(eng, Tile(0, n), -(-(TILES - n) // self.slots))

    def up(self):
        for n, c in enumerate(self.c):
            c.up(self.k * -(-(TILES - n) // self.slots))


def rings(g, *names):
    return [Ring(g, n) for n in names]


def braid(steps):
    steps = [step for step in steps if step is not None]
    while steps:
        steps = [step for step in steps if next(step, step) is not step]


def run_tiles(eng, *steps):
    offsets = [offset for offset, _ in steps]

    def whole(time):
        braid([step(Tile(0, time + offset)) for offset, step in steps if 0 <= time + offset < TILES])

    start = max(0, -min(offsets))
    laps = (TILES - 2 - max(offsets) - start + 1) // TB
    for time in range(-max(offsets), start):
        whole(time)
    with eng.Fori(0, laps) as it:
        for n in range(TB):
            braid([step(Tile(it, start + offset + n)) for offset, step in steps])
    for time in range(start + laps * TB, TILES - min(offsets)):
        whole(time)


def tile_of(table, tile):
    return table[bass.ds(tile.first_node, NB), :].rearrange("(p j) w -> p (j w)", j=NJ)


def flat(ap):
    return ap.rearrange("p j w -> p (j w)")


def turn(g, out_ps, tile, width=D):
    for j in range(NJ):
        last = g.nc.tensor.transpose(out_ps[0:width, j * P:(j + 1) * P], tile[:, j, :], g.ident[:])
    return last


class Norm:

    def __init__(self, g, sb):
        self.g = g
        self.stats = sb("ln_stats", [P, 2, NJ, 6])
        self.mv = sb("ln_mv", [P, 2, NJ, 2])
        self.ve = sb("ln_ve", [P, 2, NJ])
        self.minus = sb("ln_minus", [P, 2, NJ])
        self.rstd = sb("ln_rstd", [P, 2, NJ])
        self.shift = sb("ln_shift", [P, 2, NJ])
        self.stats_there, self.mv_there, self.var_there, self.rstd_there, self.shift_there, self.done = rings(
            g, "ln_stats", "ln_mv", "ln_var", "ln_rstd", "ln_shift", "ln_done")

    def moments(self, v, y, tile):
        nc, h = self.g.nc, tile.slot()
        for j in range(NJ):
            last = nc.vector.bn_stats(self.stats[:, h, j, :], y[:, h, j, :])
        self.stats_there.inc(last, tile)
        yield
        self.stats_there.this(v, tile)
        gate(self.g, v)
        for j in range(NJ):
            last = nc.vector.bn_aggr(self.mv[:, h, j, :], self.stats[:, h, j, :])
        self.mv_there.inc(last, tile)
        yield
        self.mv_there.this(v, tile)
        self.shift_there.slot_free(v, tile)
        nc.vector.tensor_scalar(self.minus[:, h, :], self.mv[:, h, :, 0], -1.0, None, ALU.mult)
        self.var_there.inc(nc.vector.tensor_scalar(self.ve[:, h, :], self.mv[:, h, :, 1], LN_EPS, None,
                                                   ALU.add), tile)

    def power(self, pool, tile):
        nc, h = self.g.nc, tile.slot()
        self.var_there.this(pool, tile)
        self.done.slot_free(pool, tile)
        self.rstd_there.inc(nc.gpsimd.tensor_tensor(self.rstd[:, h, :], self.ve[:, h, :],
                                                    self.g.minus_half[:], ALU.pow), tile)
        self.rstd_there.this(pool, tile)
        self.shift_there.inc(nc.gpsimd.tensor_tensor(self.shift[:, h, :], self.minus[:, h, :],
                                                     self.rstd[:, h, :], ALU.mult), tile)

    def scale(self, act, out, y, tile):
        self.shift_there.this(act, tile)
        h = tile.slot()
        for j in range(NJ):
            last = self.g.nc.scalar.activation(out[:, h, j, :], y[:, h, j, :], ACT.Identity,
                                               bias=self.shift[:, h, j:j + 1], scale=self.rstd[:, h, j:j + 1])
        self.done.inc(last, tile)

    def scale_by_dve(self, v, out, y, tile):
        self.shift_there.this(v, tile)
        h = tile.slot()
        for j in range(NJ):
            last = self.g.nc.vector.tensor_scalar(out[:, h, j, :], y[:, h, j, :], self.rstd[:, h, j:j + 1],
                                                  self.shift[:, h, j:j + 1], ALU.mult, ALU.add)
        self.done.inc(last, tile)

    def up(self):
        for r in (self.stats_there, self.mv_there, self.var_there, self.rstd_there, self.shift_there, self.done):
            r.up()


def store(eng, stored, tile, *pairs):
    if tile.is_last:
        stored.one_back(eng, tile)
    for table, buf in pairs:
        stored.inc(eng.dma_start(tile_of(table, tile), buf), tile, 16)


class Prefetch:

    def __init__(self, g, sb, side, edge_attr):
        self.g, self.side, self.edge_attr = g, side, edge_attr
        self.idx = sb("pre_idx", [P, 2, 2], I32)
        self.rows = sb("pre_rows", [P, 4, 2, D])
        self.there = Ring(g, "pre_there", 2, 32, "pool_dma")
        self.kept = Ring(g, "pre_kept", 4, 16, "dma")
        self.staged = Ring(g, "pre_staged")

    def gather(self, pool, tile):
        h = tile.slot()
        self.there.slot_free(pool, tile)
        self.staged.inc(self.g.nc.gpsimd.tensor_copy(self.idx[:, h, :], self.side.edge_i[:, bass.ds(tile.t * 2, 2)]),
                        tile)
        self.kept.slot_free(pool, tile)
        self.staged.this(pool, tile)
        for u in range(2):
            self.there.inc(pool.indirect_dma_start(
                out=self.rows[:, tile.slot(4), u, :], out_offset=None, in_=self.edge_attr,
                in_offset=bass.IndirectOffsetOnAxis(ap=self.idx[:, h, u:u + 1], axis=0)), tile, 16)

    def keep(self, act, tile):
        self.there.this(act, tile)
        self.kept.inc(act.dma_start(self.side.rows[:, bass.ds(tile.t * 2, 2), :], self.rows[:, tile.slot(4)]),
                      tile, 16)

    def up(self):
        for r in (self.there, self.kept, self.staged):
            r.up()


def gat_project_pass(g, x):
    nc = g.nc
    g.proj = g.dram("proj", [N, AW])
    g.tgt_score = g.dram("tgt_score", [N, HEADS])
    W = D + 2 * HEADS
    ctx, sb, ps = scope(g)
    with ctx:
        xin = sb("xin", [P, 4, NJ, D])
        x_t = sb("x_t", [P, 2, NB])
        pout = sb("pout", [P, 2, NJ, AW])
        sout = sb("sout", [P, 2, NJ, HEADS])
        t_ps = ps("t_ps", [P, 2, 512])
        o_ps = ps("o_ps", [P, 2, 2, 512])
        loaded = Ring(g, "node_loaded", 4, 16, "dma")
        stored = Ring(g, "node_stored", 2, 32, "dma")
        turned, x_t_there, product, ready = rings(g, "node_turned", "node_turned_sb", "node_product", "node_ready")
        with g.block() as block:
            @block.sync
            def _(sp):
                def loads(tile):
                    turned.four_back(sp, tile)
                    loaded.inc(sp.dma_start(flat(xin[:, tile.slot(4)]), tile_of(x, tile)), tile, 16)

                def stores(tile):
                    ready.this(sp, tile)
                    store(sp, stored, tile, (g.proj, flat(pout[:, tile.slot()])),
                          (g.tgt_score, flat(sout[:, tile.slot()])))

                run_tiles(sp, (3, loads), (-1, stores))
                stored.all(sp)

            @block.tensor
            def _(pe):
                def turns(tile):
                    loaded.this(pe, tile)
                    x_t_there.slot_free(pe, tile)
                    turned.inc(turn(g, t_ps[:, tile.slot()], xin[:, tile.slot(4)]), tile)

                def products(tile):
                    h = tile.slot()
                    x_t_there.this(pe, tile)
                    ready.slot_free(pe, tile)
                    for j in range(NJ):
                        last = nc.tensor.matmul(o_ps[:, h, j // 2, (j % 2) * W:(j % 2 + 1) * W],
                                                x_t[:, h, j * P:(j + 1) * P], g.w_proj[:], start=True, stop=True)
                    product.inc(last, tile)

                run_tiles(pe, (1, turns), (0, products))

            @block.scalar
            def _(act):
                def copies(tile):
                    turned.this(act, tile)
                    product.slot_free(act, tile)
                    x_t_there.inc(nc.scalar.copy(x_t[:, tile.slot(), :], t_ps[:, tile.slot(), :]), tile)

                run_tiles(act, (0, copies))

            @block.vector
            def _(v):
                def outs(tile):
                    h = tile.slot()
                    product.this(v, tile)
                    stored.slot_free(v, tile)
                    for b in range(2):
                        o = o_ps[:, h, b, 0:2 * W].rearrange("p (j w) -> p j w", w=W)
                        nc.vector.tensor_copy(pout[:, h, 2 * b:2 * b + 2, :], o[:, :, 0:AW])
                        last = nc.vector.tensor_copy(sout[:, h, 2 * b:2 * b + 2, :], o[:, :, AW:W])
                    ready.inc(last, tile)

                run_tiles(v, (0, outs))
        for r in (loaded, stored, turned, x_t_there, product, ready):
            r.up()


def gat_score_pass(g, s, e_sb):
    nc = g.nc
    ctx, sb, ps = scope(g)
    with ctx:
        rowbuf = sb("rowbuf", [P, 2, U, AW])
        tgt = sb("tgt", [P, 2, U, HEADS])
        raw = sb("raw", [P, 2, U, HEADS])
        gmax = sb("gmax", [P, 3])
        st_src, st_key = Stage(g, sb, "gather"), Stage(g, sb, "second")
        got = Halves(g, "score_rows", 16 * U * 2, by_pool=True)
        kept = Halves(g, "score_kept", 16)
        summed, scored = all_halves(g, "score_sum", "score_done")
        keys = g.sem("key_row_loaded", "dma")
        with g.block() as block:
            @block.scalar
            def _(act):
                load_key_row(g, act, s, keys)
                act.wait_ge(keys.sem, keys.base + 16)

            @block.sync
            def _(sp):
                def keep(half, it):
                    got.this(sp, half, it)
                    kept.inc(sp.dma_start(g.rows[:, bass.ds(it * (2 * U) + half * U, U), :],
                                          rowbuf[:, half, :, 0:D]), half)

                def stage(half, it):
                    got.two_back(sp, half, it)
                    st_src.load(sp, s.other_i, half, it)
                    st_key.load(sp, s.key_i, half, it)

                stage(0, 0)
                with sp.Fori(0, STEPS - 1) as it:
                    for half in range(2):
                        stage(1 - half, it + half)
                        keep(half, it)
                stage(1, STEPS - 1)
                keep(0, STEPS - 1)
                keep(1, STEPS - 1)
                for half in range(2):
                    kept.two_back(sp, half, STEPS)

            @block.gpsimd
            def _(pool):
                with pool.Fori(0, STEPS) as it:
                    for half in range(2):
                        st_src.there.this(pool, half, it)
                        st_key.there.this(pool, half, it)
                        summed.two_back(pool, half, it)
                        kept.two_back(pool, half, it)
                        for ins in gather(pool, st_src, g.proj, lambda u: rowbuf[:, half, u, :], half):
                            ins.then_inc(got.c[half].sem, 16)
                        for ins in gather(pool, st_key, g.tgt_score, lambda u: tgt[:, half, u, :], half):
                            ins.then_inc(got.c[half].sem, 16)

            @block.vector
            def _(v):
                with v.Fori(0, STEPS) as it:
                    for half in range(2):
                        got.this(v, half, it)
                        summed.inc(nc.vector.tensor_tensor(raw[:, half], rowbuf[:, half, :, D:AW], tgt[:, half],
                                                           ALU.add), half)
                        summed.this(v, half, it)
                        scored.inc(nc.vector.scalar_tensor_tensor(
                            e_sb[:, bass.ds(it * (2 * U) + half * U, U), :], raw[:, half], 0.2, raw[:, half],
                            ALU.mult, ALU.max), half)
                        scored.this(v, half, it)
        keys.up(16)
        for h in (st_src.there, st_key.there, got, kept, summed, scored):
            h.up(STEPS)
        dve, maxed, negated, powered = g.sem("max_dve"), g.sem("max_all"), g.sem("max_neg"), g.sem("max_exp")
        dve_base = dve.base
        with g.block() as block:
            @block.vector
            def _(v):
                ch = Chain(v, dve)
                ch.link(nc.vector.memset(e_sb[0:88, CH - 1, :], FAR))
                ch.step(nc.vector.reduce_max(gmax[:, 0:1], e_sb[:].rearrange("p c h -> p (c h)"), AX_X))
                v.wait_ge(maxed.sem, maxed.base + 1)
                nc.vector.tensor_scalar(gmax[:, 2:3], gmax[:, 1:2], -1.0, None, ALU.mult).then_inc(negated.sem, 1)
                ch.finish()

            @block.gpsimd
            def _(pool):
                pool.wait_ge(dve.sem, dve_base + 2)
                nc.gpsimd.partition_all_reduce(gmax[:, 1:2], gmax[:, 0:1], P, RMAX).then_inc(maxed.sem, 1)

            @block.scalar
            def _(act):
                act.wait_ge(negated.sem, negated.base + 1)
                nc.scalar.activation(e_sb[:], e_sb[:], ACT.Exp, bias=gmax[:, 2:3]).then_inc(powered.sem, 1)
                act.wait_ge(powered.sem, powered.base + 1)
        maxed.up(1)
        negated.up(1)
        powered.up(1)


def gat_finish_pass(g, x, side, edge_attr):
    nc = g.nc
    g.x1 = g.dram("x1", [N, D])
    g.hid_a = g.dram("hid_a", [N, HID])
    ctx, sb, ps = scope(g)
    with ctx:
        xin = sb("xin", [P, 4, NJ, D])
        agg = sb("agg", [P, 4, NJ, AW])
        x_t = sb("x_t", [P, 2, NB])
        y_t = sb("y_t", [P, 2, NB])
        den = sb("den", [P, 2, NJ, HEADS])
        rden = sb("rden", [P, 2, NJ, HEADS])
        mean = sb("mean", [P, 2, NJ, D])
        t = sb("t", [P, 2, NJ, D])
        power = sb("power", [P, 2, NJ, D])
        low = sb("low", [P, 2, NJ, D])
        y = sb("y", [P, 2, NJ, D])
        x1 = sb("x1_sb", [P, 2, NJ, D])
        h = sb("h_sb", [P, 2, NJ, HID])
        t_ps = ps("t_ps", [P, 2, 512])
        o_ps = ps("o_ps", [P, 2, 512])
        y_ps = ps("y_ps", [P, 2, 512])
        h_ps = ps("h_ps", [P, 2, 512])
        ln = Norm(g, sb)
        pre = Prefetch(g, sb, side, edge_attr)
        loaded = Ring(g, "node_loaded", 4, 32, "dma")
        x1_stored, h_stored = Ring(g, "x1_stored", 2, 16, "dma"), Ring(g, "hid_stored", 2, 16, "dma")
        turned, x_t_there, product, den_there, rden_there, mean_there, t_there, exped, low_there, summed = rings(
            g, "node_turned", "node_turned_sb", "node_product", "fin_den", "fin_rden", "fin_mean", "fin_t",
            "fin_exp", "fin_low", "fin_sum")
        turned1, y_t_there, product1, h_there = rings(g, "fin_turned", "fin_turned_sb", "fin_product", "fin_h")
        with g.block() as block:
            @block.sync
            def _(sp):
                def loads(tile):
                    turned.four_back(sp, tile)
                    summed.four_back(sp, tile)
                    loaded.inc(sp.dma_start(flat(xin[:, tile.slot(4)]), tile_of(x, tile)), tile, 16)
                    loaded.inc(sp.dma_start(flat(agg[:, tile.slot(4)]), tile_of(g.agg_dst, tile)), tile, 16)

                run_tiles(sp, (3, loads))

            @block.tensor
            def _(pe):
                def turns(tile):
                    loaded.this(pe, tile)
                    x_t_there.slot_free(pe, tile)
                    turned.inc(turn(g, t_ps[:, tile.slot()], xin[:, tile.slot(4)]), tile)

                def products(tile):
                    s = tile.slot()
                    x_t_there.this(pe, tile)
                    t_there.slot_free(pe, tile)
                    for j in range(NJ):
                        last = nc.tensor.matmul(o_ps[:, s, j * D:(j + 1) * D], x_t[:, s, j * P:(j + 1) * P],
                                                g.w_skip[:], start=True, stop=True)
                    product.inc(last, tile)

                def turns_x1(tile):
                    ln.done.this(pe, tile)
                    y_t_there.slot_free(pe, tile)
                    turned1.inc(turn(g, y_ps[:, tile.slot()], x1[:, tile.slot()]), tile)

                def products_x1(tile):
                    s = tile.slot()
                    y_t_there.this(pe, tile)
                    h_there.slot_free(pe, tile)
                    for j in range(NJ):
                        last = nc.tensor.matmul(h_ps[:, s, j * HID:(j + 1) * HID], y_t[:, s, j * P:(j + 1) * P],
                                                g.w1[:], start=True, stop=True)
                    product1.inc(last, tile)

                run_tiles(pe, (2, turns), (1, products), (-2, turns_x1), (-3, products_x1))

            @block.scalar
            def _(act):
                def copy_x(tile):
                    turned.this(act, tile)
                    product.slot_free(act, tile)
                    x_t_there.inc(nc.scalar.copy(x_t[:, tile.slot()], t_ps[:, tile.slot()]), tile)

                def exps(tile):
                    t_there.this(act, tile)
                    low_there.slot_free(act, tile)
                    exped.inc(nc.scalar.activation(power[:, tile.slot()], t[:, tile.slot()], ACT.Exp), tile)

                def scales(tile):
                    x1_stored.slot_free(act, tile)
                    turned1.slot_free(act, tile)
                    ln.scale(act, x1, y, tile)

                def copy_x1(tile):
                    turned1.this(act, tile)
                    product1.slot_free(act, tile)
                    y_t_there.inc(nc.scalar.copy(y_t[:, tile.slot()], y_ps[:, tile.slot()]), tile)

                def copy_h(tile):
                    product1.this(act, tile)
                    h_stored.slot_free(act, tile)
                    h_there.inc(nc.scalar.copy(flat(h[:, tile.slot()]), h_ps[:, tile.slot(), 0:NJ * HID]), tile)

                def store_x1(tile):
                    ln.done.this(act, tile)
                    store(act, x1_stored, tile, (g.x1, flat(x1[:, tile.slot()])))

                def store_h(tile):
                    h_there.this(act, tile)
                    store(act, h_stored, tile, (g.hid_a, flat(h[:, tile.slot()])))

                run_tiles(act, (2, copy_x), (-2, store_x1), (-4, store_h), (-2, lambda tile: pre.keep(act, tile)),
                          (-2, copy_x1), (-3, copy_h), (-1, scales), (1, exps))
                for r in (x1_stored, h_stored, pre.kept):
                    r.all(act)

            @block.vector
            def _(v):
                def outs(tile):
                    s, s4 = tile.slot(), tile.slot(4)
                    loaded.this(v, tile)
                    den_there.inc(nc.vector.tensor_scalar(den[:, s], agg[:, s4, :, D:AW], 1e-16, None, ALU.add), tile)
                    yield
                    den_there.this(v, tile)
                    rden_there.inc(nc.vector.reciprocal(rden[:, s], den[:, s]), tile)
                    yield
                    rden_there.this(v, tile)
                    for j in range(NJ):
                        last = nc.vector.tensor_tensor(
                            mean[:, s, j].rearrange("p (h f) -> p h f", f=HF),
                            agg[:, s4, j, 0:D].rearrange("p (h f) -> p h f", f=HF),
                            rden[:, s, j].unsqueeze(2).to_broadcast([P, HEADS, HF]), ALU.mult)
                    mean_there.inc(last, tile)
                    yield
                    mean_there.this(v, tile)
                    product.this(v, tile)
                    exped.slot_free(v, tile)
                    t_there.inc(nc.vector.tensor_tensor(flat(t[:, s]), flat(mean[:, s]), o_ps[:, s], ALU.add), tile)

                def sums(tile):
                    s = tile.slot()
                    exped.this(v, tile)
                    low_there.inc(nc.vector.scalar_tensor_tensor(
                        flat(low[:, s]), flat(power[:, s]), 1.0, flat(xin[:, tile.slot(4)]), ALU.min, ALU.add), tile)
                    yield
                    low_there.this(v, tile)
                    ln.done.slot_free(v, tile)
                    summed.inc(nc.vector.scalar_tensor_tensor(flat(y[:, s]), flat(t[:, s]), 0.0, flat(low[:, s]),
                                                              ALU.max, ALU.add), tile)
                    yield
                    summed.this(v, tile)
                    yield from ln.moments(v, y, tile)

                run_tiles(v, (1, outs), (0, sums))

            @block.gpsimd
            def _(pool):
                run_tiles(pool, (1, lambda tile: pre.gather(pool, tile)), (0, lambda tile: ln.power(pool, tile)))
        for r in (ln, pre, loaded, x1_stored, h_stored, turned, x_t_there, product, den_there, rden_there, mean_there,
                  t_there, exped, low_there, summed, turned1, y_t_there, product1, h_there):
            r.up()


def gcn_finish_pass(g, side, edge_attr, next_side):
    nc = g.nc
    g.x2 = g.dram("x2", [N, D])
    g.node_score = g.dram("node_score", [N, 1])
    ctx, sb, ps = scope(g)
    with ctx:
        xin = sb("xin", [P, 4, NJ, D])
        agg = sb("agg", [P, 4, NJ, HID])
        a_t = sb("a_t", [HID + 1, 2, NB])
        sig = sb("sig", [P, 2, NJ, D])
        y = sb("y", [P, 2, NJ, D])
        x2 = sb("x2_sb", [P, 2, NJ, D])
        junk = sb("junk", [P, 2, NJ, D], BF16)
        dot = sb("dot", [P, 2, NJ])
        sc = sb("sc", [P, 2, NJ])
        t_ps = ps("t_ps", [P, 2, 512])
        o_ps = ps("o_ps", [P, 2, 512])
        ln = Norm(g, sb)
        pre = Prefetch(g, sb, side, edge_attr)
        loaded = Ring(g, "node_loaded", 4, 32, "dma")
        x2_stored, sc_stored = Ring(g, "x2_stored", 2, 16, "dma"), Ring(g, "score_stored", 2, 16, "dma")
        turned, a_t_there, product, squashed, summed, dotted, scored = rings(
            g, "node_turned", "node_turned_sb", "node_product", "gcn_squashed", "gcn_summed", "gcn_dotted", "gcn_scored")
        ones, keys = g.sem("gcn_ones"), g.sem("key_row_loaded", "dma")
        with g.block() as block:
            @block.vector
            def _(v):
                nc.vector.memset(a_t[HID:HID + 1, :, :], 1.0).then_inc(ones.sem, 1)
                v.wait_ge(ones.sem, ones.base + 1)
        ones.up(1)
        with g.block() as block:
            @block.sync
            def _(sp):
                def loads(tile):
                    summed.four_back(sp, tile)
                    turned.four_back(sp, tile)
                    loaded.inc(sp.dma_start(flat(xin[:, tile.slot(4)]), tile_of(g.x1, tile)), tile, 16)
                    loaded.inc(sp.dma_start(flat(agg[:, tile.slot(4)]), tile_of(g.agg_hid2, tile)), tile, 16)

                load_key_row(g, sp, next_side, keys)
                run_tiles(sp, (3, loads))
                sp.wait_ge(keys.sem, keys.base + 16)

            @block.tensor
            def _(pe):
                def turns(tile):
                    loaded.this(pe, tile)
                    a_t_there.slot_free(pe, tile)
                    gate(g, pe)
                    turned.inc(turn(g, t_ps[:, tile.slot()], agg[:, tile.slot(4)], HID), tile)

                def products(tile):
                    s = tile.slot()
                    a_t_there.this(pe, tile)
                    squashed.slot_free(pe, tile)
                    for j in range(NJ):
                        last = nc.tensor.matmul(o_ps[:, s, j * D:(j + 1) * D], a_t[:, s, j * P:(j + 1) * P],
                                                g.w2[:], start=True, stop=True)
                    product.inc(last, tile)

                run_tiles(pe, (2, turns), (1, products))

            @block.scalar
            def _(act):
                def copies(tile):
                    turned.this(act, tile)
                    product.slot_free(act, tile)
                    a_t_there.inc(nc.scalar.copy(a_t[0:HID, tile.slot(), :], t_ps[0:HID, tile.slot(), :]), tile)

                def squash(tile):
                    product.this(act, tile)
                    summed.slot_free(act, tile)
                    squashed.inc(nc.scalar.activation(flat(sig[:, tile.slot()]), o_ps[:, tile.slot()],
                                                      ACT.Sigmoid), tile)

                def scales(tile):
                    x2_stored.slot_free(act, tile)
                    dotted.slot_free(act, tile)
                    ln.scale(act, x2, y, tile)

                def store_x2(tile):
                    ln.done.this(act, tile)
                    store(act, x2_stored, tile, (g.x2, flat(x2[:, tile.slot()])))

                def store_scores(tile):
                    scored.this(act, tile)
                    store(act, sc_stored, tile, (g.node_score, sc[:, tile.slot()]))

                run_tiles(act, (2, copies), (-2, store_x2), (-3, store_scores),
                          (-2, lambda tile: pre.keep(act, tile)), (-1, scales), (1, squash))
                for r in (x2_stored, sc_stored, pre.kept):
                    r.all(act)

            @block.vector
            def _(v):
                def sums(tile):
                    s = tile.slot()
                    loaded.this(v, tile)
                    squashed.this(v, tile)
                    ln.done.slot_free(v, tile)
                    summed.inc(nc.vector.tensor_tensor(y[:, s], sig[:, s], xin[:, tile.slot(4)], ALU.add), tile)
                    yield
                    summed.this(v, tile)
                    yield from ln.moments(v, y, tile)

                def scores(tile):
                    s = tile.slot()
                    ln.done.this(v, tile)
                    for j in range(NJ):
                        last = nc.vector.scalar_tensor_tensor(junk[:, s, j], x2[:, s, j], 1.0, g.att[:, 0:D],
                                                              ALU.mult, ALU.mult, accum_out=dot[:, s, j:j + 1])
                    dotted.inc(last, tile)
                    yield
                    dotted.this(v, tile)
                    sc_stored.slot_free(v, tile)
                    scored.inc(nc.vector.tensor_scalar(sc[:, s], dot[:, s], g.att_b[:], None, ALU.add), tile)

                run_tiles(v, (0, sums), (-2, scores))

            @block.gpsimd
            def _(pool):
                run_tiles(pool, (1, lambda tile: pre.gather(pool, tile)), (0, lambda tile: ln.power(pool, tile)))
        keys.up(16)
        for r in (ln, pre, loaded, x2_stored, sc_stored, turned, a_t_there, product, squashed, summed, dotted, scored):
            r.up()


def att_score_pass(g, s, score, top):
    nc = g.nc
    ctx, sb, ps = scope(g)
    with ctx:
        rowbuf = sb("rowbuf", [P, 2, U, D])
        node = sb("node", [P, 2, U])
        junk = sb("junk", [P, 2, U, D], BF16)
        dot = sb("dot", [P, 2, U])
        raw = sb("raw", [P, 2, U])
        leaky = sb("leaky", [P, 2, U])
        diag = sb("diag", [P, 2, U, P])
        far = sb("far", [P, 2, U, P])
        full = sb("full", [P, 2, U, P])
        ones = sb("ones", [P, P])
        row_ps = ps("row_ps", [P, 2, 1024])
        st_key = Stage(g, sb, "second")
        loaded = Halves(g, "score_rows", 16)
        got = Halves(g, "score_nodes", 16 * U, by_pool=True)
        dotted, summed, scored, diagonal, apart, spread, masked, topped = all_halves(
            g, "att_dotted", "att_summed", "att_scored", "att_diagonal", "att_apart", "att_spread", "att_masked", "att_topped")
        set_up = g.sem("att_ones")
        with g.block() as block:
            @block.vector
            def _(v):
                nc.vector.memset(ones[:], 1.0).then_inc(set_up.sem, 1)
                v.wait_ge(set_up.sem, set_up.base + 1)
        set_up.up(1)
        with g.block() as block:
            @block.sync
            def _(sp):
                with sp.Fori(0, STEPS) as it:
                    for half in range(2):
                        got.two_back(sp, half, it)
                        st_key.load(sp, s.key_i, half, it)
                        dotted.two_back(sp, half, it)
                        loaded.inc(sp.dma_start(rowbuf[:, half],
                                                s.rows[:, bass.ds(it * (2 * U) + half * U, U), :]), half)

            @block.gpsimd
            def _(pool):
                with pool.Fori(0, STEPS) as it:
                    for half in range(2):
                        st_key.there.this(pool, half, it)
                        summed.two_back(pool, half, it)
                        for ins in gather(pool, st_key, g.node_score, lambda u: node[:, half, u:u + 1], half):
                            ins.then_inc(got.c[half].sem, 16)

            @block.tensor
            def _(pe):
                with pe.Fori(0, STEPS) as it:
                    for half in range(2):
                        diagonal.this(pe, half, it)
                        masked.two_back(pe, half, it)
                        for u in range(U):
                            last = nc.tensor.matmul(row_ps[:, half, u * P:(u + 1) * P], ones[:],
                                                    diag[:, half, u, :], start=True, stop=True)
                        spread.inc(last, half)

            @block.vector
            def _(v):
                def scores(half, it):
                    first = it * (2 * U) + half * U
                    loaded.this(v, half, it)
                    for u in range(U):
                        last = nc.vector.scalar_tensor_tensor(
                            junk[:, half, u, :], rowbuf[:, half, u, :], 1.0, g.att[:, D:2 * D], ALU.mult,
                            ALU.mult, accum_out=dot[:, half, u:u + 1])
                    dotted.inc(last, half)
                    dotted.this(v, half, it)
                    got.this(v, half, it)
                    summed.inc(nc.vector.tensor_tensor(raw[:, half], dot[:, half], node[:, half], ALU.add), half)
                    summed.this(v, half, it)
                    scored.inc(nc.vector.scalar_tensor_tensor(leaky[:, half], raw[:, half], 0.2, raw[:, half],
                                                              ALU.mult, ALU.max), half)
                    scored.this(v, half, it)
                    nc.vector.tensor_copy(score[:, bass.ds(first, U)], leaky[:, half])
                    for u in range(U):
                        last = nc.vector.tensor_scalar(diag[:, half, u, :], g.ident[:], leaky[:, half, u:u + 1],
                                                       None, ALU.mult)
                    diagonal.inc(last, half)
                    for u in range(U):
                        last = nc.vector.tensor_scalar(far[:, half, u, :], chunk_keys(g, first + u),
                                                       s.key[:, bass.ds(first + u, 1)], FAR, ALU.not_equal,
                                                       ALU.mult)
                    apart.inc(last, half)

                def tops(half, it):
                    first = it * (2 * U) + half * U
                    apart.this(v, half, it)
                    spread.this(v, half, it)
                    masked.inc(nc.vector.tensor_tensor(
                        full[:, half].rearrange("p u q -> p (u q)"), far[:, half].rearrange("p u q -> p (u q)"),
                        row_ps[:, half, 0:U * P], ALU.add), half)
                    masked.this(v, half, it)
                    topped.inc(nc.vector.reduce_max(top[:, bass.ds(first, U)], full[:, half], AX_X), half)

                scores(0, 0)
                with v.Fori(0, STEPS - 1) as it:
                    for half in range(2):
                        scores(1 - half, it + half)
                        tops(half, it)
                scores(1, STEPS - 1)
                tops(0, STEPS - 1)
                tops(1, STEPS - 1)
                for half in range(2):
                    topped.two_back(v, half, STEPS)
        for h in (st_key.there, loaded, got, dotted, summed, scored, diagonal, apart,
                  spread, masked, topped):
            h.up(STEPS)


def att_max_pass(g, s, score, top):
    nc = g.nc
    ctx, sb, ps = scope(g)
    with ctx:
        key_first = sb("key_first", [1, CH])
        top_first = sb("top_first", [1, CH])
        whole = sb("whole", [1, CH])
        goes_on = sb("goes_on", [1, 2, CH])
        pen = sb("pen", [1, 2, CH])
        run = sb("run", [1, 2, CH])
        rows = sb("rows", [1, 4, CH])
        wide = sb("wide", [P, 4, CH])
        t1 = sb("t1", [P, 2, CH])
        t2 = sb("t2", [P, 2, CH])
        loaded, dve, spread, powered = g.sem("amax_loaded", "dma"), g.sem("amax_dve"), g.sem("amax_spread"), g.sem("amax_exp")
        with g.block() as block:
            @block.sync
            def _(sp):
                sp.dma_start(key_first[:], s.key_d[P - 1:P, :]).then_inc(loaded.sem, 16)
                sp.dma_start(top_first[:], top[P - 1:P, :]).then_inc(loaded.sem, 16)

            @block.vector
            def _(v):
                ch = Chain(v, dve)
                v.wait_ge(loaded.sem, loaded.base + 32)
                key_last = s.key[0:1, :]
                ch.step(nc.vector.memset(goes_on[:], 0.0))
                ch.step(nc.vector.memset(rows[:], FAR))
                ch.link(nc.vector.tensor_tensor(whole[:], key_first[:], key_last, ALU.is_equal))
                ch.step(nc.vector.tensor_tensor(goes_on[:, 0, :], key_first[:], s.before[:], ALU.is_equal))
                ch.link(nc.vector.tensor_tensor(goes_on[:, 1, 0:CH - 1], key_first[:, 1:CH], key_last[:, 0:CH - 1],
                                                ALU.is_equal))
                for d in range(2):
                    ch.step(nc.vector.tensor_tensor(pen[:, d, :], goes_on[:, d, :], whole[:], ALU.mult))
                ch.hold()
                ch.link(nc.vector.tensor_scalar(pen[:], pen[:], -FAR, FAR, ALU.mult, ALU.add))
                ch.step(nc.vector.tensor_tensor_scan(run[:, 0, :], pen[:, 0, :], top[0:1, :], FAR, ALU.add, ALU.max))
                ch.link(nc.vector.tensor_tensor_scan(run[:, 1, ::-1], pen[:, 1, ::-1], top_first[:, ::-1], FAR,
                                                     ALU.add, ALU.max))
                ch.step(nc.vector.tensor_copy(rows[:, 0, 1:CH], run[:, 0, 0:CH - 1]))
                ch.step(nc.vector.tensor_copy(rows[:, 1, :], s.before[:]))
                ch.step(nc.vector.tensor_copy(rows[:, 2, 0:CH - 1], run[:, 1, 1:CH]))
                ch.link(nc.vector.tensor_copy(rows[:, 3, 0:CH - 1], key_first[:, 1:CH]))
                ch.finish()
        with g.block() as block:
            @block.gpsimd
            def _(pool):
                nc.gpsimd.partition_broadcast(wide[:].rearrange("p a c -> p (a c)"),
                                              rows[:].rearrange("p a c -> p (a c)"), P).then_inc(spread.sem, 1)
                pool.wait_ge(spread.sem, spread.base + 1)
        with g.block() as block:
            @block.vector
            def _(v):
                ch = Chain(v, dve)
                for d in range(2):
                    ch.step(nc.vector.tensor_tensor(t1[:, d, :], s.key[:], wide[:, 2 * d + 1, :], ALU.not_equal))
                ch.hold()
                for d in range(2):
                    ch.step(nc.vector.scalar_tensor_tensor(t2[:, d, :], t1[:, d, :], FAR, wide[:, 2 * d, :],
                                                           ALU.mult, ALU.add))
                ch.hold()
                for d in range(2):
                    ch.link(nc.vector.tensor_tensor(top[:], top[:], t2[:, d, :], ALU.max))
                ch.link(nc.vector.tensor_tensor(score[:], score[:], top[:], ALU.subtract))
                ch.finish()
        with g.block() as block:
            @block.scalar
            def _(act):
                nc.scalar.activation(score[:], score[:], ACT.Exp).then_inc(powered.sem, 1)
                act.wait_ge(powered.sem, powered.base + 1)
        loaded.up(32)
        spread.up(1)
        powered.up(1)


def att_finish_pass(g):
    nc = g.nc
    g.x3 = g.dram("x3", [N, D])
    ctx, sb, ps = scope(g)
    with ctx:
        xin = sb("xin", [P, 4, NJ, D])
        agg = sb("agg", [P, 4, 2, NJ, AW])
        none, mx, less, fac, part, coef = [sb(n, [P, 2, 2, NJ]) for n in ("none", "mx", "less", "fac", "part", "coef")]
        both, den, empty, safe, rden, keep = [sb(n, [P, 2, NJ])
                                              for n in ("both", "den", "empty", "safe", "rden", "keep")]
        first = sb("first", [P, 2, NJ, D])
        mean = sb("mean", [P, 2, NJ, D])
        gel = sb("gel", [P, 2, NJ, D])
        y = sb("y", [P, 2, NJ, D])
        x3 = sb("x3_sb", [P, 2, NJ, D])
        ln = Norm(g, sb)
        loaded, stored = Ring(g, "node_loaded", 4, 32, "dma"), Ring(g, "node_stored", 2, 16, "dma")
        x_loaded = Ring(g, "node_x_loaded", 4, 16, "dma")
        none_there, mx_there, both_there, less_there, exped, part_there, den_there, empty_there, safe_there = rings(
            g, "join_none", "join_mx", "join_both", "join_less", "join_exp", "join_part", "join_den", "join_empty",
            "join_safe")
        rden_there, coef_there, first_there, mean_there, gelued, summed = rings(
            g, "join_rden", "join_coef", "join_first", "join_mean", "join_gelu", "join_sum")
        with g.block() as block:
            @block.sync
            def _(sp):
                def loads(tile):
                    mean_there.four_back(sp, tile)
                    s = tile.slot(4)
                    loaded.inc(sp.dma_start(flat(agg[:, s, 0]), tile_of(g.agg_src, tile)), tile, 16)
                    loaded.inc(sp.dma_start(flat(agg[:, s, 1]), tile_of(g.agg_dst, tile)), tile, 16)

                def skips(tile):
                    summed.four_back(sp, tile)
                    x_loaded.inc(sp.dma_start(flat(xin[:, tile.slot(4)]), tile_of(g.x2, tile)), tile, 16)

                def stores(tile):
                    ln.done.this(sp, tile)
                    store(sp, stored, tile, (g.x3, flat(x3[:, tile.slot()])))

                run_tiles(sp, (3, loads), (2, skips), (-3, stores))
                stored.all(sp)

            @block.scalar
            def _(act):
                def exps(tile):
                    less_there.this(act, tile)
                    coef_there.slot_free(act, tile)
                    exped.inc(nc.scalar.activation(fac[:, tile.slot()], less[:, tile.slot()], ACT.Exp), tile)

                def gelus(tile):
                    mean_there.this(act, tile)
                    summed.slot_free(act, tile)
                    gelued.inc(nc.scalar.activation(flat(gel[:, tile.slot()]), flat(mean[:, tile.slot()]),
                                                    ACT.Gelu), tile)

                def scales(tile):
                    stored.slot_free(act, tile)
                    ln.scale(act, x3, y, tile)

                run_tiles(act, (0, gelus), (-2, scales), (2, exps))

            @block.vector
            def _(v):
                def maxima(tile):
                    s, s4 = tile.slot(), tile.slot(4)
                    loaded.this(v, tile)
                    none_there.inc(nc.vector.tensor_scalar(none[:, s], agg[:, s4, :, :, D], 0.0, FAR, ALU.is_equal,
                                                             ALU.mult), tile)
                    yield
                    none_there.this(v, tile)
                    mx_there.inc(nc.vector.tensor_tensor(mx[:, s], agg[:, s4, :, :, D + 1], none[:, s], ALU.add),
                         tile)
                    yield
                    mx_there.this(v, tile)
                    both_there.inc(nc.vector.tensor_tensor(both[:, s], mx[:, s, 0], mx[:, s, 1], ALU.max), tile)
                    yield
                    both_there.this(v, tile)
                    exped.slot_free(v, tile)
                    less_there.inc(nc.vector.tensor_tensor(
                        less[:, s], mx[:, s], both[:, s].unsqueeze(1).to_broadcast([P, 2, NJ]), ALU.subtract), tile)

                def means(tile):
                    s, s4 = tile.slot(), tile.slot(4)
                    exped.this(v, tile)
                    part_there.inc(nc.vector.tensor_tensor(part[:, s], fac[:, s], agg[:, s4, :, :, D], ALU.mult),
                         tile)
                    yield
                    part_there.this(v, tile)
                    den_there.inc(nc.vector.tensor_tensor(den[:, s], part[:, s, 0], part[:, s, 1], ALU.add), tile)
                    yield
                    den_there.this(v, tile)
                    empty_there.inc(nc.vector.tensor_scalar(empty[:, s], den[:, s], 0.0, None, ALU.is_equal), tile)
                    yield
                    empty_there.this(v, tile)
                    nc.vector.tensor_scalar(keep[:, s], empty[:, s], 1.0, None, ALU.add)
                    safe_there.inc(nc.vector.tensor_tensor(safe[:, s], den[:, s], empty[:, s], ALU.add), tile)
                    yield
                    safe_there.this(v, tile)
                    rden_there.inc(nc.vector.reciprocal(rden[:, s], safe[:, s]), tile)
                    yield
                    rden_there.this(v, tile)
                    coef_there.inc(nc.vector.tensor_tensor(
                        coef[:, s], fac[:, s], rden[:, s].unsqueeze(1).to_broadcast([P, 2, NJ]), ALU.mult), tile)
                    yield
                    coef_there.this(v, tile)
                    for j in range(NJ):
                        last = nc.vector.tensor_scalar(first[:, s, j], agg[:, s4, 0, j, 0:D], coef[:, s, 0, j:j + 1],
                                                       None, ALU.mult)
                    first_there.inc(last, tile)
                    yield
                    first_there.this(v, tile)
                    gelued.slot_free(v, tile)
                    for j in range(NJ):
                        last = nc.vector.scalar_tensor_tensor(mean[:, s, j], agg[:, s4, 1, j, 0:D],
                                                              coef[:, s, 1, j:j + 1], first[:, s, j],
                                                              ALU.mult, ALU.add)
                    mean_there.inc(last, tile)

                def sums(tile):
                    s = tile.slot()
                    x_loaded.this(v, tile)
                    gelued.this(v, tile)
                    ln.done.slot_free(v, tile)
                    for j in range(NJ):
                        last = nc.vector.scalar_tensor_tensor(y[:, s, j], xin[:, tile.slot(4), j],
                                                              keep[:, s, j:j + 1], gel[:, s, j], ALU.mult, ALU.add)
                    summed.inc(last, tile)
                    yield
                    summed.this(v, tile)
                    yield from ln.moments(v, y, tile)

                run_tiles(v, (2, maxima), (-1, sums), (1, means))

            @block.gpsimd
            def _(pool):
                run_tiles(pool, (-1, lambda tile: ln.power(pool, tile)))
        for r in (ln, loaded, x_loaded, stored, none_there, mx_there, both_there, less_there, exped, part_there, den_there,
                  empty_there, safe_there, rden_there, coef_there, first_there, mean_there, gelued, summed):
            r.up()


def gru_pass(g, step, h_in, h_out, x3=None):
    nc = g.nc
    final = x3 is not None
    ctx, sb, ps = scope(g)
    with ctx:
        hin = sb("hin", [P, 4, NJ, D])
        agg = sb("agg", [P, 4, NJ, AW])
        xin = sb("xin", [P, 4, NJ, D]) if final else None
        h_t, a_t, r, z, gated, pre, new, diff, mixed, h_new = [
            sb(n, [P, 2, NB]) for n in ("h_t", "a_t", "r", "z", "gated", "pre", "new", "diff", "mixed", "h_new")]
        hout = sb("hout", [P, 2, NJ, D])
        y = sb("y", [P, 2, NJ, D]) if final else None
        turn_ps = ps("turn_ps", [P, 2, 512])
        gate_ps = ps("gate_ps", [P, 4, 512])
        back_ps = ps("back_ps", [P, 2, 512])
        ln = Norm(g, sb) if final else None
        loaded, stored = Ring(g, "node_loaded", 4, 32, "dma"), Ring(g, "node_stored", 2, 16, "dma")
        x_loaded = Ring(g, "gru_x_loaded", 4, 16, "dma") if final else None
        a_turned, h_turned, a_there, h_there, r_prod, z_prod, n_prod, i_prod = rings(
            g, "gru_a_turned", "gru_h_turned", "gru_a", "gru_h", "gru_r_product", "gru_z_product",
            "gru_n_product", "gru_i_product")
        r_there, z_there, gated_there, pre_there, new_there, diff_there, mixed_there, h_new_there, back, out_there = \
            rings(g, "gru_r", "gru_z", "gru_gated", "gru_pre", "gru_new", "gru_diff", "gru_mixed", "gru_h_new",
                  "gru_back", "gru_out")
        with g.block() as block:
            @block.sync
            def _(sp):
                def loads(tile):
                    h_turned.four_back(sp, tile)
                    s = tile.slot(4)
                    loaded.inc(sp.dma_start(flat(hin[:, s]), tile_of(h_in, tile)), tile, 16)
                    loaded.inc(sp.dma_start(flat(agg[:, s]), tile_of(g.agg_dst, tile)), tile, 16)

                def skips(tile):
                    out_there.four_back(sp, tile)
                    x_loaded.inc(sp.dma_start(flat(xin[:, tile.slot(4)]), tile_of(x3, tile)), tile, 16)

                def stores(tile):
                    (ln.done if final else out_there).this(sp, tile)
                    store(sp, stored, tile, (h_out, flat(hout[:, tile.slot()])))

                run_tiles(sp, (3, loads), *([(1, skips), (-3, stores)] if final else [(-2, stores)]))
                stored.all(sp)

            @block.tensor
            def _(pe):
                def turns(tile):
                    s = tile.slot(4)
                    loaded.this(pe, tile)
                    a_there.one_back(pe, tile)
                    a_turned.inc(turn(g, turn_ps[:, 0], agg[:, s, :, 0:D]), tile)
                    h_there.one_back(pe, tile)
                    h_turned.inc(turn(g, turn_ps[:, 1], hin[:, s]), tile)

                def products(tile):
                    a_there.this(pe, tile)
                    h_there.this(pe, tile)
                    w_in, a, h = g.w_in[:, step], a_t[:, tile.slot()], h_t[:, tile.slot()]
                    for b, (free, done) in enumerate(((r_there, r_prod), (z_there, z_prod))):
                        free.one_back(pe, tile)
                        nc.tensor.matmul(gate_ps[:, b], w_in[:, b * D:(b + 1) * D], a, start=True, stop=False)
                        done.inc(nc.tensor.matmul(gate_ps[:, b], g.w_hid[:, b * D:(b + 1) * D], h,
                                                  start=False, stop=True), tile)
                    gated_there.one_back(pe, tile)
                    n_prod.inc(nc.tensor.matmul(gate_ps[:, 2], g.w_hid[:, 2 * D:3 * D], h, start=True,
                                                stop=True), tile)
                    pre_there.one_back(pe, tile)
                    i_prod.inc(nc.tensor.matmul(gate_ps[:, 3], w_in[:, 2 * D:3 * D], a, start=True,
                                                stop=True), tile)

                def backs(tile):
                    s = tile.slot()
                    h_new_there.this(pe, tile)
                    out_there.slot_free(pe, tile)
                    for j in range(NJ):
                        last = nc.tensor.transpose(back_ps[:, s, j * D:(j + 1) * D],
                                                   h_new[:, s, j * P:(j + 1) * P], g.ident[:])
                    back.inc(last, tile)

                run_tiles(pe, (1, turns), (0, products), (-1, backs))

            @block.scalar
            def _(act):
                def copies(tile):
                    s = tile.slot()
                    a_turned.this(act, tile)
                    i_prod.slot_free(act, tile)
                    a_there.inc(nc.scalar.copy(a_t[:, s], turn_ps[:, 0]), tile)
                    h_turned.this(act, tile)
                    diff_there.slot_free(act, tile)
                    h_there.inc(nc.scalar.copy(h_t[:, s], turn_ps[:, 1]), tile)

                def gates(tile):
                    s = tile.slot()
                    r_prod.this(act, tile)
                    gated_there.slot_free(act, tile)
                    r_there.inc(nc.scalar.activation(r[:, s], gate_ps[:, 0], ACT.Sigmoid,
                                                     bias=g.b_sum[:, 0:1]), tile)
                    z_prod.this(act, tile)
                    mixed_there.slot_free(act, tile)
                    z_there.inc(nc.scalar.activation(z[:, s], gate_ps[:, 1], ACT.Sigmoid,
                                                     bias=g.b_sum[:, 1:2]), tile)
                    pre_there.this(act, tile)
                    h_new_there.slot_free(act, tile)
                    new_there.inc(nc.scalar.activation(new[:, s], pre[:, s], ACT.Tanh,
                                                       bias=g.b_in[:, 2:3]), tile)

                run_tiles(act, (1, copies), (0, gates))

            @block.vector
            def _(v):
                def cell(tile):
                    s = tile.slot()
                    n_prod.this(v, tile)
                    r_there.this(v, tile)
                    gated_there.inc(nc.vector.scalar_tensor_tensor(
                        gated[:, s], gate_ps[:, 2], g.b_hid[:, 2:3], r[:, s], ALU.add, ALU.mult), tile)
                    yield
                    i_prod.this(v, tile)
                    gated_there.this(v, tile)
                    new_there.slot_free(v, tile)
                    pre_there.inc(nc.vector.tensor_tensor(pre[:, s], gated[:, s], gate_ps[:, 3], ALU.add), tile)
                    yield
                    new_there.this(v, tile)
                    h_there.this(v, tile)
                    diff_there.inc(nc.vector.tensor_tensor(diff[:, s], h_t[:, s], new[:, s], ALU.subtract), tile)
                    yield
                    z_there.this(v, tile)
                    diff_there.this(v, tile)
                    mixed_there.inc(nc.vector.tensor_tensor(mixed[:, s], diff[:, s], z[:, s], ALU.mult), tile)
                    yield
                    mixed_there.this(v, tile)
                    back.slot_free(v, tile)
                    h_new_there.inc(nc.vector.tensor_tensor(h_new[:, s], mixed[:, s], new[:, s], ALU.add), tile)

                def outs(tile):
                    s = tile.slot()
                    yield
                    back.this(v, tile)
                    stored.slot_free(v, tile)
                    out_there.inc(nc.vector.tensor_copy(flat(hout[:, s]), back_ps[:, s]), tile)

                def norms(tile):
                    s = tile.slot()
                    yield
                    back.this(v, tile)
                    x_loaded.this(v, tile)
                    ln.done.slot_free(v, tile)
                    out_there.inc(nc.vector.tensor_tensor(flat(y[:, s]), flat(xin[:, tile.slot(4)]), back_ps[:, s],
                                                          ALU.add), tile)
                    yield
                    out_there.this(v, tile)
                    yield from ln.moments(v, y, tile)

                def scales(tile):
                    yield
                    stored.slot_free(v, tile)
                    ln.scale_by_dve(v, hout, y, tile)

                run_tiles(v, (0, cell), *([(-2, scales), (-1, norms)] if final else [(-1, outs)]))

            if final:
                @block.gpsimd
                def _(pool):
                    run_tiles(pool, (-1, lambda tile: ln.power(pool, tile)))
        for h in (*((ln, x_loaded) if final else ()), loaded, stored, a_turned, h_turned, a_there, h_there, r_prod,
                  z_prod, n_prod, i_prod, r_there, z_there, gated_there, pre_there, new_there, diff_there,
                  mixed_there, h_new_there, back, out_there):
            h.up()


def program(g, a, out):
    constants_pass(g)
    weights_pass(g, a)
    gat_project_pass(g, a["x"])
    sort_pass(g, a["src"], a["dst"], a["edge_weight"])
    g.key_row = g.sb("key_row", [P, EP])
    g.rows = g.dram("rows", [P, CH, D])
    dst, src = Side(g, "dst"), Side(g, "src")
    side_pass(g, dst)
    side_pass(g, src)

    ctx, sb, ps = scope(g)
    with ctx:
        e_sb = sb("gat_exp", [P, CH, HEADS])
        gat_score_pass(g, dst, e_sb)
        edge_pass(g, dst, rows=g.rows, heads=e_sb, out=g.agg_dst, out_width=AW)
    gat_finish_pass(g, a["x"], src, a["edge_attr_128"])

    edge_pass(g, dst, table=g.hid_a, idx=dst.other_i, width=HID, weight=dst.weight, out=g.agg_hid, out_width=HID)
    edge_pass(g, dst, table=g.agg_hid, idx=dst.other_i, width=HID, weight=dst.weight, squash=g.b1[:],
              out=g.agg_hid2, out_width=HID)
    gcn_finish_pass(g, dst, a["edge_attr_128"], src)

    ctx, sb, ps = scope(g)
    with ctx:
        score, top = sb("score", [P, CH]), sb("top", [P, CH])
        for s, table in ((src, g.agg_src), (dst, g.agg_dst)):
            if s is dst:
                key_row_pass(g, s)
            att_score_pass(g, s, score, top)
            att_max_pass(g, s, score, top)
            edge_pass(g, s, rows=s.rows, weight=score, seg_max=top, out=table, out_width=AW)
    att_finish_pass(g)

    h = [g.x3, g.dram("h1", [N, D]), g.dram("h2", [N, D]), out]
    for i in range(3):
        edge_pass(g, dst, table=h[i], idx=dst.other_i, weight=dst.weight, out=g.agg_dst, out_width=AW)
        gru_pass(g, i, h[i], h[i + 1], g.x3 if i == 2 else None)


_INS = ['x', 'src', 'dst', 'edge_attr_128', 'edge_weight', 'L0_gnn_W_proj', 'L0_gnn_W_skip', 'L0_gnn_a_src',
        'L0_gnn_a_tgt', 'L1_gnn_w1', 'L1_gnn_b1', 'L1_gnn_w2', 'L1_gnn_b2', 'L2_gnn_W_att_w', 'L2_gnn_W_att_b',
        'L3_gnn_W', 'L3_gnn_w_ih', 'L3_gnn_w_hh', 'L3_gnn_b_ih', 'L3_gnn_b_hh']


def build(nc, args, out):
    with ExitStack() as ctx:
        program(Net(nc, ctx, args["x"]), args, out)


def kernel(**inputs):
    import numpy as _np
    import concourse.bacc as _bacc
    from concourse import mybir as _mybir
    from concourse.bass_utils import run_bass_kernel_spmd as _run

    nc = _bacc.Bacc("TRN2", target_bir_lowering=False, num_devices=1)
    arrays, args = {}, {}
    for name in _INS:
        a = _np.ascontiguousarray(inputs[name])
        arrays[f"in_{name}_dram"] = a
        args[name] = nc.dram_tensor(f"in_{name}_dram", a.shape, _mybir.dt.from_np(a.dtype), kind="ExternalInput").ap()
    out = nc.dram_tensor("out_0_dram", (N, D), F32, kind="ExternalOutput").ap()
    build(nc, args, out)
    r = _run(nc, [arrays], core_ids=[0])
    return r.results[0]["out_0_dram"]
```
